# Optimizing a Trainium2 kernel written in Bass

```python
import numpy as np
import jax
import jax.numpy as jnp

def _softmax(x, axis=-1):
    return jax.nn.softmax(x, axis=axis)

def _gelu(x):
    return jax.nn.gelu(x, approximate=True)

def _silu(x):
    return jax.nn.silu(x)

def _sigmoid(x):
    return jax.nn.sigmoid(x)

def _layernorm(x, axis=-1, eps=1e-05):
    m = jnp.mean(x, axis=axis, keepdims=True)
    v = jnp.var(x, axis=axis, keepdims=True)
    return (x - m) / jnp.sqrt(v + eps)

def _scatter_add(tgt, idx, src, axis=0):
    return tgt.at[idx].add(src)

def _segment_sum(src, seg, n):
    return jax.ops.segment_sum(src, seg, n)
kernel_name = 'mk_xattn_ffn_d4_seqx_r8_e317d5'

def setup_inputs(seed: int=0):
    np.random.seed(seed)
    _w = jnp.asarray

    def _rec_inputs():
        import jax
        import jax.numpy as jnp
        _rk = jax.random.key(seed)
        x = 2.818e-05 + 1 * jax.random.normal(jax.random.fold_in(_rk, 1), (4, 256, 128), jnp.float32)
        _lenS = 256 - jax.random.randint(jax.random.fold_in(_rk, 7), (4,), 0, max(1, 256 // 4) + 1, jnp.int32)
        _lenS2 = 256 - jax.random.randint(jax.random.fold_in(_rk, 8), (4,), 0, max(1, 256 // 4) + 1, jnp.int32)
        _ctx_2048P = jax.random.normal(jax.random.fold_in(_rk, 11), (4, 16, 256), jnp.float32)
        _ctx_2048c = jax.random.dirichlet(jax.random.fold_in(_rk, 511), 0.3 * jnp.ones((16,), jnp.float32), (4, 256))
        _ctx_2048t = jnp.einsum('bsk,bkd->bsd', _ctx_2048c, _ctx_2048P)
        _ctx_2048t = _ctx_2048t * jax.lax.rsqrt(jnp.mean(jnp.square(_ctx_2048t)) + 1e-12) * 0.953939
        ctx_2048 = -0.000125008 + 0.999885 * (_ctx_2048t + 0.3 * jax.random.normal(jax.random.fold_in(_rk, 611), (4, 256, 256), jnp.float32))
        _validS = jnp.arange(256)[None, :] < _lenS[:, None]
        _validS2 = jnp.arange(256)[None, :] < _lenS2[:, None]
        _causal = jnp.tril(jnp.ones((256, 256), dtype=bool))
        mask_BxS2_fk1 = jnp.where(jnp.broadcast_to(_validS2[:, :], (4, 256)), 1.0, 0.0).astype(jnp.float32)
        mask_BxS2_if0 = jnp.where(jnp.ones((4, 256), dtype=bool), 4, 0).astype(jnp.int32)
        return (x, ctx_2048, mask_BxS2_fk1, mask_BxS2_if0)
    x, ctx_2048, mask_BxS2_fk1, mask_BxS2_if0 = _rec_inputs()

    def _L0_xattn_setup():
        import jax, jax.numpy as jnp
        import numpy as np
        B, S, T = (32, 64, 64)
        SRC_SIZE, TGT_SIZE, OUT_SIZE, NUM_HEAD = (256, 128, 128, 8)
        HEAD_DIM = OUT_SIZE // NUM_HEAD
        key = jax.random.key(seed)
        ks = jax.random.split(key, 12)
        src = jax.random.normal(ks[0], (B, S, SRC_SIZE), dtype=jnp.float32)
        tgt = jax.random.normal(ks[1], (B, T, TGT_SIZE), dtype=jnp.float32)
        src_mask = (jax.random.uniform(ks[2], (B, S)) > 0.3).astype(jnp.float32)
        src_mask = src_mask.at[:, 0].set(1.0)
        tgt_mask = (jax.random.uniform(ks[3], (B, T)) > 0.3).astype(jnp.float32)
        tgt_mask = tgt_mask.at[:, 0].set(1.0)

        def lin(k, out_f, in_f):
            return jax.random.normal(k, (out_f, in_f), dtype=jnp.float32) / np.sqrt(in_f)
        W_src = lin(ks[4], 2 * OUT_SIZE, SRC_SIZE)
        b_src = jnp.zeros((2 * OUT_SIZE,), jnp.float32)
        W_tgt = lin(ks[5], OUT_SIZE, TGT_SIZE)
        b_tgt = jnp.zeros((OUT_SIZE,), jnp.float32)
        W_out = lin(ks[6], OUT_SIZE, OUT_SIZE + TGT_SIZE)
        b_out = jnp.zeros((OUT_SIZE,), jnp.float32)
        return {'src': src, 'tgt': tgt, 'src_mask': src_mask, 'tgt_mask': tgt_mask, 'W_src': W_src, 'b_src': b_src, 'W_tgt': W_tgt, 'b_tgt': b_tgt, 'W_out': W_out, 'b_out': b_out}
    _L0_xattn_all = _L0_xattn_setup()
    _L0_xattn_in = {k: v for k, v in _L0_xattn_all.items() if k in ('W_src', 'b_src', 'W_tgt', 'b_tgt', 'W_out', 'b_out')}
    del _L0_xattn_all

    def _L0_ffn_setup():
        import jax, jax.numpy as jnp
        import numpy as np
        B, S, H, F, E, R, TOPK = (4, 256, 128, 512, 4, 4, 2)

        def _more_forward(x, Wg, bg, W1, b1, W2, b2):
            b, s, h = x.shape
            cur = x
            for r in range(R):
                flat = cur.reshape(-1, h)
                logits = flat @ Wg[r] + bg[r]
                vals, idx = jax.lax.top_k(logits, TOPK)
                w = jax.nn.softmax(vals, axis=-1)
                cw = jnp.sum(jax.nn.one_hot(idx, E, dtype=flat.dtype) * w[..., None], axis=1)
                hmid = jax.nn.gelu(jnp.einsum('nh,ehf->enf', flat, W1) + b1[:, None, :])
                y = jnp.einsum('enf,efh->enh', hmid, W2) + b2[:, None, :]
                out = jnp.einsum('ne,enh->nh', cw, y)
                cur = cur + out.reshape(b, s, h)
            return cur
        key = jax.random.key(seed)
        ks = jax.random.split(key, 8)
        scale = 0.02
        return {'x': jax.random.normal(ks[0], (B, S, H), dtype=jnp.float32), 'Wg': jax.random.normal(ks[1], (R, H, E), dtype=jnp.float32) * scale, 'bg': jnp.zeros((R, E), dtype=jnp.float32), 'W1': jax.random.normal(ks[2], (E, H, F), dtype=jnp.float32) * scale, 'b1': jnp.zeros((E, F), dtype=jnp.float32), 'W2': jax.random.normal(ks[3], (E, F, H), dtype=jnp.float32) * scale, 'b2': jnp.zeros((E, H), dtype=jnp.float32)}
    _L0_ffn_all = _L0_ffn_setup()
    _L0_ffn_in = {k: v for k, v in _L0_ffn_all.items() if k in ('Wg', 'bg', 'W1', 'b1', 'W2', 'b2')}
    del _L0_ffn_all

    def _L1_xattn_setup():
        import jax, jax.numpy as jnp
        import numpy as np
        NUM_HEADS = 16
        key = jax.random.key(seed)
        ks = jax.random.split(key, 5)
        dim = 128
        B, N, N_c = (4, 128, 32)
        x = jax.random.normal(ks[0], (B, N, dim), dtype=jnp.float32)
        context = jax.random.normal(ks[1], (B, N_c, 2 * dim), dtype=jnp.float32)
        w_qkv = jax.random.normal(ks[2], (3 * dim, dim), dtype=jnp.float32) * 0.02
        w_proj = jax.random.normal(ks[3], (dim, dim), dtype=jnp.float32) * 0.02
        b_proj = jax.random.normal(ks[4], (dim,), dtype=jnp.float32) * 0.02
        return {'x': x, 'context': context, 'w_qkv': w_qkv, 'w_proj': w_proj, 'b_proj': b_proj}
    _L1_xattn_all = _L1_xattn_setup()
    _L1_xattn_in = {k: v for k, v in _L1_xattn_all.items() if k in ('w_qkv', 'w_proj', 'b_proj')}
    del _L1_xattn_all

    def _L1_ffn_setup():
        import jax, jax.numpy as jnp
        import numpy as np
        B, S, D = (2, 256, 128)
        H, E, P, K = (8, 8, 128, 2)
        SCALE = 1.0 / np.sqrt(P)

        def _get_sel_gate(x, w, route_scale):
            logits = jnp.einsum('bsd,ed->bse', x, w).astype(jnp.float32)
            raw = logits.reshape(x.shape[0], x.shape[1], H, E)
            probs = jax.nn.sigmoid(raw)
            vals, idx = jax.lax.top_k(probs, K)
            vals = vals / jnp.clip(vals.sum(-1, keepdims=True), 1e-09)
            vals = vals * route_scale
            gate = (jax.nn.one_hot(idx, E, dtype=vals.dtype) * vals[..., None]).sum(-2)
            return gate
        key = jax.random.key(seed)
        ks = jax.random.split(key, 8)
        std = 1.0 / np.sqrt(D)
        return {'x': jax.random.normal(ks[0], (B, S, D), jnp.float32), 'q_w': jax.random.normal(ks[1], (H * P, D), jnp.float32) * std, 'k_w': jax.random.normal(ks[2], (H * P, D), jnp.float32) * std, 'v_w': jax.random.normal(ks[3], (H * E, D, P), jnp.float32) * std, 'o_w': jax.random.normal(ks[4], (H * E, P, D), jnp.float32) * (1.0 / np.sqrt(H * P)), 'sel_v_w': jax.random.normal(ks[5], (H * E, D), jnp.float32) * std, 'sel_o_w': jax.random.normal(ks[6], (H * E, D), jnp.float32) * std, 'route_scale': jnp.ones((1,), jnp.float32)}
    _L1_ffn_all = _L1_ffn_setup()
    _L1_ffn_in = {k: v for k, v in _L1_ffn_all.items() if k in ('q_w', 'k_w', 'v_w', 'o_w', 'sel_v_w', 'sel_o_w', 'route_scale')}
    del _L1_ffn_all

    def _L2_xattn_setup():
        import jax, jax.numpy as jnp
        import numpy as np
        B, L, P = (4, 512, 128)
        D_MODEL = 128
        D_GLOBAL = 256
        HEADDIM = 32
        EPSILON = 0.001
        RMS_EPS = 1e-05

        def rmsnorm(x, g, eps=RMS_EPS):
            var = jnp.mean(jnp.square(x), axis=-1, keepdims=True)
            return x * jax.lax.rsqrt(var + eps) * g

        def _hnet_depool(h, h_patch_full, patch_lens):
            h_patch = h_patch_full[..., :D_MODEL]
            bsz, plen = (h_patch.shape[0], h_patch.shape[1])
            seqlen = h.shape[1]
            logp = jnp.full((bsz, plen), -EPSILON, dtype=jnp.float32)
            bidx = jnp.cumsum(patch_lens, axis=1) - 1
            boundary_mask = jnp.zeros((bsz, seqlen), dtype=jnp.int32)
            boundary_mask = boundary_mask.at[jnp.arange(bsz)[:, None], bidx].set(1)
            dt = (-jnp.log(-jnp.expm1(logp))).astype(h_patch.dtype)
            x = h_patch / dt[..., None]
            n_heads = D_MODEL // HEADDIM
            A = -jnp.ones((n_heads,), dtype=jnp.float32)
            bcoef = jnp.exp(logp).astype(h_patch.dtype)
            x4 = x.reshape(bsz, plen, n_heads, HEADDIM)
            a = jnp.exp(dt[:, :, None] * A[None, None, :])
            u = (dt * bcoef)[:, :, None, None] * x4
            a_b = jnp.broadcast_to(a[..., None], u.shape)

            def comb(lft, rgt):
                aL, uL = lft
                aR, uR = rgt
                return (aL * aR, uL * aR + uR)
            _, s = jax.lax.associative_scan(comb, (a_b, u), axis=1)
            depool = s.reshape(bsz, plen, D_MODEL)
            plug = jnp.clip(jnp.cumsum(boundary_mask, axis=1) - 1, 0, plen - 1)
            depool_out = depool[jnp.arange(bsz)[:, None], plug]
            return depool_out + h
        key = jax.random.key(seed)
        k1, k2, k3, k4 = jax.random.split(key, 4)
        embeds = jax.random.normal(k1, (B, L, D_MODEL), dtype=jnp.float32)
        patch_embeds = jax.random.normal(k2, (B, P, D_GLOBAL), dtype=jnp.float32)
        patch_lens = jnp.full((B, P), L // P, dtype=jnp.int64)
        W_in = jax.random.normal(k3, (D_MODEL, D_MODEL), dtype=jnp.float32) * 0.02
        b_in = jnp.zeros((D_MODEL,), dtype=jnp.float32)
        g_res = jnp.ones((D_MODEL,), dtype=jnp.float32)
        g_init = jnp.ones((D_GLOBAL,), dtype=jnp.float32)
        return {'embeds': embeds, 'patch_embeds': patch_embeds, 'patch_lens': patch_lens, 'W_in': W_in, 'b_in': b_in, 'g_res': g_res, 'g_init': g_init}
    _L2_xattn_all = _L2_xattn_setup()
    _L2_xattn_in = {k: v for k, v in _L2_xattn_all.items() if k in ('W_in', 'b_in', 'g_res', 'g_init')}
    del _L2_xattn_all

    def _L2_ffn_setup():
        import jax, jax.numpy as jnp
        import numpy as np
        E, D, F = (8, 128, 512)
        B, S = (4, 256)

        def _layernorm(x, g, b, eps=1e-05):
            mu = jnp.mean(x, axis=-1, keepdims=True)
            var = jnp.var(x, axis=-1, keepdims=True)
            return (x - mu) * jax.lax.rsqrt(var + eps) * g + b
        key = jax.random.key(seed)
        ks = jax.random.split(key, 5)
        return {'input_features': jax.random.normal(ks[0], (B, S, D), jnp.float32), 'centroids': jax.random.normal(ks[1], (E, D), jnp.float32) * 0.1, 'ln_g': jnp.ones((E, D), jnp.float32), 'ln_b': jnp.zeros((E, D), jnp.float32), 'w1': jax.random.normal(ks[2], (E, F, D), jnp.float32) * (1.0 / np.sqrt(D).astype(np.float32)), 'b1': jnp.zeros((E, F), jnp.float32), 'w2': jax.random.normal(ks[3], (E, D, F), jnp.float32) * (1.0 / np.sqrt(F).astype(np.float32)), 'b2': jnp.zeros((E, D), jnp.float32)}
    _L2_ffn_all = _L2_ffn_setup()
    _L2_ffn_in = {k: v for k, v in _L2_ffn_all.items() if k in ('centroids', 'ln_g', 'ln_b', 'w1', 'b1', 'w2', 'b2')}
    del _L2_ffn_all

    def _L3_xattn_setup():
        import jax, jax.numpy as jnp
        import numpy as np
        B, N, DIM = (8, 512, 128)
        M, CTX = (32, 256)
        HEADS, DH = (16, 64)
        INNER = HEADS * DH
        EPS = 1e-06

        def _split_heads(t):
            b, n, _ = t.shape
            return t.reshape(b, n, HEADS, DH).transpose(0, 2, 1, 3)
        key = jax.random.key(seed)
        ks = jax.random.split(key, 6)
        x = jax.random.normal(ks[0], (B, N, DIM), dtype=jnp.float32)
        context = jax.random.normal(ks[1], (B, M, CTX), dtype=jnp.float32)
        Wq = jax.random.normal(ks[2], (DIM, INNER), dtype=jnp.float32) / np.sqrt(DIM)
        Wkv = jax.random.normal(ks[3], (CTX, 2 * INNER), dtype=jnp.float32) / np.sqrt(CTX)
        null_kv = jax.random.normal(ks[4], (2, DH), dtype=jnp.float32) / np.sqrt(2.0)
        Wout = jax.random.normal(ks[5], (INNER, DIM), dtype=jnp.float32) / np.sqrt(INNER)
        ln_scale = jnp.ones((DIM,), dtype=jnp.float32)
        ln_bias = jnp.zeros((DIM,), dtype=jnp.float32)
        return {'x': x, 'context': context, 'Wq': Wq, 'Wkv': Wkv, 'null_kv': null_kv, 'Wout': Wout, 'ln_scale': ln_scale, 'ln_bias': ln_bias}
    _L3_xattn_all = _L3_xattn_setup()
    _L3_xattn_in = {k: v for k, v in _L3_xattn_all.items() if k in ('Wq', 'Wkv', 'null_kv', 'Wout', 'ln_scale', 'ln_bias')}
    del _L3_xattn_all

    def _L3_ffn_setup():
        import math
        import jax, jax.numpy as jnp
        import numpy as np
        CAPACITY_FACTOR = 1.25
        key = jax.random.key(seed)
        ks = jax.random.split(key, 5)
        B, S, H, F, E = (4, 512, 128, 128, 32)
        scale_in = 1.0 / math.sqrt(H)
        scale_mid = 1.0 / math.sqrt(F)
        return {'x': jax.random.normal(ks[0], (B, S, H), dtype=jnp.float32), 'w_router': jax.random.normal(ks[1], (H, E), dtype=jnp.float32) * scale_in, 'w_gate': jax.random.normal(ks[2], (E, H, F), dtype=jnp.float32) * scale_in, 'w_up': jax.random.normal(ks[3], (E, H, F), dtype=jnp.float32) * scale_in, 'w_down': jax.random.normal(ks[4], (E, F, H), dtype=jnp.float32) * scale_mid}
    _L3_ffn_all = _L3_ffn_setup()
    _L3_ffn_in = {k: v for k, v in _L3_ffn_all.items() if k in ('w_router', 'w_gate', 'w_up', 'w_down')}
    del _L3_ffn_all
    return {'x': x, 'ctx_2048': ctx_2048, 'mask_BxS2_fk1': mask_BxS2_fk1, 'mask_BxS2_if0': mask_BxS2_if0, 'L0_xattn_W_src': _L0_xattn_in['W_src'], 'L0_xattn_b_src': _L0_xattn_in['b_src'], 'L0_xattn_W_tgt': _L0_xattn_in['W_tgt'], 'L0_xattn_b_tgt': _L0_xattn_in['b_tgt'], 'L0_xattn_W_out': _L0_xattn_in['W_out'], 'L0_xattn_b_out': _L0_xattn_in['b_out'], 'L0_ffn_Wg': _L0_ffn_in['Wg'], 'L0_ffn_bg': _L0_ffn_in['bg'], 'L0_ffn_W1': _L0_ffn_in['W1'], 'L0_ffn_b1': _L0_ffn_in['b1'], 'L0_ffn_W2': _L0_ffn_in['W2'], 'L0_ffn_b2': _L0_ffn_in['b2'], 'L1_xattn_w_qkv': _L1_xattn_in['w_qkv'], 'L1_xattn_w_proj': _L1_xattn_in['w_proj'], 'L1_xattn_b_proj': _L1_xattn_in['b_proj'], 'L1_ffn_q_w': _L1_ffn_in['q_w'], 'L1_ffn_k_w': _L1_ffn_in['k_w'], 'L1_ffn_v_w': _L1_ffn_in['v_w'], 'L1_ffn_o_w': _L1_ffn_in['o_w'], 'L1_ffn_sel_v_w': _L1_ffn_in['sel_v_w'], 'L1_ffn_sel_o_w': _L1_ffn_in['sel_o_w'], 'L1_ffn_route_scale': _L1_ffn_in['route_scale'], 'L2_xattn_W_in': _L2_xattn_in['W_in'], 'L2_xattn_b_in': _L2_xattn_in['b_in'], 'L2_xattn_g_res': _L2_xattn_in['g_res'], 'L2_xattn_g_init': _L2_xattn_in['g_init'], 'L2_ffn_centroids': _L2_ffn_in['centroids'], 'L2_ffn_ln_g': _L2_ffn_in['ln_g'], 'L2_ffn_ln_b': _L2_ffn_in['ln_b'], 'L2_ffn_w1': _L2_ffn_in['w1'], 'L2_ffn_b1': _L2_ffn_in['b1'], 'L2_ffn_w2': _L2_ffn_in['w2'], 'L2_ffn_b2': _L2_ffn_in['b2'], 'L3_xattn_Wq': _L3_xattn_in['Wq'], 'L3_xattn_Wkv': _L3_xattn_in['Wkv'], 'L3_xattn_null_kv': _L3_xattn_in['null_kv'], 'L3_xattn_Wout': _L3_xattn_in['Wout'], 'L3_xattn_ln_scale': _L3_xattn_in['ln_scale'], 'L3_xattn_ln_bias': _L3_xattn_in['ln_bias'], 'L3_ffn_w_router': _L3_ffn_in['w_router'], 'L3_ffn_w_gate': _L3_ffn_in['w_gate'], 'L3_ffn_w_up': _L3_ffn_in['w_up'], 'L3_ffn_w_down': _L3_ffn_in['w_down']}

def reference(x, ctx_2048, mask_BxS2_fk1, mask_BxS2_if0, L0_xattn_W_src, L0_xattn_b_src, L0_xattn_W_tgt, L0_xattn_b_tgt, L0_xattn_W_out, L0_xattn_b_out, L0_ffn_Wg, L0_ffn_bg, L0_ffn_W1, L0_ffn_b1, L0_ffn_W2, L0_ffn_b2, L1_xattn_w_qkv, L1_xattn_w_proj, L1_xattn_b_proj, L1_ffn_q_w, L1_ffn_k_w, L1_ffn_v_w, L1_ffn_o_w, L1_ffn_sel_v_w, L1_ffn_sel_o_w, L1_ffn_route_scale, L2_xattn_W_in, L2_xattn_b_in, L2_xattn_g_res, L2_xattn_g_init, L2_ffn_centroids, L2_ffn_ln_g, L2_ffn_ln_b, L2_ffn_w1, L2_ffn_b1, L2_ffn_w2, L2_ffn_b2, L3_xattn_Wq, L3_xattn_Wkv, L3_xattn_null_kv, L3_xattn_Wout, L3_xattn_ln_scale, L3_xattn_ln_bias, L3_ffn_w_router, L3_ffn_w_gate, L3_ffn_w_up, L3_ffn_w_down):
    import jax
    import jax.numpy as jnp

    def _L0_xattn_ref(src, tgt, src_mask, tgt_mask, W_src, b_src, W_tgt, b_tgt, W_out, b_out):
        import jax, jax.numpy as jnp
        import numpy as np
        B, S, T = (32, 64, 64)
        SRC_SIZE, TGT_SIZE, OUT_SIZE, NUM_HEAD = (256, 128, 128, 8)
        HEAD_DIM = OUT_SIZE // NUM_HEAD
        b, s, _ = src.shape
        t = tgt.shape[1]
        src_trans = jnp.einsum('bsf,of->bso', src, W_src) + b_src
        tgt_trans = jnp.einsum('btf,of->bto', tgt, W_tgt) + b_tgt
        src_trans = src_trans * src_mask[:, :, None]
        tgt_trans = tgt_trans * tgt_mask[:, :, None]
        src_key, src_val = jnp.split(src_trans, 2, axis=2)
        k = src_key.reshape(b, s, NUM_HEAD, HEAD_DIM)
        v = src_val.reshape(b, s, NUM_HEAD, HEAD_DIM)
        q = tgt_trans.reshape(b, t, NUM_HEAD, HEAD_DIM)
        scores = jnp.einsum('bthd,bshd->bhts', q, k) / np.sqrt(HEAD_DIM)
        scores = jnp.where(src_mask[:, None, None, :] == 0, -jnp.inf, scores)
        attn = jax.nn.softmax(scores, axis=-1)
        tgt_update = jnp.einsum('bhts,bshd->bthd', attn, v).reshape(b, t, OUT_SIZE)
        cat_tgt = jnp.concatenate([tgt, tgt_update], axis=2)
        return jnp.einsum('btf,of->bto', cat_tgt, W_out) + b_out

    def _L0_ffn_ref(x, Wg, bg, W1, b1, W2, b2):
        import jax, jax.numpy as jnp
        import numpy as np
        B, S, H, F, E, R, TOPK = (4, 256, 128, 512, 4, 4, 2)

        def _more_forward(x, Wg, bg, W1, b1, W2, b2):
            b, s, h = x.shape
            cur = x
            for r in range(R):
                flat = cur.reshape(-1, h)
                logits = flat @ Wg[r] + bg[r]
                vals, idx = jax.lax.top_k(logits, TOPK)
                w = jax.nn.softmax(vals, axis=-1)
                cw = jnp.sum(jax.nn.one_hot(idx, E, dtype=flat.dtype) * w[..., None], axis=1)
                hmid = jax.nn.gelu(jnp.einsum('nh,ehf->enf', flat, W1) + b1[:, None, :])
                y = jnp.einsum('enf,efh->enh', hmid, W2) + b2[:, None, :]
                out = jnp.einsum('ne,enh->nh', cw, y)
                cur = cur + out.reshape(b, s, h)
            return cur
        return _more_forward(x, Wg, bg, W1, b1, W2, b2)

    def _L1_xattn_ref(x, context, w_qkv, w_proj, b_proj):
        import jax, jax.numpy as jnp
        import numpy as np
        NUM_HEADS = 16
        B, N, C = x.shape
        H = NUM_HEADS
        D = C // H
        scale = D ** (-0.5)
        qkv = (x @ w_qkv.T).reshape(B, N, 3, H, D).transpose(2, 0, 3, 1, 4)
        q, k, v = (qkv[0], qkv[1], qkv[2])
        N_c = context.shape[1]
        kv = context.reshape(B, N_c, 2, H, D).transpose(2, 0, 3, 1, 4)
        extra_k, extra_v = (kv[0], kv[1])
        k = jnp.concatenate([extra_k, k], axis=2)
        v = jnp.concatenate([extra_v, v], axis=2)
        dtype = q.dtype
        attn = jnp.einsum('bhnd,bhmd->bhnm', q * scale, k).astype(jnp.float32)
        attn = jax.nn.softmax(attn, axis=-1).astype(dtype)
        out = jnp.einsum('bhnm,bhmd->bhnd', attn, v)
        out = out.transpose(0, 2, 1, 3).reshape(B, N, C)
        return out @ w_proj.T + b_proj

    def _L1_ffn_ref(x, q_w, k_w, v_w, o_w, sel_v_w, sel_o_w, route_scale):
        import jax, jax.numpy as jnp
        import numpy as np
        B, S, D = (2, 256, 128)
        H, E, P, K = (8, 8, 128, 2)
        SCALE = 1.0 / np.sqrt(P)

        def _get_sel_gate(x, w, route_scale):
            logits = jnp.einsum('bsd,ed->bse', x, w).astype(jnp.float32)
            raw = logits.reshape(x.shape[0], x.shape[1], H, E)
            probs = jax.nn.sigmoid(raw)
            vals, idx = jax.lax.top_k(probs, K)
            vals = vals / jnp.clip(vals.sum(-1, keepdims=True), 1e-09)
            vals = vals * route_scale
            gate = (jax.nn.one_hot(idx, E, dtype=vals.dtype) * vals[..., None]).sum(-2)
            return gate
        rs = route_scale[0]
        gate_v = _get_sel_gate(x, sel_v_w, rs)
        gate_o = _get_sel_gate(x, sel_o_w, rs)
        q = jnp.einsum('bsd,hpd->bhsp', x, q_w.reshape(H, P, D))
        k = jnp.einsum('bsd,hpd->bhsp', x, k_w.reshape(H, P, D))
        xv = jnp.einsum('bsd,hedp->bshep', x, v_w.reshape(H, E, D, P))
        v = jnp.einsum('bshep,bshe->bhsp', xv, gate_v)
        att = jax.nn.softmax(jnp.einsum('bhqp,bhkp->bhqk', q, k) * SCALE, axis=-1)
        ctx = jnp.einsum('bhqk,bhkp->bqhp', att, v)
        weighted = ctx[:, :, :, None, :] * gate_o[..., None]
        out = jnp.einsum('bshep,hepd->bsd', weighted, o_w.reshape(H, E, P, D))
        return out

    def _L2_xattn_ref(embeds, patch_embeds, patch_lens, W_in, b_in, g_res, g_init):
        import jax, jax.numpy as jnp
        import numpy as np
        B, L, P = (4, 512, 128)
        D_MODEL = 128
        D_GLOBAL = 256
        HEADDIM = 32
        EPSILON = 0.001
        RMS_EPS = 1e-05

        def rmsnorm(x, g, eps=RMS_EPS):
            var = jnp.mean(jnp.square(x), axis=-1, keepdims=True)
            return x * jax.lax.rsqrt(var + eps) * g

        def _hnet_depool(h, h_patch_full, patch_lens):
            h_patch = h_patch_full[..., :D_MODEL]
            bsz, plen = (h_patch.shape[0], h_patch.shape[1])
            seqlen = h.shape[1]
            logp = jnp.full((bsz, plen), -EPSILON, dtype=jnp.float32)
            bidx = jnp.cumsum(patch_lens, axis=1) - 1
            boundary_mask = jnp.zeros((bsz, seqlen), dtype=jnp.int32)
            boundary_mask = boundary_mask.at[jnp.arange(bsz)[:, None], bidx].set(1)
            dt = (-jnp.log(-jnp.expm1(logp))).astype(h_patch.dtype)
            x = h_patch / dt[..., None]
            n_heads = D_MODEL // HEADDIM
            A = -jnp.ones((n_heads,), dtype=jnp.float32)
            bcoef = jnp.exp(logp).astype(h_patch.dtype)
            x4 = x.reshape(bsz, plen, n_heads, HEADDIM)
            a = jnp.exp(dt[:, :, None] * A[None, None, :])
            u = (dt * bcoef)[:, :, None, None] * x4
            a_b = jnp.broadcast_to(a[..., None], u.shape)

            def comb(lft, rgt):
                aL, uL = lft
                aR, uR = rgt
                return (aL * aR, uL * aR + uR)
            _, s = jax.lax.associative_scan(comb, (a_b, u), axis=1)
            depool = s.reshape(bsz, plen, D_MODEL)
            plug = jnp.clip(jnp.cumsum(boundary_mask, axis=1) - 1, 0, plen - 1)
            depool_out = depool[jnp.arange(bsz)[:, None], plug]
            return depool_out + h
        h = rmsnorm(embeds, g_res)
        h = jnp.einsum('bld,ed->ble', h, W_in) + b_in
        h_patch = rmsnorm(patch_embeds, g_init)
        return _hnet_depool(h, h_patch, patch_lens)

    def _L2_ffn_ref(input_features, centroids, ln_g, ln_b, w1, b1, w2, b2):
        import jax, jax.numpy as jnp
        import numpy as np
        E, D, F = (8, 128, 512)
        B, S = (4, 256)

        def _layernorm(x, g, b, eps=1e-05):
            mu = jnp.mean(x, axis=-1, keepdims=True)
            var = jnp.var(x, axis=-1, keepdims=True)
            return (x - mu) * jax.lax.rsqrt(var + eps) * g + b
        Bf, Sf, Df = input_features.shape
        x = input_features.reshape(-1, Df)
        aff = x @ centroids.T
        assign = jnp.argmax(aff, axis=1)
        order = jnp.argsort(assign)
        xs = x[order]
        es = assign[order]
        alpha = jax.nn.sigmoid(jnp.take_along_axis(aff[order], es[:, None], axis=1))
        nE = centroids.shape[0]
        y = jnp.zeros_like(xs)
        for e in range(nE):
            h = _layernorm(xs, ln_g[e], ln_b[e])
            h = jax.nn.relu(h @ w1[e].T + b1[e])
            ye = xs + h @ w2[e].T + b2[e]
            y = y + jnp.where((es == e)[:, None], ye, 0.0)
        out_sorted = alpha * y + (1.0 - alpha) * xs
        inv = jnp.argsort(order)
        return out_sorted[inv].reshape(Bf, Sf, Df)

    def _L3_xattn_ref(x, context, Wq, Wkv, null_kv, Wout, ln_scale, ln_bias):
        import jax, jax.numpy as jnp
        import numpy as np
        B, N, DIM = (8, 512, 128)
        M, CTX = (32, 256)
        HEADS, DH = (16, 64)
        INNER = HEADS * DH
        EPS = 1e-06

        def _split_heads(t):
            b, n, _ = t.shape
            return t.reshape(b, n, HEADS, DH).transpose(0, 2, 1, 3)
        scale = DH ** (-0.5)
        b = x.shape[0]
        q = _split_heads(jnp.einsum('bnd,df->bnf', x, Wq))
        kv = jnp.einsum('bmc,cf->bmf', context, Wkv)
        k, v = jnp.split(kv, 2, axis=-1)
        k, v = (_split_heads(k), _split_heads(v))
        nk = jnp.broadcast_to(null_kv[0], (b, HEADS, 1, DH))
        nv = jnp.broadcast_to(null_kv[1], (b, HEADS, 1, DH))
        k = jnp.concatenate((nk, k), axis=-2)
        v = jnp.concatenate((nv, v), axis=-2)
        q = q * scale
        sim = jnp.einsum('bhid,bhjd->bhij', q, k)
        attn = jax.nn.softmax(sim, axis=-1)
        out = jnp.einsum('bhij,bhjd->bhid', attn, v)
        out = out.transpose(0, 2, 1, 3).reshape(b, -1, INNER)
        out = jnp.einsum('bnf,fd->bnd', out, Wout)
        mu = jnp.mean(out, axis=-1, keepdims=True)
        var = jnp.var(out, axis=-1, keepdims=True)
        out = (out - mu) * jax.lax.rsqrt(var + EPS) * ln_scale + ln_bias
        return out

    def _L3_ffn_ref(x, w_router, w_gate, w_up, w_down):
        import math
        import jax, jax.numpy as jnp
        import numpy as np
        CAPACITY_FACTOR = 1.25
        B, S, H = x.shape
        E = w_gate.shape[0]
        T = B * S
        C = int(math.ceil(CAPACITY_FACTOR * T / E))
        xt = x.reshape(T, H)
        logits = xt @ w_router
        probs = jax.nn.softmax(logits, axis=-1)
        top1 = jnp.argmax(probs, axis=-1)
        gate = jnp.take_along_axis(probs, top1[:, None], axis=1)[:, 0]
        onehot = jax.nn.one_hot(top1, E, dtype=jnp.int32)
        pos = jnp.cumsum(onehot, axis=0)[jnp.arange(T), top1] - 1
        accepted = pos < C
        slot = jnp.where(accepted, top1 * C + pos, E * C)
        buf = jnp.zeros((E * C + 1, H), dtype=x.dtype).at[slot].set(xt)
        buf = buf[:E * C].reshape(E, C, H)
        g = jnp.einsum('ech,ehf->ecf', buf, w_gate)
        u = jnp.einsum('ech,ehf->ecf', buf, w_up)
        y = jnp.einsum('ecf,efh->ech', jax.nn.silu(g) * u, w_down)
        out_tok = y.reshape(E * C, H)[jnp.clip(slot, 0, E * C - 1)]
        out_tok = jnp.where(accepted[:, None], out_tok * gate[:, None], 0.0)
        return (xt + out_tok).reshape(B, S, H)
    x = x + _L0_xattn_ref(ctx_2048, _layernorm(x, axis=-1), mask_BxS2_fk1, mask_BxS2_fk1, L0_xattn_W_src, L0_xattn_b_src, L0_xattn_W_tgt, L0_xattn_b_tgt, L0_xattn_W_out, L0_xattn_b_out)
    x = x + _L0_ffn_ref(_layernorm(x, axis=-1), L0_ffn_Wg, L0_ffn_bg, L0_ffn_W1, L0_ffn_b1, L0_ffn_W2, L0_ffn_b2)
    x = x + _L1_xattn_ref(_layernorm(x, axis=-1), ctx_2048, L1_xattn_w_qkv, L1_xattn_w_proj, L1_xattn_b_proj)
    x = x + _L1_ffn_ref(_layernorm(x, axis=-1), L1_ffn_q_w, L1_ffn_k_w, L1_ffn_v_w, L1_ffn_o_w, L1_ffn_sel_v_w, L1_ffn_sel_o_w, L1_ffn_route_scale)
    x = x + _L2_xattn_ref(_layernorm(x, axis=-1), ctx_2048, mask_BxS2_if0, L2_xattn_W_in, L2_xattn_b_in, L2_xattn_g_res, L2_xattn_g_init)
    x = x + _L2_ffn_ref(_layernorm(x, axis=-1), L2_ffn_centroids, L2_ffn_ln_g, L2_ffn_ln_b, L2_ffn_w1, L2_ffn_b1, L2_ffn_w2, L2_ffn_b2)
    x = x + _L3_xattn_ref(_layernorm(x, axis=-1), ctx_2048, L3_xattn_Wq, L3_xattn_Wkv, L3_xattn_null_kv, L3_xattn_Wout, L3_xattn_ln_scale, L3_xattn_ln_bias)
    x = x + _L3_ffn_ref(_layernorm(x, axis=-1), L3_ffn_w_router, L3_ffn_w_gate, L3_ffn_w_up, L3_ffn_w_down)
    return x

_drawn_inputs = setup_inputs


def setup_inputs(seed=0):
    import zlib

    import numpy as np

    out = dict(_drawn_inputs(seed))
    spreads = {'L0_xattn_b_src': (0.0, 0.1),
     'L0_xattn_b_tgt': (0.0, 0.351),
     'L0_xattn_b_out': (0.0, 0.1),
     'L0_ffn_bg': (0.0, 0.1),
     'L0_ffn_b1': (0.0, 0.1),
     'L0_ffn_b2': (0.0, 0.1),
     'L2_xattn_b_in': (0.0, 0.1),
     'L2_xattn_g_res': (1.0, 0.2),
     'L2_xattn_g_init': (1.0, 0.2),
     'L2_ffn_ln_g': (1.0, 0.2),
     'L2_ffn_ln_b': (0.0, 0.502),
     'L2_ffn_b1': (0.0, 0.499),
     'L2_ffn_b2': (0.0, 0.359),
     'L3_xattn_ln_scale': (1.0, 0.2),
     'L3_xattn_ln_bias': (0.0, 0.31)}
    factors = {'L1_xattn_w_qkv': 4.632,
     'L1_xattn_b_proj': 2.823,
     'L3_xattn_null_kv': 8.0,
     'L3_ffn_w_router': 2.699,
     'L3_ffn_w_gate': 2.736}
    for name, (base, spread) in spreads.items():
        noise = np.random.default_rng([zlib.crc32(name.encode()), seed]).standard_normal(out[name].shape)
        drawn = base * np.exp(spread * noise) if base else spread * noise
        out[name] = jnp.asarray(drawn.astype(out[name].dtype))
    for name, factor in factors.items():
        out[name] = (out[name] * factor).astype(out[name].dtype)
    return out
```

```python
from contextlib import ExitStack

import numpy as np

import concourse.bass as bass
from concourse import mybir

F32 = mybir.dt.float32
BF16 = mybir.dt.bfloat16
I32 = mybir.dt.int32
ALU = mybir.AluOpType
ACT = mybir.ActivationFunctionType
AX = mybir.AxisListType

P = 128
B, S, D = 4, 256, 128
CTX = 256
T = B * S
NT = T // P
TPB = S // P
HALF = 512
MASKED = -1.0e30
SLOT = 32
TERMS = ((0, 0), (0, 1), (0, 2), (1, 0), (1, 1), (2, 0))


class Chain:

    def __init__(self, engine, semaphore):
        self.engine, self.semaphore, self.count = engine, semaphore, 0

    def then(self, instruction):
        self.count += 1
        instruction.then_inc(self.semaphore, 1)
        self.engine.wait_ge(self.semaphore, self.count)


class Count:

    def __init__(self, semaphore, base):
        self.semaphore, self.base = semaphore, base

    def at(self, n):
        return self.semaphore, self.base + n


class Norm:

    def __init__(self, k, name):
        self.k = k
        self.var_ready = k.sem(f"{name}_var_ready")
        self.rstd_ready = k.sem(f"{name}_rstd_ready")
        self.ready = k.sem(f"{name}_ready")
        self.turned = k.sem(f"{name}_turned")
        self.T_ready = k.sem(f"{name}_T_ready")

    def statistics(self, dve, chain, n, src, eps, rms=False):
        k = self.k
        for t in range(NT):
            ins = dve.bn_stats(k.stats[:, t, :], src[:, t, :])
        chain.then(ins)
        for t in range(NT):
            ins = dve.bn_aggr(k.mean_var[:, t, :], k.stats[:, t, :])
        chain.then(ins)
        if rms:
            chain.then(dve.tensor_tensor(k.var_eps[:, :], k.mean_var[:, :, 0], k.mean_var[:, :, 0], ALU.mult))
            chain.then(dve.tensor_tensor(k.var_eps[:, :], k.var_eps[:, :], k.mean_var[:, :, 1], ALU.add))
            dve.tensor_scalar(k.var_eps[:, :], k.var_eps[:, :], eps, None, ALU.add).then_inc(self.var_ready, 1)
        else:
            dve.tensor_scalar(k.var_eps[:, :], k.mean_var[:, :, 1], eps, None, ALU.add).then_inc(self.var_ready, 1)
        dve.wait_ge(self.rstd_ready, n + 1)

    def vector(self, dve, chain, n, src, dst, eps, rms=False):
        k = self.k
        self.statistics(dve, chain, n, src, eps, rms)
        for t in range(NT):
            if rms:
                ins = dve.tensor_scalar(dst[:, t, :], src[:, t, :], k.rstd[:, t:t + 1], None, ALU.mult)
            else:
                ins = dve.tensor_scalar(dst[:, t, :], src[:, t, :], k.mean_var[:, t, 0:1], k.rstd[:, t:t + 1],
                                        ALU.subtract, ALU.mult)
            ins.then_inc(self.ready, 1)

    def gpsimd(self, pool, n):
        k = self.k
        pool.wait_ge(self.var_ready, n + 1)
        pool.tensor_tensor(k.rstd[:, :], k.var_eps[:, :], k.minus_half[:, :], ALU.pow).then_inc(self.rstd_ready, 1)

    def tensor(self, pe, n, src, banks=(6, 7)):
        k = self.k
        for t in range(NT):
            pe.wait_ge(self.ready, NT * n + t + 1)
            ins = pe.transpose(k.bank[banks[t // 4]][:, (t % 4) * P:(t % 4 + 1) * P], src[:, t, :], k.ident[:, :])
            if t % 4 == 3:
                ins.then_inc(self.turned, 1)

    def scalar(self, act, n, dst, banks=(6, 7), scale=1.0):
        k = self.k
        for h in range(2):
            act.wait_ge(self.turned, 2 * n + h + 1)
            act.activation(dst[:, h * HALF:(h + 1) * HALF], k.bank[banks[h]], ACT.Copy, scale=scale)\
                .then_inc(self.T_ready, 1)


def packed_attention(k, name, number, NH, HD, key_tiles, masked, eps, W):
    NHG = NH // 4
    R_MASK = len(TERMS) * HD
    R_MAX = R_MASK + (1 if masked else 0)
    ROWS = R_MAX + 3
    NK = key_tiles * P
    STEPS = NHG * key_tiles
    NG1 = TPB * NH * NK // HALF
    HPG = HALF // NK
    PER = NG1 // STEPS
    scale = float(HD) ** -0.5
    assert PER * STEPS == NG1 and NH * HD == D

    k.carve_from(0)
    QS = [k.carve(BF16, NH, S) for _ in range(2)]
    KS = [k.carve(BF16, NH, NK) for _ in range(2)]
    VA = [k.carve(F32, key_tiles, NH, SLOT) for _ in range(2)]
    NM = k.carve(F32, B, NH, TPB)
    NMr = k.carve(F32, P)
    NMp = [k.carve(BF16, P) for _ in range(3)]
    vtmp = k.carve(F32, HALF)
    mark = k.carve_mark()
    q32, k32 = k.carve(F32, T), k.carve(F32, T)
    qp = [k.carve(BF16, T) for _ in range(3)]
    kp = [k.carve(BF16, T) for _ in range(3)]
    cp = [] if masked else [k.carve(BF16, T) for _ in range(3)]
    k.carve_back(mark)
    PT = [k.carve(F32, 4 * S) for _ in range(2)]
    OT = k.carve(F32, NHG, T)
    OTn = [k.carve(F32, NHG, P) for _ in range(2)]
    R = k.carve(F32, NT, NH)
    RX = [k.carve(F32, NH * SLOT) for _ in range(2)]

    q_dram, k_dram = k.q_dram[number], k.k_dram[number]
    c_dram = k.c_dram

    use = k.norm_use[number]

    def count(what, total):
        return k.count(f"packed_{what}", total)

    fill_done = count("fill_done", 1)
    q_psum = count("q_psum", 2)
    k_psum = count("k_psum", 2)
    v_psum = count("v_psum", B)
    q_sb = count("q_sb", 2)
    k_sb = count("k_sb", 2)
    part = count("part", 4 if masked else 6)
    rest = count("rest", 4 if masked else 6)
    stored = count("stored", 16 * (6 if masked else 9))
    loaded = [count(f"loaded{i}", 2 * k.loads_of(name)) for i in range(2)]
    v_sb = count("v_sb", B)
    p1_psum = count("p1_psum", B * NG1)
    p1_max = count("p1_max", B * NG1)
    nm_psum = count("nm_psum", B)
    nm_part = count("nm_part", 2 * B)
    nm_rest = count("nm_rest", 2 * B)
    nm_loaded = count("nm_loaded", 48 * B)
    p2_psum = count("p2_psum", B * STEPS)
    p2_exp = count("p2_exp", B * STEPS)
    av_done = count("av_done", B * STEPS)
    av_out = count("av_out", B * NHG)
    den_psum = count("den_psum", 1)
    den_ready = count("den_ready", 1)
    wide_ready = count("wide_ready", NT)
    bc_psum = count("bc_psum", NT)
    normed = count("normed", NT)
    out_psum = count("out_psum", NT)

    def tensor(pe):
        bank = k.bank
        k.norm.tensor(pe, use, k.xn)
        pe.wait_ge(k.weights[name], 16)
        if masked:
            pe.wait_ge(k.ctxT_ready, 4)
        for h in range(2):
            cols = slice(h * HALF, (h + 1) * HALF)
            if masked:
                for c in range(2):
                    ins = pe.matmul(bank[2 + h][:, :], W("k")[:, c, :], k.ctxT[:, c, cols], start=c == 0, stop=c == 1)
            else:
                pe.wait_ge(k.norm.T_ready, 2 * use + h + 1)
                ins = pe.matmul(bank[2 + h][:, :], W("k"), k.xnT[:, cols], start=True, stop=True)
            ins.then_inc(k_psum.semaphore, 1)
        for h in range(2):
            pe.wait_ge(k.norm.T_ready, 2 * use + h + 1)
            pe.matmul(bank[h][:, :], W("q"), k.xnT[:, h * HALF:(h + 1) * HALF], start=True, stop=True).then_inc(q_psum.semaphore, 1)

        def values(b):
            if b >= 1:
                pe.wait_ge(*v_sb.at(b))
                pe.wait_ge(*nm_rest.at(2 * b))
            for t in range(TPB):
                tt = b * TPB + t
                if masked:
                    for c in range(2):
                        ins = pe.matmul(bank[7][:, t * P:(t + 1) * P], k.ctxT[:, c, tt * P:(tt + 1) * P],
                                        W("v")[:, c, :], start=c == 0, stop=c == 1)
                else:
                    ins = pe.matmul(bank[7][:, t * P:(t + 1) * P], k.xnT[:, tt * P:(tt + 1) * P], W("v"),
                                    start=True, stop=True)
            ins.then_inc(v_psum.semaphore, 1)

        def first_pass(b, n):
            g = b * NG1 + n
            if g >= 2:
                pe.wait_ge(*p1_max.at(g - 1))
            t, h0 = n // (NG1 // TPB), n % (NG1 // TPB) * HPG
            for j in range(HPG):
                ins = pe.matmul(bank[g % 2][:, j * NK:(j + 1) * NK],
                                QS[b % 2][0:R_MAX, h0 + j, t * P:(t + 1) * P],
                                KS[b % 2][0:R_MAX, h0 + j, :], start=True, stop=True)
            ins.then_inc(p1_psum.semaphore, 1)

        def second_pass(b, s):
            g = b * STEPS + s
            hg, kt = s // key_tiles, s % key_tiles
            if g >= 2:
                pe.wait_ge(*p2_exp.at(g - 1))
            for j in range(4):
                ins = pe.matmul(bank[2 + 2 * (g % 2) + j // 2][:, (j % 2) * S:(j % 2 + 1) * S],
                                KS[b % 2][0:ROWS, 4 * hg + j, kt * P:(kt + 1) * P],
                                QS[b % 2][0:ROWS, 4 * hg + j, :], start=True, stop=True)
            ins.then_inc(p2_psum.semaphore, 1)

        def weighted_values(b, s):
            g = b * STEPS + s
            hg, kt = s // key_tiles, s % key_tiles
            pe.wait_ge(*p2_exp.at(g + 1))
            if s == 0:
                pe.wait_ge(*v_sb.at(b + 1))
            if kt == 0 and g >= 1:
                pe.wait_ge(*av_out.at(b * NHG + hg))
            for j in range(4):
                ins = pe.matmul(bank[6][SLOT * j:SLOT * (j + 1), 0:S], VA[b % 2][:, kt, 4 * hg + j, :],
                                PT[g % 2][:, j * S:(j + 1) * S], start=kt == 0, stop=kt == key_tiles - 1,
                                tile_position=(0, SLOT * j))
            ins.then_inc(av_done.semaphore, 1)

        for b in range(B + 1):
            if b < B:
                values(b)
                if b == 0:
                    pe.wait_ge(*k_sb.at(2))
                    pe.wait_ge(*q_sb.at(2))
                pe.wait_ge(*loaded[b % 2].at(k.loads_of(name) * (b // 2 + 1)))
            for s in range(STEPS):
                if b < B:
                    for i in range(PER):
                        first_pass(b, PER * s + i)
                if b > 0:
                    if s == 0:
                        pe.wait_ge(*nm_loaded.at(48 * b))
                    second_pass(b - 1, s)
                    if s > 0:
                        weighted_values(b - 1, s - 1)
            if b > 0:
                weighted_values(b - 1, STEPS - 1)
            if b < B:
                pe.wait_ge(*p1_max.at(NG1 * (b + 1)))
                pe.wait_ge(*v_sb.at(b + 1))
                pe.transpose(bank[7][0:TPB * NH, 0:P], NM[:, b, :, :].rearrange("p h t -> p (h t)"),
                             k.ident[:, :]).then_inc(nm_psum.semaphore, 1)
        pe.wait_ge(*av_out.at(B * NHG))
        for t in range(NT):
            for hg in range(NHG):
                ins = pe.matmul(bank[0][:, (t * NHG + hg) * 4:(t * NHG + hg + 1) * 4], OT[:, hg, t * P:(t + 1) * P],
                                W("pick"), start=True, stop=True)
        ins.then_inc(den_psum.semaphore, 1)

        def spread(t):
            pe.wait_ge(*wide_ready.at(t + 1))
            if t >= 3:
                pe.wait_ge(*normed.at(t - 2))
            for hg in range(NHG):
                ins = pe.matmul(bank[1 + t % 3][:, hg * P:(hg + 1) * P], RX[t % 2][:, hg * P:(hg + 1) * P],
                                k.ident[:, :], start=True, stop=True)
            ins.then_inc(bc_psum.semaphore, 1)

        def project(t):
            pe.wait_ge(*normed.at(t + 1))
            if t >= 4:
                pe.wait_ge(k.x_tiles, NT * number + t - 3)
            dst = bank[4 + t % 4][:, 0:P]
            if masked:
                pe.matmul(dst, k.xnT[:, t * P:(t + 1) * P], W("ox"), start=True, stop=False)
            for hg in range(NHG):
                ins = pe.matmul(dst, OTn[t % 2][:, hg, :], W("o")[:, hg, :], start=hg == 0 and not masked,
                                stop=hg == NHG - 1)
            ins.then_inc(out_psum.semaphore, 1)

        for t in range(NT + 1):
            if t < NT:
                spread(t)
            if t > 0:
                project(t - 1)

    def scalar(act):
        k.norm.scalar(act, use, k.xnT)
        act.wait_ge(*fill_done.at(1))
        if not masked:
            act.activation(cp[0], k.ctxT[:, 0, :], ACT.Copy).then_inc(part.semaphore, 1)
            act.wait_ge(*rest.at(1))
            act.activation(cp[1], q32, ACT.Copy).then_inc(part.semaphore, 1)
            for h in range(2):
                act.wait_ge(*k_psum.at(h + 1))
                act.activation(k32[:, h * HALF:(h + 1) * HALF], k.bank[2 + h][:, :], ACT.Copy).then_inc(k_sb.semaphore, 1)
            act.wait_ge(*rest.at(2))
            for h in range(2):
                act.wait_ge(*q_psum.at(h + 1))
                act.activation(q32[:, h * HALF:(h + 1) * HALF], k.bank[h][:, :], ACT.Copy).then_inc(q_sb.semaphore, 1)
        n = 0 if masked else 2
        for src, parts, ready in ((k32, kp, k_sb), (q32, qp, q_sb)):
            act.wait_ge(*ready.at(2))
            act.activation(parts[0], src, ACT.Copy).then_inc(part.semaphore, 1)
            act.wait_ge(*rest.at(n + 1))
            act.activation(parts[1], src, ACT.Copy).then_inc(part.semaphore, 1)
            n += 2

        def maxima(b):
            act.wait_ge(*nm_psum.at(b + 1))
            if b >= 1:
                act.wait_ge(*nm_loaded.at(48 * b))
            rows = slice(0, TPB * NH)
            act.activation(NMp[0][rows, :], k.bank[7][rows, 0:P], ACT.Copy).then_inc(nm_part.semaphore, 1)
            act.wait_ge(*nm_rest.at(2 * b + 1))
            act.activation(NMp[1][rows, :], NMr[rows, :], ACT.Copy).then_inc(nm_part.semaphore, 1)

        for b in range(B):
            maxima(b)
            for s in range(STEPS):
                g = b * STEPS + s
                act.wait_ge(*p2_psum.at(g + 1))
                if g >= 2:
                    act.wait_ge(*av_done.at(g - 1))
                act.activation(PT[g % 2].rearrange("p (a n) -> p a n", a=2), k.pair(2 + 2 * (g % 2)),
                               ACT.Exp, scale=scale).then_inc(p2_exp.semaphore, 1)
        act.wait_ge(*den_ready.at(1))
        for t in range(NT):
            if t >= 2:
                act.wait_ge(*bc_psum.at(t - 1))
            act.activation(RX[t % 2].rearrange("p (h s) -> p h s", h=NH),
                           R[:, t, :].unsqueeze(2).broadcast_to([P, NH, SLOT]), ACT.Copy).then_inc(wide_ready.semaphore, 1)

    def gpsimd(pool):
        k.norm.gpsimd(pool, use)
        for i in range(2):
            pool.memset(QS[i][:, :, :], 1.0)
            pool.memset(KS[i][:, :, :], 1.0)
            pool.memset(VA[i][:, :, :, :], 0.0).then_inc(k.pool_chain, 1)
            k.pool_count += 1
        pool.wait_ge(k.pool_chain, k.pool_count)
        pool.memset(VA[0][:, :, :, HD], 1.0)
        pool.memset(VA[1][:, :, :, HD], 1.0).then_inc(fill_done.semaphore, 1)

    def sync(sp):
        def store(dram, parts, count):
            sp.wait_ge(*count[0])
            sp.dma_start(dram[0], parts[0]).then_inc(stored.semaphore, 16)
            sp.wait_ge(*count[1])
            sp.dma_start(dram[1], parts[1]).then_inc(stored.semaphore, 16)
            sp.wait_ge(*count[2])
            sp.dma_start(dram[2], parts[2]).then_inc(stored.semaphore, 16)

        n = 0
        if not masked:
            store(c_dram, cp, (part.at(1), part.at(2), rest.at(2)))
            n = 2
        store(k_dram, kp, (part.at(n + 1), part.at(n + 2), rest.at(n + 2)))
        store(q_dram, qp, (part.at(n + 3), part.at(n + 4), rest.at(n + 4)))
        sp.wait_ge(*stored.at(16 * (6 if masked else 9)))
        sp.wait_ge(*fill_done.at(1))

        def heads(dram, i, b):
            return dram[i].rearrange("(h d) t -> d h t", d=HD)[:, :, b * S:(b + 1) * S]

        def load(b):
            if b >= 2:
                sp.wait_ge(*av_done.at(STEPS * (b - 1)))
            for r, (iq, ik) in enumerate(TERMS):
                rows = slice(r * HD, (r + 1) * HD)
                sp.dma_start(QS[b % 2][rows, :, :], heads(q_dram, iq, b)).then_inc(loaded[b % 2].semaphore, 16)
                sp.dma_start(KS[b % 2][rows, :, NK - S:NK], heads(k_dram, ik, b)).then_inc(loaded[b % 2].semaphore, 16)
                if not masked:
                    sp.dma_start(KS[b % 2][rows, :, 0:S], heads(c_dram, ik, b)).then_inc(loaded[b % 2].semaphore, 16)
            if masked:
                sp.dma_start(KS[b % 2][R_MASK:R_MASK + 1, :, :],
                             k.mask_bias[0:1, b * S:(b + 1) * S].unsqueeze(1).broadcast_to([1, NH, S]))\
                    .then_inc(loaded[b % 2].semaphore, 16)

        load(0)
        load(1)
        for b in range(B):
            for i in range(3):
                if i < 2:
                    sp.wait_ge(*nm_part.at(2 * b + i + 1))
                else:
                    sp.wait_ge(*nm_rest.at(2 * b + 2))
                sp.dma_start(QS[b % 2][R_MAX + i:R_MAX + i + 1, :, :].rearrange("p h (t n) -> p (h t) n", t=TPB),
                             NMp[i][0:TPB * NH, :]).then_inc(nm_loaded.semaphore, 16)
            if 1 <= b < B - 1:
                load(b + 1)

    def vector(dve, chain):
        k.norm.vector(dve, chain, use, k.x, k.xn, eps)
        bank = k.bank
        dve.wait_ge(k.weights[name], 16)
        if masked:
            dve.wait_ge(k.mask_ready, 1)
            for src, dst, bias, ready, done in ((2, k32, "bk", k_psum, k_sb), (0, q32, "bq", q_psum, q_sb)):
                for h in range(2):
                    cols = slice(h * HALF, (h + 1) * HALF)
                    dve.wait_ge(*ready.at(h + 1))
                    dve.scalar_tensor_tensor(out=dst[:, cols], in0=bank[src + h][:, :], scalar=W(bias),
                                             in1=k.mask_bc[:, cols], op0=ALU.add, op1=ALU.mult).then_inc(done.semaphore, 1)
        n = 0
        if not masked:
            dve.wait_ge(*part.at(1))
            dve.tensor_tensor(q32, k.ctxT[:, 0, :], cp[0], ALU.subtract).then_inc(rest.semaphore, 1)
            dve.wait_ge(*part.at(2))
            dve.tensor_tensor(cp[2], q32, cp[1], ALU.subtract).then_inc(rest.semaphore, 1)
            n = 2
        for src, parts in ((k32, kp), (q32, qp)):
            dve.wait_ge(*part.at(n + 1))
            dve.tensor_tensor(src, src, parts[0], ALU.subtract).then_inc(rest.semaphore, 1)
            dve.wait_ge(*part.at(n + 2))
            dve.tensor_tensor(parts[2], src, parts[1], ALU.subtract).then_inc(rest.semaphore, 1)
            n += 2
        dve.wait_ge(*fill_done.at(1))

        def values(b):
            dve.wait_ge(*v_psum.at(b + 1))
            if b >= 2:
                dve.wait_ge(*av_done.at(STEPS * (b - 1)))
            dst = VA[b % 2][:, key_tiles - TPB:key_tiles, :, 0:HD]
            src = bank[7][:, 0:TPB * P].rearrange("p (t h d) -> p t h d", t=TPB, h=NH)
            if masked:
                tmp = vtmp[:, 0:TPB * P].rearrange("p (t n) -> p t n", t=TPB)
                chain.then(dve.tensor_tensor(tmp, bank[7][:, 0:TPB * P].rearrange("p (t n) -> p t n", t=TPB),
                                             W("bv").unsqueeze(1).broadcast_to([P, TPB, P]), ALU.add))
                for t in range(TPB):
                    tt = b * TPB + t
                    ins = dve.tensor_scalar(VA[b % 2][:, t, :, 0:HD],
                                            vtmp[:, t * P:(t + 1) * P].rearrange("p (h d) -> p h d", h=NH),
                                            k.mask_col[:, tt:tt + 1], None, ALU.mult)
            else:
                for t in range(TPB):
                    dve.tensor_copy(VA[b % 2][:, t, :, 0:HD],
                                    k.ctx_sb[:, b * TPB + t, P:2 * P].rearrange("p (h d) -> p h d", h=NH))
                for t in range(TPB):
                    ins = dve.tensor_copy(VA[b % 2][:, TPB + t, :, 0:HD],
                                          bank[7][:, t * P:(t + 1) * P].rearrange("p (h d) -> p h d", h=NH))
            ins.then_inc(v_sb.semaphore, 1)

        def row_maxima(b, n):
            g = b * NG1 + n
            t, h0 = n // (NG1 // TPB), n % (NG1 // TPB) * HPG
            dve.wait_ge(*p1_psum.at(g + 1))
            dve.tensor_reduce(NM[:, b, h0:h0 + HPG, t], bank[g % 2][:, :].rearrange("p (j n) -> p j n", j=HPG),
                              AX.X, ALU.max, negate=True).then_inc(p1_max.semaphore, 1)

        for b in range(B + 1):
            if b < B:
                values(b)
            for s in range(STEPS):
                if b < B:
                    for i in range(PER):
                        row_maxima(b, PER * s + i)
                if b > 0 and s > 0 and s % key_tiles == 0:
                    take_output(dve, b - 1, s // key_tiles - 1)
            if b > 0:
                take_output(dve, b - 1, NHG - 1)
            if b < B:
                rows = slice(0, TPB * NH)
                dve.wait_ge(*nm_part.at(2 * b + 1))
                dve.tensor_tensor(NMr[rows, :], bank[7][rows, 0:P], NMp[0][rows, :], ALU.subtract).then_inc(nm_rest.semaphore, 1)
                dve.wait_ge(*nm_part.at(2 * b + 2))
                if b >= 1:
                    dve.wait_ge(*nm_loaded.at(48 * b))
                dve.tensor_tensor(NMp[2][rows, :], NMr[rows, :], NMp[1][rows, :], ALU.subtract).then_inc(nm_rest.semaphore, 1)
        dve.wait_ge(*den_psum.at(1))
        dve.reciprocal(R.rearrange("p t h -> p (t h)"), bank[0][:, 0:NT * NH]).then_inc(den_ready.semaphore, 1)

        def add_output(t):
            dve.wait_ge(*out_psum.at(t + 1))
            dve.tensor_tensor(k.x[:, t, :], k.x[:, t, :], bank[4 + t % 4][:, 0:P], ALU.add).then_inc(k.x_tiles, 1)

        chain.then(dve.tensor_tensor(k.x[:, :, :], k.x[:, :, :], W("bo").unsqueeze(1).broadcast_to([P, NT, P]), ALU.add))
        for t in range(NT):
            dve.wait_ge(*bc_psum.at(t + 1))
            if t >= 2:
                dve.wait_ge(*out_psum.at(t - 1))
            dve.tensor_tensor(OTn[t % 2], OT[:, :, t * P:(t + 1) * P],
                              bank[1 + t % 3][:, 0:NHG * P].rearrange("p (g n) -> p g n", g=NHG), ALU.mult)\
                .then_inc(normed.semaphore, 1)
            if t >= 1:
                add_output(t - 1)
        add_output(NT - 1)
        dve.wait_ge(k.x_tiles, NT * (number + 1))

    def take_output(dve, b, hg):
        dve.wait_ge(*av_done.at(STEPS * b + (hg + 1) * key_tiles))
        dve.tensor_copy(OT[:, hg, b * S:(b + 1) * S], k.bank[6][:, 0:S]).then_inc(av_out.semaphore, 1)

    return tensor, scalar, vector, gpsimd, sync


def first_of_maxima(dve, chain, values, weights, maxima, tagged, top, chosen, shape):
    chain.then(dve.tensor_reduce(maxima, values, AX.X, ALU.max))
    chain.then(dve.tensor_tensor(tagged, values, maxima.unsqueeze(2).broadcast_to(shape), ALU.is_equal))
    chain.then(dve.tensor_tensor(tagged, tagged, weights, ALU.mult))
    chain.then(dve.tensor_reduce(top, tagged, AX.X, ALU.max))
    chain.then(dve.tensor_tensor(chosen, tagged, top.unsqueeze(2).broadcast_to(shape), ALU.is_equal))


def dense_experts(k, name, number, E, W, routing):
    ROUNDS = 4 if routing else 1
    FT = 4
    ITEMS = 2 * E
    TPH = NT // 2
    shape = [P, NT, E]
    k.carve_from(REGION_B)
    H = [k.carve(F32, FT, HALF) for _ in range(2)]
    hT = None if routing else [k.carve(F32, T) for _ in range(2)]
    xl = None if routing else k.carve(F32, NT, D)
    xlT = None if routing else k.carve(F32, T)
    cwT = k.carve(F32, T)
    logits, tagged, sel1, sel2, low = (k.carve(F32, NT, E) for _ in range(5))
    cw = k.carve(F32, NT, E)
    m1, m2, top, th, w1, w2 = (k.carve(F32, NT) for _ in range(6))

    use = k.norm_use[number]

    def count(what, total):
        return k.count(f"experts_{what}", total)

    logits_psum = count("logits_psum", ROUNDS)
    margin = count("margin", ROUNDS)
    tanh_ready = count("tanh_ready", ROUNDS)
    cw_ready = count("cw_ready", ROUNDS)
    cwT_psum = count("cwT_psum", 2 * ROUNDS)
    cwT_sb = count("cwT_sb", 2 * ROUNDS)
    b2_psum = count("b2_psum", 2 * ROUNDS)
    turned = count("turned", 2 * (ROUNDS - 1))
    T_ready = count("T_ready", 2 * (ROUNDS - 1))
    up_psum = count("up_psum", FT * ITEMS * ROUNDS)
    h_ready = count("h_ready", FT * ITEMS * ROUNDS)
    down_psum = count("down_psum", ITEMS * ROUNDS)
    combined = count("combined", ITEMS * ROUNDS)
    hT_ready = count("hT_ready", 0 if routing else E)

    acc = k.xn

    def x_for(pe, e, half):
        cols = slice(half * HALF, (half + 1) * HALF)
        return k.xnT[:, cols] if routing else hT[e % 2][:, cols]

    def tensor(pe):
        bank = k.bank
        pe.wait_ge(k.weights[name], 16 if routing else 32)

        def up(r, i):
            g = r * ITEMS + i
            e, half = i // 2, i % 2
            if not routing and half == 0:
                pe.wait_ge(*hT_ready.at(e + 1))
            for f in range(FT):
                if g >= 1:
                    pe.wait_ge(*h_ready.at(FT * (g - 1) + f + 1))
                pe.matmul(bank[f], W("w1")[:, e, f * P:(f + 1) * P], x_for(pe, e, half), start=True, stop=True)\
                    .then_inc(up_psum.semaphore, 1)

        def down(r, i):
            g = r * ITEMS + i
            pe.wait_ge(*h_ready.at(FT * (g + 1)))
            if g >= 2:
                pe.wait_ge(*combined.at(g - 1))
            for t in range(TPH):
                for f in range(FT):
                    ins = pe.matmul(bank[4 + g % 2][:, t * P:(t + 1) * P], H[g % 2][:, f, t * P:(t + 1) * P],
                                    W("w2")[:, i // 2, f, :], start=f == 0, stop=f == FT - 1)
            ins.then_inc(down_psum.semaphore, 1)

        for r in range(ROUNDS):
            if r == 0:
                k.norm.tensor(pe, use, k.xn)
                if not routing:
                    k.norm2.tensor(pe, 1, xl, banks=(4, 5))
                turned_in = (k.norm.T_ready, 2 * use + 2)
            else:
                for t in range(NT):
                    pe.wait_ge(*combined.at(r * ITEMS - 1 + t // TPH))
                    ins = pe.transpose(bank[6 + t // TPH][:, (t % TPH) * P:(t % TPH + 1) * P], k.xn[:, t, :],
                                       k.ident[:, :])
                    if t % TPH == TPH - 1:
                        ins.then_inc(turned.semaphore, 1)
                turned_in = T_ready.at(2 * r)
            pe.wait_ge(*turned_in)
            for t in range(NT):
                ins = pe.matmul(bank[6][:, t * E:(t + 1) * E], k.xnT[:, t * P:(t + 1) * P], W("router")[:, r, :],
                                start=True, stop=True)
            ins.then_inc(logits_psum.semaphore, 1)
            up(r, 0)
            up(r, 1)
            pe.wait_ge(*cw_ready.at(r + 1))
            for t in range(NT):
                ins = pe.transpose(bank[6 + t // TPH][0:E, (t % TPH) * P:(t % TPH + 1) * P], cw[:, t, :],
                                   k.ident[:, :])
                if t % TPH == TPH - 1:
                    ins.then_inc(cwT_psum.semaphore, 1)
            down(r, 0)
            for t in range(NT):
                pe.wait_ge(*cwT_sb.at(2 * r + t // TPH + 1))
                ins = pe.matmul(bank[6 + t // TPH][:, (t % TPH) * P:(t % TPH + 1) * P], cwT[0:E, t * P:(t + 1) * P],
                                W("b2")[0:E, :], start=True, stop=True)
                if t % TPH == TPH - 1:
                    ins.then_inc(b2_psum.semaphore, 1)
            for i in range(2, ITEMS):
                up(r, i)
                down(r, i - 1)
            down(r, ITEMS - 1)

    def scalar(act):
        bank = k.bank
        act.wait_ge(k.weights[name], 16 if routing else 32)

        def hidden(r, i):
            g = r * ITEMS + i
            if g >= 2:
                act.wait_ge(*down_psum.at(g - 1))
            for f in range(FT):
                act.wait_ge(*up_psum.at(FT * g + f + 1))
                act.activation(H[g % 2][:, f, :], bank[f], ACT.Gelu_apprx_tanh if routing else ACT.Relu,
                               bias=W("b1")[:, (i // 2) * FT + f:(i // 2) * FT + f + 1]).then_inc(h_ready.semaphore, 1)

        for r in range(ROUNDS):
            if r == 0:
                k.norm.scalar(act, use, k.xnT)
                if not routing:
                    k.norm2.scalar(act, 1, xlT, banks=(4, 5))
            else:
                for h in range(2):
                    act.wait_ge(*turned.at(2 * (r - 1) + h + 1))
                    act.activation(k.xnT[:, h * HALF:(h + 1) * HALF], bank[6 + h], ACT.Copy).then_inc(T_ready.semaphore, 1)
            hidden(r, 0)
            act.wait_ge(*margin.at(r + 1))
            act.activation(th, m2, ACT.Tanh, scale=0.5).then_inc(tanh_ready.semaphore, 1)
            hidden(r, 1)
            for h in range(2):
                act.wait_ge(*cwT_psum.at(2 * r + h + 1))
                act.activation(cwT[0:E, h * HALF:(h + 1) * HALF], bank[6 + h][0:E, :], ACT.Copy).then_inc(cwT_sb.semaphore, 1)
            for i in range(2, ITEMS):
                hidden(r, i)

    def vector(dve, chain):
        bank = k.bank
        k.norm.vector(dve, chain, use, k.x, k.xn, 1e-5)
        dve.wait_ge(k.weights[name], 16 if routing else 32)
        if not routing:
            dve.wait_ge(k.norm.ready, NT * (use + 1))
            k.norm2.vector(dve, chain, 1, k.xn, xl, 1e-5)
        falling = W("falling").unsqueeze(1).broadcast_to(shape)
        for r in range(ROUNDS):
            dve.wait_ge(*logits_psum.at(r + 1))
            src = bank[6][:, 0:NT * E].rearrange("p (t e) -> p t e", t=NT)
            if routing:
                chain.then(dve.tensor_tensor(logits, src, W("bg")[:, r, :].unsqueeze(1).broadcast_to(shape), ALU.add))
            else:
                chain.then(dve.tensor_copy(logits, src))
            first_of_maxima(dve, chain, logits, falling, m1, tagged, top, sel1, shape)
            if routing:
                chain.then(dve.scalar_tensor_tensor(out=low, in0=sel1, scalar=-3.0e38, in1=logits, op0=ALU.mult,
                                                    op1=ALU.add))
                first_of_maxima(dve, chain, low, falling, m2, tagged, top, sel2, shape)
                dve.tensor_tensor(m2, m1, m2, ALU.subtract).then_inc(margin.semaphore, 1)
            else:
                dve.tensor_copy(m2, m1).then_inc(margin.semaphore, 1)
            dve.wait_ge(*tanh_ready.at(r + 1))
            chain.then(dve.tensor_scalar(w1, th, 0.5, 0.5, ALU.mult, ALU.add))
            if routing:
                chain.then(dve.tensor_scalar(w2, th, -0.5, 0.5, ALU.mult, ALU.add))
                chain.then(dve.tensor_tensor(sel1, sel1, w1.unsqueeze(2).broadcast_to(shape), ALU.mult))
                chain.then(dve.tensor_tensor(sel2, sel2, w2.unsqueeze(2).broadcast_to(shape), ALU.mult))
                dve.tensor_tensor(cw, sel1, sel2, ALU.add).then_inc(cw_ready.semaphore, 1)
            else:
                dve.tensor_tensor(cw, sel1, w1.unsqueeze(2).broadcast_to(shape), ALU.mult).then_inc(cw_ready.semaphore, 1)
            for h in range(2):
                dve.wait_ge(*b2_psum.at(2 * r + h + 1))
                part = acc[:, h * TPH:(h + 1) * TPH, :]
                chain.then(dve.tensor_tensor(part, part, bank[6 + h].rearrange("p (t d) -> p t d", t=TPH), ALU.add))
            for i in range(ITEMS):
                g = r * ITEMS + i
                dve.wait_ge(*down_psum.at(g + 1))
                if i >= 2:
                    dve.wait_ge(*combined.at(g - 1))
                for t in range(TPH):
                    tt = (i % 2) * TPH + t
                    ins = dve.scalar_tensor_tensor(out=acc[:, tt, :], in0=bank[4 + g % 2][:, t * P:(t + 1) * P],
                                                   scalar=cw[:, tt, i // 2:i // 2 + 1], in1=acc[:, tt, :],
                                                   op0=ALU.mult, op1=ALU.add)
                ins.then_inc(combined.semaphore, 1)
        dve.wait_ge(*combined.at(ROUNDS * ITEMS))
        dve.tensor_tensor(k.x[:, :, :], k.x[:, :, :], k.xn[:, :, :], ALU.add).then_inc(k.x_tiles, NT)
        dve.wait_ge(k.x_tiles, NT * (number + 1))

    def gpsimd(pool):
        k.norm.gpsimd(pool, use)
        if not routing:
            k.norm2.gpsimd(pool, 1)
            pool.wait_ge(k.weights[name], 16 if routing else 32)
            pool.wait_ge(k.norm2.T_ready, 4)
            for e in range(E):
                if e >= 2:
                    pool.wait_ge(*h_ready.at(2 * FT * (e - 1)))
                pool.tensor_scalar(hT[e % 2], xlT, W("g")[:, e:e + 1], W("b")[:, e:e + 1],
                                   ALU.mult, ALU.add).then_inc(hT_ready.semaphore, 1)

    def sync(sp):
        pass

    return tensor, scalar, vector, gpsimd, sync


def gated_attention(k, name, number, W):
    NH, E = 8, 8
    HD = P
    GROUPS = NT * 2 * NH
    scale = float(HD) ** -0.5
    k.carve_from(REGION_B)
    qT, kT, V, oT = ([k.carve(F32, T) for _ in range(2)] for _ in range(4))
    PR = k.carve(F32, B, TPB, S)
    PT = k.carve(F32, B, TPB, S)
    probs = k.carve(F32, GROUPS, E)
    gate = k.carve(F32, GROUPS, E)
    HALF_E = E // 2
    mark = k.carve_mark()
    scaled = [k.carve(F32, HALF_E, P) for _ in range(2)]
    rest = [k.carve(F32, P) for _ in range(2)]
    k.carve_back(mark)
    sel1 = k.carve(F32, GROUPS, E)
    sel2 = k.carve(F32, GROUPS, E)
    m1, m2, top = (k.carve(F32, GROUPS) for _ in range(3))
    NM = k.carve(F32, NT)
    den, rec = k.carve(F32, 2, NT), k.carve(F32, NT)
    og = [k.carve(F32, NT, E) for _ in range(2)]

    use = k.norm_use[number]

    def sem(what):
        return k.sem(f"{name}_{what}")

    v_weights, o_weights = k.weights["l1v"], k.weights["l1o"]
    sel_psum = sem("sel_psum")
    probs_ready = sem("probs_ready")
    qk_psum = sem("qk_psum")
    qk_sb = sem("qk_sb")
    ex_psum = sem("ex_psum")
    first_half = sem("first_half")
    scaled_ready = sem("scaled_ready")
    rest_ready = sem("rest_ready")
    summed = sem("summed")
    gates_ready = sem("gates_ready")
    score_psum = sem("score_psum")
    max_ready = sem("max_ready")
    exp_ready = sem("exp_ready")
    pt_psum = sem("pt_psum")
    pt_sb = sem("pt_sb")
    av_psum = sem("av_psum")
    av_sb = sem("av_sb")
    og_ready = sem("og_ready")

    def values_block(h):
        return 0 if h == 0 else 2 * h - 1

    def output_block(h):
        return min(2 * h + 2, 2 * NH - 1)

    def tensor(pe):
        bank = k.bank
        k.norm.tensor(pe, use, k.xn)
        pe.wait_ge(k.weights[name], 16)
        pe.wait_ge(k.norm.T_ready, 2 * use + 2)
        for t in range(NT):
            ins = pe.matmul(bank[6 + t // 4][:, (t % 4) * P:(t % 4 + 1) * P], k.xnT[:, t * P:(t + 1) * P], W("sel"),
                            start=True, stop=True)
        ins.then_inc(sel_psum, 1)

        def queries_and_keys(h):
            for i in range(4):
                if h == 0 and i == 2:
                    pe.wait_ge(probs_ready, 1)
                if h > 0:
                    pe.wait_ge(av_sb, B * (h - 1) + i + 1)
                pe.matmul(bank[4 + i], W("q" if i < 2 else "k")[:, h, :], k.xnT[:, (i % 2) * HALF:(i % 2 + 1) * HALF],
                          start=True, stop=True).then_inc(qk_psum, 1)

        def experts(block, src, weights, h):
            for t in range(NT):
                n = block * NT + t
                for c in range(2):
                    if n >= 2:
                        pe.wait_ge(first_half if c == 0 else scaled_ready, n - 1)
                    ins = pe.matmul(bank[2 * (n % 2) + c], src[:, t * P:(t + 1) * P],
                                    weights[:, h * 2 * HALF + c * HALF:h * 2 * HALF + (c + 1) * HALF],
                                    start=True, stop=True)
                ins.then_inc(ex_psum, 1)

        pe.wait_ge(v_weights, 16)
        for h in range(NH + 1):
            if h < NH:
                queries_and_keys(h)
                experts(values_block(h), k.xnT, k.region["A"], h)
                for b in range(B):
                    if b == 0:
                        pe.wait_ge(qk_sb, 4 * (h + 1))
                    for t in range(TPB):
                        tt = b * TPB + t
                        ins = pe.matmul(bank[4 + b][:, t * S:(t + 1) * S], qT[h % 2][:, tt * P:(tt + 1) * P],
                                        kT[h % 2][:, b * S:(b + 1) * S], start=True, stop=True)
                    ins.then_inc(score_psum, 1)
            if h > 0:
                if h == 1:
                    pe.wait_ge(o_weights, 16)
                pe.wait_ge(av_sb, B * h)
                experts(output_block(h - 1), oT[(h - 1) % 2], k.region["B"], h - 1)
            if h < NH:
                for b in range(B):
                    pe.wait_ge(exp_ready, B * h + b + 1)
                    for kt in range(TPB):
                        for t in range(TPB):
                            ins = pe.transpose(bank[4 + b][:, kt * S + t * P:kt * S + (t + 1) * P],
                                               PR[:, b, t, kt * P:(kt + 1) * P], k.ident[:, :])
                    ins.then_inc(pt_psum, 1)
                for b in range(B):
                    pe.wait_ge(pt_sb, B * h + b + 1)
                    if b == 0:
                        pe.wait_ge(summed, NT * (values_block(h) + 1))
                    for kt in range(TPB):
                        tt = b * TPB + kt
                        ins = pe.matmul(bank[4 + b][:, 0:S], V[h % 2][:, tt * P:(tt + 1) * P], PT[:, b, kt, :],
                                        start=kt == 0, stop=kt == TPB - 1)
                    ins.then_inc(av_psum, 1)

    def scalar(act):
        bank = k.bank
        k.norm.scalar(act, use, k.xnT)
        act.wait_ge(sel_psum, 1)
        act.activation(probs.rearrange("p (a g) e -> p a (g e)", a=2), k.pair(6), ACT.Sigmoid).then_inc(probs_ready, 1)

        def scale_products(n, scalars):
            act.wait_ge(ex_psum, n + 1)
            if n >= 2:
                act.wait_ge(rest_ready, n - 1)
            for e in range(HALF_E):
                ins = act.activation(scaled[n % 2][:, e, :], bank[2 * (n % 2) + 1][:, e * P:(e + 1) * P], ACT.Copy,
                                     scale=scalars[:, n % NT, HALF_E + e:HALF_E + e + 1])
            ins.then_inc(scaled_ready, 1)

        def exponentials(h, b):
            act.wait_ge(max_ready, B * h + b + 1)
            if h >= 1 and b == 0:
                act.wait_ge(pt_psum, B * h)
            if h >= 2 and b == 0:
                act.wait_ge(og_ready, h - 1)
            for t in range(TPB):
                tt = b * TPB + t
                ins = act.activation(PR[:, b, t, :], bank[4 + b][:, t * S:(t + 1) * S], ACT.Exp,
                                     bias=NM[:, tt:tt + 1], accum_out=den[:, h % 2, tt:tt + 1])
            ins.then_inc(exp_ready, 1)

        gates = gate.rearrange("p (t a h) e -> p t a h e", t=NT, a=2)
        for h in range(NH + 1):
            if h < NH:
                for i in range(4):
                    act.wait_ge(qk_psum, 4 * h + i + 1)
                    dst = (qT if i < 2 else kT)[h % 2]
                    act.activation(dst[:, (i % 2) * HALF:(i % 2 + 1) * HALF], bank[4 + i], ACT.Copy,
                                   scale=scale if i < 2 else 1.0).then_inc(qk_sb, 1)
                if h == 0:
                    act.wait_ge(gates_ready, 1)
                for t in range(NT):
                    scale_products(values_block(h) * NT + t, gates[:, :, 0, h, :])
            for t in range(NT):
                if h > 0:
                    if t == 0:
                        act.wait_ge(og_ready, h)
                    scale_products(output_block(h - 1) * NT + t, og[(h - 1) % 2])
                if t % TPB == TPB - 1 and h < NH:
                    exponentials(h, t // TPB)
            if h == NH:
                break
            for b in range(B):
                act.wait_ge(pt_psum, B * h + b + 1)
                if h >= 1:
                    act.wait_ge(av_psum, B * (h - 1) + b + 1)
                act.activation(PT[:, b, :, :].rearrange("p a n -> p (a n)"), bank[4 + b], ACT.Copy).then_inc(pt_sb, 1)
            for b in range(B):
                act.wait_ge(av_psum, B * h + b + 1)
                if h >= 2 and b == 0:
                    act.wait_ge(ex_psum, NT * (output_block(h - 2) + 1))
                act.activation(oT[h % 2][:, b * S:(b + 1) * S], bank[4 + b][:, 0:S], ACT.Copy).then_inc(av_sb, 1)

    def vector(dve, chain):
        bank = k.bank
        k.norm.vector(dve, chain, use, k.x, k.xn, 1e-5)
        dve.wait_ge(k.weights[name], 16)
        dve.wait_ge(probs_ready, 1)
        shape = [P, GROUPS, E]
        falling = W("falling").unsqueeze(1).broadcast_to(shape)
        first_of_maxima(dve, chain, probs, falling, m1, gate, top, sel1, shape)
        chain.then(dve.scalar_tensor_tensor(out=gate, in0=sel1, scalar=-2.0, in1=probs, op0=ALU.mult, op1=ALU.add))
        chain.then(dve.tensor_copy(sel2, gate))
        first_of_maxima(dve, chain, sel2, falling, m2, gate, top, sel2, shape)
        chain.then(dve.tensor_tensor(sel1, sel1, sel2, ALU.add))
        chain.then(dve.tensor_tensor(gate, sel1, probs, ALU.mult))
        chain.then(dve.tensor_tensor(m1, m1, m2, ALU.add))
        chain.then(dve.tensor_scalar(m1, m1, 1.0e-9, None, ALU.max))
        chain.then(dve.reciprocal(m2, m1))
        chain.then(dve.tensor_scalar(m2, m2, W("route_scale"), None, ALU.mult))
        dve.tensor_tensor(gate, gate, m2.unsqueeze(2).broadcast_to(shape), ALU.mult).then_inc(gates_ready, 1)
        dve.wait_ge(gates_ready, 1)
        gates = gate.rearrange("p (t a h) e -> p t a h e", t=NT, a=2)

        def sum_first_half(n, dst, scalars, first):
            dve.wait_ge(ex_psum, n + 1)
            for e in range(HALF_E):
                src = bank[2 * (n % 2)][:, e * P:(e + 1) * P]
                scalar = scalars[:, n % NT, e:e + 1]
                if e == 0 and first:
                    ins = dve.tensor_scalar(dst, src, scalar, None, ALU.mult)
                else:
                    ins = dve.scalar_tensor_tensor(out=dst, in0=src, scalar=scalar, in1=dst, op0=ALU.mult, op1=ALU.add)
                if e < HALF_E - 1:
                    chain.then(ins)
            ins.then_inc(first_half, 1)

        def add_rest(n, dst, last):
            dve.wait_ge(rest_ready, n + 1)
            dve.wait_ge(first_half, n + 1)
            dve.tensor_tensor(dst, dst, rest[n % 2], ALU.add).then_inc(k.x_tiles if last else summed, 1)

        def sum_experts(block, dst, scalars, first, last=False, middle=None):
            for t in range(NT + 1):
                n = block * NT + t
                if t < NT:
                    sum_first_half(n, dst(t), scalars, first)
                if t > 0:
                    add_rest(n - 1, dst(t - 1), last)
                if t == NT // 2 and middle:
                    middle()

        def denominators(h):
            dve.wait_ge(exp_ready, B * (h + 1))
            if h >= 2:
                dve.wait_ge(summed, NT * (output_block(h - 2) + 1))
            chain.then(dve.reciprocal(rec, den[:, h % 2, :]))
            dve.tensor_tensor(og[h % 2], gates[:, :, 1, h, :], rec.unsqueeze(2).broadcast_to([P, NT, E]), ALU.mult)\
                .then_inc(og_ready, 1)

        for h in range(NH + 1):
            if h < NH:
                sum_experts(values_block(h), lambda t: V[h % 2][:, t * P:(t + 1) * P], gates[:, :, 0, h, :], True)
                if h >= 1:
                    dve.wait_ge(exp_ready, B * h)
                for b in range(B):
                    dve.wait_ge(score_psum, B * h + b + 1)
                    dve.tensor_reduce(NM[:, b * TPB:(b + 1) * TPB], bank[4 + b].rearrange("p (t n) -> p t n", t=TPB),
                                      AX.X, ALU.max, negate=True).then_inc(max_ready, 1)
            if h > 0:
                dve.wait_ge(og_ready, h)
                sum_experts(output_block(h - 1), lambda t: k.x[:, t, :], og[(h - 1) % 2], False, last=h == NH)
            if h < NH:
                denominators(h)
        dve.wait_ge(k.x_tiles, NT * (number + 1))

    def gpsimd(pool):
        k.norm.gpsimd(pool, use)
        for n in range(2 * NH * NT):
            pool.wait_ge(scaled_ready, n + 1)
            pool.tensor_tensor(scaled[n % 2][:, 0:2, :], scaled[n % 2][:, 0:2, :], scaled[n % 2][:, 2:4, :], ALU.add)\
                .then_inc(k.pool_chain, 1)
            k.pool_count += 1
            if n >= 2:
                if n - 2 < (2 * NH - 1) * NT:
                    pool.wait_ge(summed, n - 1)
                else:
                    pool.wait_ge(k.x_tiles, NT * number + n - 1 - (2 * NH - 1) * NT)
            pool.wait_ge(k.pool_chain, k.pool_count)
            pool.tensor_tensor(rest[n % 2], scaled[n % 2][:, 0, :], scaled[n % 2][:, 1, :], ALU.add).then_inc(rest_ready, 1)

    def sync(sp):
        sp.wait_ge(k.x_tiles, NT * number)
        k.load_weights(sp, k.dram, "l1o")
        sp.wait_ge(ex_psum, NT * (values_block(NH - 1) + 1))
        k.load_weights(sp, k.dram, "l2f")

    return tensor, scalar, vector, gpsimd, sync


PATCH_EPS = 1.0e-3
DT = -float(np.log(-np.expm1(-PATCH_EPS)))
KEEP = float(np.exp(-PATCH_EPS))


def patch_attention(k, name, number, W):
    k.carve_from(REGION_B)
    upto = k.carve(F32, TPB, S)
    ones = k.carve(F32, P)
    column = k.carve(F32, S)
    part_id = k.carve(F32, TPB)
    lens = k.carve(F32, NT)
    ends = k.carve(F32, NT)
    wrap = k.carve(F32, NT)
    hit = k.carve(F32, NT, S)
    bound = k.carve(F32, NT)
    plug = k.carve(F32, B, S)
    G = [k.carve(F32, B, S) for _ in range(TPB)]
    keep = [k.carve(F32, B, S) for _ in range(TPB)]
    u = k.carve(F32, NT, D)
    xr = k.carve(F32, NT, D)
    xrT = k.carve(F32, T)

    def sem(what):
        return k.sem(f"{name}_{what}")

    consts = sem("consts")
    lens_ready = sem("lens_ready")
    ends_psum = sem("ends_psum")
    hit_ready = sem("hit_ready")
    count_psum = sem("count_psum")
    bound_ready = sem("bound_ready")
    plug_psum = sem("plug_psum")
    gap_ready = sem("gap_ready")
    decay_ready = sem("decay_ready")
    G_ready = sem("G_ready")
    u_ready = sem("u_ready")
    out_psum = sem("out_psum")

    def tensor(pe):
        bank = k.bank
        pe.wait_ge(consts, 1)
        pe.wait_ge(lens_ready, 1)
        by_tile = lens.rearrange("p (b t) -> p t b", t=TPB)
        pe.matmul(bank[0][:, 0:B], upto[:, 0, 0:P], by_tile[:, 0, :], start=True, stop=True)
        pe.matmul(bank[0][:, B:2 * B], ones, by_tile[:, 0, :], start=True, stop=False)
        pe.matmul(bank[0][:, B:2 * B], upto[:, 0, 0:P], by_tile[:, 1, :], start=False, stop=True).then_inc(ends_psum, 1)
        pe.wait_ge(hit_ready, 1)
        for b in range(B):
            for t in range(TPB):
                for j in range(TPB):
                    ins = pe.matmul(bank[1][:, b * TPB + t:b * TPB + t + 1], hit[:, b * TPB + j, t * P:(t + 1) * P],
                                    ones[:, 0:1], start=j == 0, stop=j == TPB - 1)
        ins.then_inc(count_psum, 1)
        pe.wait_ge(bound_ready, 1)
        for b in range(B):
            for t in range(TPB):
                ins = pe.matmul(bank[2 + b // 2][:, (b % 2) * S:(b % 2 + 1) * S],
                                bound[:, b * TPB + t:b * TPB + t + 1].broadcast_to([P, P]), upto[:, t, :],
                                start=t == 0, stop=t == TPB - 1)
        ins.then_inc(plug_psum, 1)
        k.norm2.tensor(pe, 0, xr, banks=(6, 7))
        pe.wait_ge(k.weights[name], 16)
        pe.wait_ge(k.norm2.T_ready, 2)
        pe.wait_ge(G_ready, TPB)
        pe.wait_ge(u_ready, 1)
        for t in range(NT):
            if t >= 4:
                pe.wait_ge(k.x_tiles, NT * number + t - 3)
            b, dst = t // TPB, bank[4 + t % 4][:, 0:P] if t % 4 < 2 else bank[t % 4][:, 0:P]
            for j in range(TPB):
                pe.matmul(dst, G[j][:, b, (t % TPB) * P:(t % TPB + 1) * P], u[:, b * TPB + j, :], start=j == 0, stop=False)
            pe.matmul(dst, xrT[:, t * P:(t + 1) * P], W("w"), start=False, stop=True).then_inc(out_psum, 1)

    def scalar(act):
        for j in range(TPB):
            act.wait_ge(gap_ready, j + 1)
            act.activation(G[j], G[j], ACT.Exp, scale=-DT).then_inc(decay_ready, 1)
        act.wait_ge(k.weights[name], 16)
        k.norm2.scalar(act, 0, xrT, banks=(6, 7), scale=W("g_res"))

    def vector(dve, chain):
        bank = k.bank
        k.norm_plain.vector(dve, chain, 0, k.x, k.xn, 1e-5)
        dve.wait_ge(k.norm_plain.ready, NT)
        k.norm2.vector(dve, chain, 0, k.xn, xr, 1e-5, rms=True)
        dve.wait_ge(k.lens_loaded, 16)
        dve.wait_ge(k.weights[name], 16)
        dve.wait_ge(consts, 1)
        dve.tensor_copy(lens, k.lens[:, :]).then_inc(lens_ready, 1)
        k.norm_ctx.statistics(dve, chain, 0, k.ctx_sb, 1e-5, rms=True)
        chain.then(dve.tensor_scalar(k.rstd[:, :], k.rstd[:, :], KEEP, None, ALU.mult))
        for t in range(NT):
            ins = dve.scalar_tensor_tensor(out=u[:, t, :], in0=k.ctx_sb[:, t, 0:D], scalar=k.rstd[:, t:t + 1],
                                           in1=W("g_init"), op0=ALU.mult, op1=ALU.mult)
        ins.then_inc(u_ready, 1)
        dve.wait_ge(ends_psum, 1)
        chain.then(dve.tensor_scalar(ends.rearrange("p (b t) -> p t b", t=TPB),
                                     bank[0][:, 0:NT].rearrange("p (t b) -> p t b", t=TPB), 1.0, None, ALU.subtract))
        chain.then(dve.tensor_scalar(wrap, ends, 0.0, float(S), ALU.is_lt, ALU.mult))
        chain.then(dve.tensor_tensor(ends, ends, wrap, ALU.add))
        for t in range(NT):
            ins = dve.tensor_scalar(hit[:, t, :], column, ends[:, t:t + 1], None, ALU.is_equal)
        ins.then_inc(hit_ready, 1)
        dve.wait_ge(count_psum, 1)
        dve.tensor_scalar(bound, bank[1][:, 0:NT], 1.0, None, ALU.min).then_inc(bound_ready, 1)
        dve.wait_ge(plug_psum, 1)
        flat = plug.rearrange("p b s -> p (b s)")
        chain.then(dve.tensor_scalar(flat.rearrange("p (a n) -> p a n", a=2), k.pair(2), 1.0, 0.0, ALU.subtract, ALU.max))
        chain.then(dve.tensor_scalar(flat, flat, float(S - 1), None, ALU.min))
        for j in range(TPB):
            dve.tensor_scalar(G[j], plug, part_id[:, j:j + 1], 0.0, ALU.subtract, ALU.max).then_inc(gap_ready, 1)
            chain.then(dve.tensor_scalar(keep[j], plug, part_id[:, j:j + 1], None, ALU.is_ge))
        for j in range(TPB):
            dve.wait_ge(decay_ready, j + 1)
            dve.tensor_tensor(G[j], G[j], keep[j], ALU.mult).then_inc(G_ready, 1)
        chain.then(dve.tensor_tensor(k.x[:, :, :], k.x[:, :, :], W("b").unsqueeze(1).broadcast_to([P, NT, P]), ALU.add))
        for t in range(NT):
            dve.wait_ge(out_psum, t + 1)
            src = bank[4 + t % 4][:, 0:P] if t % 4 < 2 else bank[t % 4][:, 0:P]
            dve.tensor_tensor(k.x[:, t, :], k.x[:, t, :], src, ALU.add).then_inc(k.x_tiles, 1)
        dve.wait_ge(k.x_tiles, NT * (number + 1))

    def gpsimd(pool):
        k.norm_plain.gpsimd(pool, 0)
        k.norm2.gpsimd(pool, 0)
        pool.memset(ones, 1.0)
        pool.memset(upto, 1.0).then_inc(k.pool_chain, 1)
        k.pool_count += 1
        pool.iota(column, [[1, S]], base=0, channel_multiplier=0, allow_small_or_imprecise_dtypes=True)
        pool.iota(part_id, [[P, TPB]], base=0, channel_multiplier=1, allow_small_or_imprecise_dtypes=True)
        pool.wait_ge(k.pool_chain, k.pool_count)
        pool.affine_select(out=upto, in_=upto, compare_op=ALU.is_ge, fill=0.0, base=0, pattern=[[-P, TPB], [1, S]],
                           channel_multiplier=-1).then_inc(consts, 1)
        k.norm_ctx.gpsimd(pool, 0)

    def sync(sp):
        sp.wait_ge(k.x_tiles, NT * number)
        for later in ("l3x", "l3x_small", "l3f_small"):
            if later in k.dram:
                k.load_weights(sp, k.dram, later)

    return tensor, scalar, vector, gpsimd, sync


def null_key_attention(k, name, number, W):
    PAIRS, DH = 8, 64
    NK = S + 1
    ITEMS = 2 * B
    CHUNKS = ("q", "k", "q", "k", "v", "v")
    MADE_IN = ((0, 1), (2, 3), (4,), (5,))
    k.carve_from(REGION_B)
    q = [[k.carve(F32, T) for _ in range(2)] for _ in range(2)]
    kT = [k.carve(F32, B, NK) for _ in range(2)]
    V = [k.carve(F32, NT, P) for _ in range(2)]
    mark = k.carve_mark()
    PR = [k.carve(F32, TPB, NK) for _ in range(4)]
    PT = [k.carve(F32, TPB, S) for _ in range(4)]
    end = k.carve_mark()
    k.carve_back(mark)
    y = k.carve(F32, NT, D)
    yn = k.carve(F32, NT, D)
    k.carve(F32, 4 * TPB)
    ENT = k.carve(F32, T)
    k.carve_back(end)
    free_a = k.region["A"][:, L3F_WORDS:]
    in_a = free_a.shape[1] // T
    oT = [free_a[:, p * T:(p + 1) * T] for p in range(in_a)]
    oT += [k.carve(F32, T) for _ in range(PAIRS - in_a)]
    EN = k.carve(F32, NT, 2 * PAIRS)
    NVW = k.carve(F32, D)
    NM, den, rec = (k.carve(F32, 4, TPB) for _ in range(3))
    use = k.norm_use[number]
    HEADS = 2 * PAIRS

    def sem(what):
        return k.sem(f"{name}_{what}")

    null_ready = sem("null_ready")
    nvw_psum = sem("nvw_psum")
    nvw_sb = sem("nvw_sb")
    proj_psum = sem("proj_psum")
    proj_sb = sem("proj_sb")
    score_psum = sem("score_psum")
    max_ready = sem("max_ready")
    exp_ready = sem("exp_ready")
    rec_ready = sem("rec_ready")
    prob_ready = sem("prob_ready")
    pt_psum = sem("pt_psum")
    pt_sb = sem("pt_sb")
    av_psum = sem("av_psum")
    av_sb = sem("av_sb")
    ent_psum = sem("ent_psum")
    ent_sb = sem("ent_sb")
    out_psum = sem("out_psum")
    y_ready = sem("y_ready")

    def tensor(pe):
        bank = k.bank
        k.norm.tensor(pe, use, k.xn)
        pe.wait_ge(k.weights[name], 32)
        for p in range(PAIRS):
            ins = pe.matmul(bank[0][0:HEADS, 0:D], W("nv")[:, p, :], W("o")[:, p, :], start=p == 0, stop=p == PAIRS - 1)
        ins.then_inc(nvw_psum, 1)
        pe.wait_ge(k.norm.T_ready, 2 * use + 2)
        pe.wait_ge(nvw_sb, 1)

        def project(p, c):
            n, h, what = len(CHUNKS) * p + c, c // 2 % 2 if c < 4 else c - 4, CHUNKS[c]
            cols, dst = slice(p * P, (p + 1) * P), bank[6 + n % 2]
            if n >= 2:
                pe.wait_ge(proj_sb, n - 1)
            if what == "q":
                ins = pe.matmul(dst, W("q")[:, cols], k.xnT[:, h * HALF:(h + 1) * HALF], start=True, stop=True)
            elif what == "k":
                for c in range(2):
                    ins = pe.matmul(dst, W("k")[:, c, cols], k.ctxT[:, c, h * HALF:(h + 1) * HALF],
                                    start=c == 0, stop=c == 1)
            else:
                for t in range(4):
                    for c in range(2):
                        ins = pe.matmul(dst[:, t * P:(t + 1) * P], k.ctxT[:, c, (4 * h + t) * P:(4 * h + t + 1) * P],
                                        W("v")[:, c, cols], start=c == 0, stop=c == 1)
            ins.then_inc(proj_psum, 1)

        def scores(g):
            p, b, j = g // ITEMS, g % ITEMS // 2, g % 2
            if j == 0 and b % 2 == 0:
                pe.wait_ge(proj_sb, len(CHUNKS) * p + b + 2)
            if g >= 2:
                pe.wait_ge(exp_ready, g - 1)
            for t in range(TPB):
                tt = b * TPB + t
                ins = pe.matmul(bank[2 * (g % 2) + t][:, 0:NK], q[p % 2][j][:, tt * P:(tt + 1) * P],
                                kT[p % 2][:, b, :], start=True, stop=True)
            ins.then_inc(score_psum, 1)

        def turn(g):
            pe.wait_ge(prob_ready, g + 1)
            if g >= 2:
                if g % 2 == 0:
                    pe.wait_ge(av_sb, g // 2)
                else:
                    pe.wait_ge(pt_sb, g - 1)
            for kt in range(TPB):
                for t in range(TPB):
                    ins = pe.transpose(bank[4 + g % 2][:, kt * S + t * P:kt * S + (t + 1) * P],
                                       PR[g % 4][:, t, kt * P:(kt + 1) * P], k.ident[:, :])
            ins.then_inc(pt_psum, 1)

        for c in range(len(CHUNKS)):
            project(0, c)
        pe.wait_ge(null_ready, 1)
        scores(0)
        scores(1)
        for p in range(PAIRS):
            for b in range(B):
                g = ITEMS * p + 2 * b
                for i in range(2):
                    if g + i + 2 < ITEMS * PAIRS:
                        scores(g + i + 2)
                    turn(g + i)
                if p + 1 < PAIRS:
                    for c in MADE_IN[b]:
                        project(p + 1, c)
                pe.wait_ge(pt_sb, g + 2)
                if b % 2 == 0:
                    pe.wait_ge(proj_sb, len(CHUNKS) * p + 5 + b // 2)
                for kt in range(TPB):
                    for j in range(2):
                        ins = pe.matmul(bank[4][j * DH:(j + 1) * DH, 0:S], V[p % 2][:, b * TPB + kt, j * DH:(j + 1) * DH],
                                        PT[(g + j) % 4][:, kt, :], start=kt == 0, stop=kt == TPB - 1,
                                        tile_position=(0, j * DH))
                ins.then_inc(av_psum, 1)
        for t in range(NT):
            ins = pe.transpose(bank[t // 4][0:HEADS, (t % 4) * P:(t % 4 + 1) * P], EN[:, t, :], k.ident[:, :])
        ins.then_inc(ent_psum, 1)
        pe.wait_ge(av_sb, B * PAIRS)
        for t in range(NT):
            dst = bank[6 + t // 4][:, (t % 4) * P:(t % 4 + 1) * P]
            for p in range(PAIRS):
                pe.matmul(dst, oT[p][:, t * P:(t + 1) * P], W("o")[:, p, :], start=p == 0, stop=False)
            if t == 0:
                pe.wait_ge(ent_sb, 1)
            ins = pe.matmul(dst, ENT[0:HEADS, t * P:(t + 1) * P], NVW[0:HEADS, :], start=False, stop=True)
            if t % 4 == 3:
                ins.then_inc(out_psum, 1)

    def scalar(act):
        bank = k.bank
        k.norm.scalar(act, use, k.xnT)
        act.wait_ge(k.weights[name], 32)

        def exponentials(g):
            act.wait_ge(max_ready, g + 1)
            if g >= 4:
                act.wait_ge(pt_psum, g - 3)
            for t in range(TPB):
                ins = act.activation(PR[g % 4][:, t, :], bank[2 * (g % 2) + t][:, 0:NK], ACT.Exp,
                                     bias=NM[:, g % 4, t:t + 1], accum_out=den[:, g % 4, t:t + 1])
            ins.then_inc(exp_ready, 1)

        def projections(p, c):
            n, h, what = len(CHUNKS) * p + c, c // 2 % 2 if c < 4 else c - 4, CHUNKS[c]
            src = bank[6 + n % 2]
            act.wait_ge(proj_psum, n + 1)
            if what == "q":
                for j in range(2):
                    ins = act.activation(q[p % 2][j][:, h * HALF:(h + 1) * HALF], src, ACT.Copy, scale=W("half")[:, j:j + 1])
            elif what == "k":
                ins = act.activation(kT[p % 2][:, 2 * h:2 * h + 2, 0:S], src.rearrange("p (b n) -> p b n", b=2), ACT.Copy)
            else:
                ins = act.activation(V[p % 2][:, 4 * h:4 * h + 4, :], src.rearrange("p (t n) -> p t n", t=4), ACT.Copy)
            ins.then_inc(proj_sb, 1)

        for c in range(len(CHUNKS)):
            projections(0, c)
        exponentials(0)
        exponentials(1)
        for p in range(PAIRS):
            for b in range(B):
                g = ITEMS * p + 2 * b
                if g + 2 < ITEMS * PAIRS:
                    exponentials(g + 2)
                    exponentials(g + 3)
                if p + 1 < PAIRS:
                    for c in MADE_IN[b]:
                        projections(p + 1, c)
                act.wait_ge(av_psum, B * p + b + 1)
                act.activation(oT[p][:, b * S:(b + 1) * S], bank[4][:, 0:S], ACT.Copy).then_inc(av_sb, 1)
        act.wait_ge(ent_psum, 1)
        act.activation(ENT[0:HEADS, :].rearrange("p (a n) -> p a n", a=2), k.pair(0)[0:HEADS, :, :], ACT.Copy)\
            .then_inc(ent_sb, 1)

    def vector(dve, chain):
        bank = k.bank
        k.norm.vector(dve, chain, use, k.x, k.xn, 1e-5)
        dve.wait_ge(nvw_psum, 1)
        dve.tensor_copy(NVW[0:HEADS, :], bank[0][0:HEADS, 0:D]).then_inc(nvw_sb, 1)

        def maxima(g):
            dve.wait_ge(score_psum, g + 1)
            dve.tensor_reduce(NM[:, g % 4, :], k.pair(2 * (g % 2))[:, :, 0:NK], AX.X, ALU.max, negate=True)\
                .then_inc(max_ready, 1)

        def reciprocals(g):
            dve.wait_ge(exp_ready, g + 1)
            if g >= 4:
                dve.wait_ge(prob_ready, g - 3)
            dve.reciprocal(rec[:, g % 4, :], den[:, g % 4, :]).then_inc(rec_ready, 1)

        def copy_turned(g):
            dve.wait_ge(pt_psum, g + 1)
            if g >= 4:
                dve.wait_ge(av_psum, g // 2 - 1)
            dve.tensor_copy(PT[g % 4].rearrange("p a n -> p (a n)"), bank[4 + g % 2]).then_inc(pt_sb, 1)

        maxima(0)
        maxima(1)
        reciprocals(0)
        reciprocals(1)
        for g in range(0, ITEMS * PAIRS, 2):
            more = g + 2 < ITEMS * PAIRS
            if more:
                maxima(g + 2)
            copy_turned(g)
            if more:
                maxima(g + 3)
                reciprocals(g + 2)
            copy_turned(g + 1)
            if more:
                reciprocals(g + 3)
        for h in range(2):
            dve.wait_ge(out_psum, h + 1)
            chain.then(dve.tensor_copy(y[:, 4 * h:4 * h + 4, :].rearrange("p t d -> p (t d)"), bank[6 + h]))
        k.norm_plain.vector(dve, chain, 1, y, yn, 1e-6)
        dve.wait_ge(k.norm_plain.ready, 2 * NT)
        wide = [P, NT, P]
        chain.then(dve.tensor_tensor(yn, yn, W("ln_scale").unsqueeze(1).broadcast_to(wide), ALU.mult))
        chain.then(dve.tensor_tensor(yn, yn, W("ln_bias").unsqueeze(1).broadcast_to(wide), ALU.add))
        dve.tensor_tensor(k.x[:, :, :], k.x[:, :, :], yn, ALU.add).then_inc(k.x_tiles, NT)
        dve.wait_ge(k.x_tiles, NT * (number + 1))

    def gpsimd(pool):
        k.norm.gpsimd(pool, use)
        pool.wait_ge(k.weights[name], 32)
        for i in range(2):
            ins = pool.tensor_copy(kT[i][:, :, S:NK], W("nk").unsqueeze(1).broadcast_to([P, B, 1]))
        ins.then_inc(null_ready, 1)
        for g in range(PAIRS * ITEMS):
            p, b, j = g // ITEMS, g % ITEMS // 2, g % 2
            pool.wait_ge(rec_ready, g + 1)
            pool.wait_ge(exp_ready, g + 1)
            r = rec[:, g % 4, :].unsqueeze(2)
            pool.tensor_tensor(EN[:, b * TPB:(b + 1) * TPB, 2 * p + j:2 * p + j + 1], PR[g % 4][:, :, S:NK], r, ALU.mult)
            pool.tensor_tensor(PR[g % 4][:, :, 0:S], PR[g % 4][:, :, 0:S], r.broadcast_to([P, TPB, S]), ALU.mult)\
                .then_inc(prob_ready, 1)
        k.norm_plain.gpsimd(pool, 1)

    def sync(sp):
        sp.wait_ge(k.x_tiles, NT * number)
        if "l3f" in k.dram:
            k.load_weights(sp, k.dram, "l3f")

    return tensor, scalar, vector, gpsimd, sync


def sparse_experts(k, name, number, W):
    E = 32
    ROOM = -(-T * 5 // (4 * E))
    SLOTS = E * ROOM
    ST = SLOTS // P
    GROUP = HALF // ROOM
    groups = [(e, min(E, e + GROUP)) for e in range(0, E, GROUP)]
    NG = len(groups)
    shape = [P, NT, E]
    assert SLOTS % P == 0 and NG == 3
    k.carve_from(REGION_B)
    mark = k.carve_mark()
    to_slot = k.carve(F32, NT, SLOTS)
    k.carve_back(mark)
    from_slot = k.carve(F32, NT, ST, P)
    bufT, silu, hid, yT = (k.carve(F32, SLOTS) for _ in range(4))
    mark = k.carve_mark()
    slot_row = k.carve(F32, SLOTS)
    k.carve_back(mark)
    y = k.carve(F32, ST, P)
    logits, tagged, chosen, exps = (k.carve(F32, NT, E) for _ in range(4))
    upto = k.carve(F32, P)
    ones = k.carve(F32, P)
    slot_id = k.carve(F32, ST)
    maxima, top, place, slot, total, gate, fits = (k.carve(F32, NT) for _ in range(7))
    use = k.norm_use[number]

    def sem(what):
        return k.sem(f"{name}_{what}")

    consts = sem("consts")
    logits_psum = sem("logits_psum")
    shifted = sem("shifted")
    exps_ready = sem("exps_ready")
    chosen_ready = sem("chosen_ready")
    place_psum = sem("place_psum")
    slot_ready = sem("slot_ready")
    to_slot_ready = sem("to_slot_ready")
    slot_psum = sem("slot_psum")
    from_slot_ready = sem("from_slot_ready")
    buf_psum = sem("buf_psum")
    buf_sb = sem("buf_sb")
    gate_psum = sem("gate_psum")
    up_psum = sem("up_psum")
    silu_ready = sem("silu_ready")
    hid_ready = sem("hid_ready")
    yT_psum = sem("yT_psum")
    yT_sb = sem("yT_sb")
    y_psum = sem("y_psum")
    y_sb = sem("y_sb")
    out_psum = sem("out_psum")

    def of(g):
        return slice(groups[g][0] * ROOM, groups[g][1] * ROOM)

    def width(g):
        return (groups[g][1] - groups[g][0]) * ROOM

    def out_bank(t):
        return k.bank[3 + t % 5][:, 0:P]

    def tensor(pe):
        bank = k.bank
        k.norm.tensor(pe, use, k.xn)
        pe.wait_ge(k.weights[name], 32)
        pe.wait_ge(consts, 1)
        pe.wait_ge(k.norm.T_ready, 2 * use + 2)
        for t in range(NT):
            ins = pe.matmul(bank[0][:, t * E:(t + 1) * E], k.xnT[:, t * P:(t + 1) * P], W("router"), start=True, stop=True)
        ins.then_inc(logits_psum, 1)
        pe.wait_ge(chosen_ready, 1)
        pe.matmul(bank[1][:, 0:NT * E], upto, chosen.rearrange("p t e -> p (t e)"), start=True, stop=True)
        for t in range(NT - 1):
            ins = pe.matmul(bank[1][:, (t + 1) * E:NT * E], ones,
                            chosen[:, t:t + 1, :].broadcast_to([P, NT - 1 - t, E]), start=False, stop=True,
                            skip_group_check=True)
        ins.then_inc(place_psum, 1)
        pe.wait_ge(slot_ready, 1)
        for t in range(NT):
            ins = pe.matmul(bank[6 + t // 4][:, (t % 4) * P:(t % 4 + 1) * P], slot[:, t:t + 1].broadcast_to([P, P]),
                            k.ident[:, :], start=True, stop=True)
        ins.then_inc(slot_psum, 1)
        for t in range(NT):
            pe.wait_ge(to_slot_ready, t + 1)
            for g in range(NG):
                ins = pe.matmul(bank[g][:, 0:width(g)], k.xn[:, t, :], to_slot[:, t, of(g)], start=t == 0, stop=t == NT - 1)
                if t == NT - 1:
                    ins.then_inc(buf_psum, 1)
        for g, (first, end) in enumerate(groups):
            pe.wait_ge(buf_sb, g + 1)
            for what, dst, done in (("gate", bank[3 + g], gate_psum), ("up", bank[g], up_psum)):
                for e in range(first, end):
                    ins = pe.matmul(dst[:, (e - first) * ROOM:(e - first + 1) * ROOM], W(what)[:, e, :],
                                    bufT[:, e * ROOM:(e + 1) * ROOM], start=True, stop=True)
                ins.then_inc(done, 1)
        for g, (first, end) in enumerate(groups):
            pe.wait_ge(hid_ready, g + 1)
            for e in range(first, end):
                ins = pe.matmul(bank[3 + g][:, (e - first) * ROOM:(e - first + 1) * ROOM], W("down")[:, e, :],
                                hid[:, e * ROOM:(e + 1) * ROOM], start=True, stop=True)
            ins.then_inc(yT_psum, 1)
        pe.wait_ge(yT_sb, NG)
        for s in range(ST):
            ins = pe.transpose(bank[s // 4][:, (s % 4) * P:(s % 4 + 1) * P], yT[:, s * P:(s + 1) * P], k.ident[:, :])
            if s % 4 == 3 or s == ST - 1:
                ins.then_inc(y_psum, 1)
        for t in range(NT):
            pe.wait_ge(from_slot_ready, t + 1)
            if t == 3:
                pe.wait_ge(from_slot_ready, NT)
            if t >= 5:
                pe.wait_ge(k.x_tiles, NT * number + t - 4)
            for s in range(ST):
                if t == 0 and (s % 4 == 0):
                    pe.wait_ge(y_sb, s // 4 + 1)
                ins = pe.matmul(out_bank(t), from_slot[:, t, s, :], y[:, s, :], start=s == 0, stop=s == ST - 1)
            ins.then_inc(out_psum, 1)

    def scalar(act):
        bank = k.bank
        k.norm.scalar(act, use, k.xnT)
        act.wait_ge(shifted, 1)
        act.activation(exps, logits, ACT.Exp).then_inc(exps_ready, 1)
        for g in range(NG):
            act.wait_ge(buf_psum, g + 1)
            act.activation(bufT[:, of(g)], bank[g][:, 0:width(g)], ACT.Copy).then_inc(buf_sb, 1)
        for g in range(NG):
            act.wait_ge(gate_psum, g + 1)
            act.activation(silu[:, of(g)], bank[3 + g][:, 0:width(g)], ACT.Silu).then_inc(silu_ready, 1)
        for g in range(NG):
            act.wait_ge(yT_psum, g + 1)
            act.activation(yT[:, of(g)], bank[3 + g][:, 0:width(g)], ACT.Copy).then_inc(yT_sb, 1)
        for g in range(NG):
            act.wait_ge(y_psum, g + 1)
            n = min(4, ST - 4 * g)
            act.activation(y[:, 4 * g:4 * g + n, :].rearrange("p s d -> p (s d)"), bank[g][:, 0:n * P], ACT.Copy)\
                .then_inc(y_sb, 1)

    def vector(dve, chain):
        bank = k.bank
        k.norm.vector(dve, chain, use, k.x, k.xn, 1e-5)
        dve.wait_ge(k.weights[name], 32)
        dve.wait_ge(logits_psum, 1)
        chain.then(dve.tensor_copy(exps, bank[0][:, 0:NT * E].rearrange("p (t e) -> p t e", t=NT)))
        first_of_maxima(dve, chain, exps, W("falling").unsqueeze(1).broadcast_to(shape), maxima, tagged, top, chosen, shape)
        dve.tensor_tensor(logits, exps, maxima.unsqueeze(2).broadcast_to(shape), ALU.subtract).then_inc(shifted, 1)
        dve.tensor_tensor(k.x[:, :, :], k.x[:, :, :], k.xn[:, :, :], ALU.add).then_inc(chosen_ready, 1)
        dve.wait_ge(place_psum, 1)
        chain.then(dve.tensor_tensor(tagged, chosen, bank[1][:, 0:NT * E].rearrange("p (t e) -> p t e", t=NT), ALU.mult))
        chain.then(dve.tensor_reduce(place, tagged, AX.X, ALU.add))
        dve.tensor_scalar(fits, place, float(ROOM), None, ALU.is_le)
        chain.then(dve.tensor_scalar(top, top, -float(ROOM), float(ROOM * E), ALU.mult, ALU.add))
        chain.then(dve.tensor_tensor(slot, top, place, ALU.add))
        dve.tensor_tensor(slot, slot, fits, ALU.mult).then_inc(slot_ready, 1)
        dve.wait_ge(slot_ready, 1)
        dve.wait_ge(consts, 1)
        for t in range(NT):
            dve.tensor_scalar(to_slot[:, t, :], slot_row, slot[:, t:t + 1], None, ALU.is_equal).then_inc(to_slot_ready, 1)
        dve.wait_ge(exps_ready, 1)
        chain.then(dve.tensor_reduce(total, exps, AX.X, ALU.add))
        chain.then(dve.reciprocal(gate, total))
        dve.wait_ge(slot_psum, 1)
        dve.wait_ge(buf_psum, NG)

        def back(t):
            dve.tensor_tensor(from_slot[:, t, :, :], bank[6 + t // 4][:, (t % 4) * P:(t % 4 + 1) * P]
                              .unsqueeze(1).broadcast_to([P, ST, P]), slot_id.unsqueeze(2).broadcast_to([P, ST, P]),
                              ALU.is_equal).then_inc(from_slot_ready, 1)

        done = 0
        for g in range(NG):
            for t in range(done, min(NT, done + 3)):
                back(t)
            done = min(NT, done + 3)
            dve.wait_ge(up_psum, g + 1)
            dve.wait_ge(silu_ready, g + 1)
            dve.tensor_tensor(hid[:, of(g)], silu[:, of(g)], bank[g][:, 0:width(g)], ALU.mult).then_inc(hid_ready, 1)
        for t in range(NT):
            dve.wait_ge(out_psum, t + 1)
            dve.scalar_tensor_tensor(out=k.x[:, t, :], in0=out_bank(t), scalar=gate[:, t:t + 1], in1=k.x[:, t, :],
                                     op0=ALU.mult, op1=ALU.add).then_inc(k.x_tiles, 1)
        dve.wait_ge(k.x_tiles, NT * (number + 1))

    def gpsimd(pool):
        k.norm.gpsimd(pool, use)
        pool.memset(ones, 1.0)
        pool.memset(upto, 1.0).then_inc(k.pool_chain, 1)
        k.pool_count += 1
        pool.iota(slot_row, [[1, SLOTS]], base=1, channel_multiplier=0, allow_small_or_imprecise_dtypes=True)
        pool.iota(slot_id, [[P, ST]], base=1, channel_multiplier=1, allow_small_or_imprecise_dtypes=True)
        pool.wait_ge(k.pool_chain, k.pool_count)
        pool.affine_select(out=upto, in_=upto, compare_op=ALU.is_ge, fill=0.0, base=0, pattern=[[1, P]],
                           channel_multiplier=-1).then_inc(consts, 1)

    def sync(sp):
        pass

    return tensor, scalar, vector, gpsimd, sync


def build(nc, dram, out, last_stage=8):
    with ExitStack() as ctx:
        k = Kit(nc, ctx, dram)
        prelude = load_and_prepare(k, dram)
        stages = [prelude]
        W0 = k.weight_views("l0x", L0X)
        stages.append(packed_attention(k, "l0x", 0, 8, 16, 2, True, 1e-5, W0))
        if last_stage >= 2:
            stages.append(dense_experts(k, "l0f", 1, 4, k.weight_views("l0f", L0F), routing=True))
        if last_stage >= 3:
            stages.append(packed_attention(k, "l1x", 2, 16, 8, 4, False, 1e-5, k.weight_views("l1x", L1X)))
        if last_stage >= 4:
            stages.append(gated_attention(k, "l1f", 3, k.weight_views("l1f", L1F)))
        if last_stage >= 5:
            stages.append(patch_attention(k, "l2x", 4, k.weight_views("l2x", L2X)))
        if last_stage >= 6:
            stages.append(dense_experts(k, "l2f", 5, 8, k.weight_views("l2f", L2F, "l2f_small", L2F_SMALL), routing=False))
        if last_stage >= 7:
            stages.append(null_key_attention(k, "l3x", 6, k.weight_views("l3x", L3X, "l3x_small", L3X_SMALL)))
        if last_stage >= 8:
            stages.append(sparse_experts(k, "l3f", 7, k.weight_views("l3f", L3F, "l3f_small", L3F_SMALL)))

        block = ctx.enter_context(nc.Block())

        @block.tensor
        def _(pe):
            for stage in stages:
                stage[0](pe)

        @block.scalar
        def _(act):
            for stage in stages:
                stage[1](act)

        @block.vector
        def _(dve):
            chain = Chain(dve, k.sem("vector_chain"))
            for stage in stages:
                stage[2](dve, chain)

        @block.gpsimd
        def _(pool):
            for stage in stages:
                stage[3](pool)

        @block.sync
        def _(sp):
            for stage in stages:
                stage[4](sp)
            sp.wait_ge(k.x_tiles, NT * last_stage)
            sp.dma_start(out, k.x[:, :, :]).then_inc(k.out_stored, 16)
            sp.wait_ge(k.out_stored, 16)


class Kit:

    def __init__(self, nc, ctx, dram):
        self.nc, self.ctx, self.dram = nc, ctx, dram
        sb = lambda name, shape, dt=F32: ctx.enter_context(nc.sbuf_tensor(name, shape, dt))
        self.x = sb("x", [P, NT, D])
        self.xn = sb("xn", [P, NT, D])
        self.xnT = sb("xnT", [P, T])
        self.ctx_sb = sb("ctx", [P, NT, CTX])
        self.ctxT = sb("ctxT", [P, 2, T])
        self.ident = sb("ident", [P, P])
        self.minus_half = sb("minus_half", [P, NT])
        self.stats = sb("stats", [P, NT, 6])
        self.mean_var = sb("mean_var", [P, NT, 2])
        self.var_eps = sb("var_eps", [P, NT])
        self.rstd = sb("rstd", [P, NT])
        self.mask_col = sb("mask_col", [P, NT])
        self.region = {"A": sb("region_a", [P, 8192]), "C": sb("region_c", [P, 4352]), "D": sb("region_d", [P, 4508]), "E": sb("region_e", [P, 584])}
        self.work = sb("work", [P, WORK])
        self.region["B"] = self.work[:, 0:REGION_B]
        self.psum = ctx.enter_context(nc.psum_tensor("psum", [P, 8, HALF], F32))
        self.bank = [self.psum[:, i, :] for i in range(8)]
        self.at = 0
        self.counts = {}
        self.q_dram = {n: dram["scratch"](f"q_parts{n}") for n in (0, 2)}
        self.k_dram = {n: dram["scratch"](f"k_parts{n}") for n in (0, 2)}
        self.c_dram = dram["scratch"]("ctx_parts")
        self.weights = {n: self.sem(f"{n}_weights") for n in WEIGHTS if not n.endswith("_small")}
        self.x_tiles = self.sem("x_tiles")
        self.out_stored = self.sem("out_stored")
        self.inputs_loaded = self.sem("inputs_loaded")
        self.mask_loaded = self.sem("mask_loaded")
        self.consts_ready = self.sem("consts_ready")
        self.ctx_turned = self.sem("ctx_turned")
        self.ctxT_ready = self.sem("ctxT_ready")
        self.mask_ready = self.sem("mask_ready")
        self.pool_chain = self.sem("pool_chain")
        self.pool_count = 0
        self.norm = Norm(self, "norm")
        self.norm2 = Norm(self, "inner_norm")
        self.norm_use = {0: 0, 1: 1, 2: 2, 3: 3, 5: 4, 6: 5, 7: 6}
        self.norm_plain = Norm(self, "plain_norm")
        self.norm_ctx = Norm(self, "ctx_norm")
        self.lens = sb("lens", [P, NT], I32)
        self.lens_loaded = self.sem("lens_loaded")

    def sem(self, name):
        return self.ctx.enter_context(self.nc.semaphore(name))

    def count(self, name, total):
        if name not in self.counts:
            self.counts[name] = [self.sem(name), 0]
        semaphore, base = self.counts[name]
        self.counts[name][1] += total
        return Count(semaphore, base)

    def pair(self, i):
        return self.psum[:, i:i + 2, :]

    def carve(self, dtype, *shape):
        size = int(np.prod(shape))
        words = size if dtype != BF16 else size // 2
        flat = self.work[:, self.at:self.at + words]
        self.at += words
        assert self.at <= WORK, (self.at, WORK)
        if dtype != F32:
            flat = flat.bitcast(dtype)
        names = [f"a{i}" for i in range(len(shape))]
        if len(shape) == 1:
            return flat
        return flat.rearrange(f"p ({' '.join(names)}) -> p {' '.join(names)}", **dict(zip(names, shape)))

    def carve_mark(self):
        return self.at

    def carve_back(self, mark):
        self.at = mark

    def carve_from(self, start):
        self.at = start

    def loads_of(self, name):
        return 16 * (2 * len(TERMS) + 1 if name == "l0x" else 3 * len(TERMS))

    def weight_views(self, name, layout, *more):
        region, at = WEIGHTS[name]
        views = {}
        if more:
            rest = self.weight_views(*more)
            views = {what: rest(what) for what, *_ in more[1]}
        for what, *shape in layout:
            size = int(np.prod(shape))
            flat = self.region[region][:, at:at + size]
            if len(shape) > 1:
                names = [f"a{i}" for i in range(len(shape))]
                flat = flat.rearrange(f"p ({' '.join(names)}) -> p {' '.join(names)}", **dict(zip(names, shape)))
            views[what] = flat
            at += size
        return lambda what: views[what]

    def load_weights(self, engine, dram, name):
        region, at = WEIGHTS[name]
        src = dram[name]
        engine.dma_start(self.region[region][:, at:at + src.shape[1]], src)\
            .then_inc(self.weights[name.removesuffix("_small")], 16)


REGION_B = 8192
WORK = REGION_B + 18090
WEIGHTS = {"l0x": ("D", 0), "l0f": ("C", 0), "l1x": ("D", 1290), "l1f": ("D", 2320), "l1v": ("A", 0), "l1o": ("B", 0), "l2x": ("E", 0),
           "l2f": ("A", 0), "l2f_small": ("E", 386),
           "l3x": ("C", 0), "l3x_small": ("D", 0), "l3f": ("A", 0), "l3f_small": ("B", 0)}
L0X = (("k", 2, P), ("v", 2, P), ("q", P), ("ox", P), ("o", 2, P), ("pick", 4), ("bk", 1), ("bq", 1), ("bv", P), ("bo", P))
L0F = (("w1", 4, 512), ("w2", 4, 4, P), ("router", 4, 4), ("bg", 4, 4), ("b1", 16), ("b2", P), ("falling", 4))
L1F = (("q", 8, P), ("k", 8, P), ("sel", P), ("route_scale", 1), ("falling", 8))
L2X = (("w", P), ("g_init", P), ("b", P), ("g_res", 1))
L2F = (("w1", 8, 512), ("w2", 8, 4, P))
L3X = (("k", 2, 8 * P), ("v", 2, 8 * P))
L3X_SMALL = (("q", 8 * P), ("o", 8, P), ("nv", 8, 16), ("nk", 1), ("half", 2), ("ln_scale", P), ("ln_bias", P))
L3F = (("down", 32, P), ("router", 32), ("falling", 32))
L3F_WORDS = 32 * P + 32 + 32
L3F_SMALL = (("gate", 32, P), ("up", 32, P))
L2F_SMALL = (("router", 1, 8), ("b1", 32), ("b2", P), ("falling", 8), ("g", 8), ("b", 8))
L1X = (("k", P), ("v", P), ("q", P), ("o", 4, P), ("pick", 4), ("bo", P))


def load_and_prepare(k, dram):

    def tensor(pe):
        pe.wait_ge(k.consts_ready, 1)
        pe.wait_ge(k.inputs_loaded, 32)
        for c in range(2):
            for t in range(NT):
                ins = pe.transpose(k.bank[2 * c + t // 4][:, (t % 4) * P:(t % 4 + 1) * P],
                                   k.ctx_sb[:, t, c * P:(c + 1) * P], k.ident[:, :])
                if t % 4 == 3:
                    ins.then_inc(k.ctx_turned, 1)

    def scalar(act):
        for n, name in enumerate(("l0f",)):
            if name in dram:
                k.load_weights(act, dram, name)
        for i in range(4):
            act.wait_ge(k.ctx_turned, i + 1)
            act.activation(k.ctxT[:, i // 2, (i % 2) * HALF:(i % 2 + 1) * HALF], k.bank[i], ACT.Copy)\
                .then_inc(k.ctxT_ready, 1)

    def vector(dve, chain):
        dve.wait_ge(k.mask_loaded, 32)
        dve.tensor_scalar(k.mask_bias[0:1, :], k.mask_bc[0:1, :], 0.0, MASKED, ALU.is_equal, ALU.mult)\
            .then_inc(k.mask_ready, 1)
        dve.wait_ge(k.inputs_loaded, 32)

    def gpsimd(pool):
        pool.memset(k.minus_half[:, :], -0.5)
        pool.memset(k.ident[:, :], 0.0).then_inc(k.pool_chain, 1)
        k.pool_count += 1
        pool.wait_ge(k.pool_chain, k.pool_count)
        pool.affine_select(out=k.ident[:, :], in_=k.ident[:, :], compare_op=ALU.not_equal, fill=1.0,
                           base=0, pattern=[[-1, P]], channel_multiplier=1).then_inc(k.consts_ready, 1)

    def sync(sp):
        sp.dma_start(k.x[:, :, :], dram["x"]).then_inc(k.inputs_loaded, 16)
        sp.dma_start(k.ctx_sb[:, :, :], dram["ctx"]).then_inc(k.inputs_loaded, 16)
        k.load_weights(sp, dram, "l0x")
        sp.dma_start(k.mask_bc[:, :], dram["mask"].partition_broadcast(P)).then_inc(k.mask_loaded, 16)
        sp.dma_start(k.mask_col[:, :], dram["mask_col"]).then_inc(k.mask_loaded, 16)
        sp.dma_start(k.lens[:, :], dram["lens"]).then_inc(k.lens_loaded, 16)
        for name in ("l1x", "l1f", "l1v", "l2x", "l2f_small"):
            if name in dram:
                k.load_weights(sp, dram, name)

    k.mask_bc = k.ctx.enter_context(k.nc.sbuf_tensor("mask_bc", [P, T], F32))
    k.mask_bias = k.ctx.enter_context(k.nc.sbuf_tensor("mask_bias", [1, T], BF16))
    return tensor, scalar, vector, gpsimd, sync


def tiles(a):
    n = a.shape[0] // P
    return np.ascontiguousarray(a.reshape(n, P, -1).transpose(1, 0, 2)).reshape(P, -1)


def across(v):
    return np.broadcast_to(v.reshape(1, -1), (P, v.size))


def slots(w, heads):
    width = w.shape[0] // heads
    out = np.zeros((heads, SLOT, w.shape[1]), w.dtype)
    out[:, :width] = w.reshape(heads, width, -1)
    return out.reshape(heads * SLOT, -1)


def pick(width):
    out = np.zeros((P, P // SLOT), np.float32)
    for j in range(P // SLOT):
        out[SLOT * j + width, j] = 1.0
    return out


def columns(v):
    return v.reshape(-1, P).T


def rows(v):
    out = np.zeros((P, v.shape[1]), v.dtype)
    out[:v.shape[0]] = v
    return out


def expert_weights(w1, w2):
    E = w2.shape[0]
    return [w1.reshape(P, -1), w2.reshape(E, 4, P, D).transpose(2, 0, 1, 3).reshape(P, -1)]


def pack(i):
    f = {n: np.asarray(a) for n, a in i.items()}
    w = {}
    src, wo = f["L0_xattn_W_src"], f["L0_xattn_W_out"]
    w["l0x"] = [tiles(src[:D].T), tiles(src[D:].T), f["L0_xattn_W_tgt"].T, wo[:, :D].T, tiles(slots(wo[:, D:].T, 8)),
                pick(16), f["L0_xattn_b_src"][:D, None], f["L0_xattn_b_tgt"][:, None],
                across(f["L0_xattn_b_src"][D:]), across(f["L0_xattn_b_out"])]
    qkv = f["L1_xattn_w_qkv"]
    w["l1x"] = [qkv[D:2 * D].T, qkv[2 * D:].T, qkv[:D].T, tiles(slots(f["L1_xattn_w_proj"].T, 16)), pick(8),
                across(f["L1_xattn_b_proj"])]
    w["l0f"] = expert_weights(f["L0_ffn_W1"].transpose(1, 0, 2), f["L0_ffn_W2"])
    w["l0f"] += [f["L0_ffn_Wg"].transpose(1, 0, 2).reshape(P, -1), across(f["L0_ffn_bg"]),
                 columns(f["L0_ffn_b1"]), rows(f["L0_ffn_b2"]), across(np.arange(4, 0, -1, dtype=np.float32))]
    by_head = lambda a: a.reshape(8, P, D).transpose(2, 0, 1).reshape(P, -1)
    w["l1f"] = [by_head(f["L1_ffn_q_w"]), by_head(f["L1_ffn_k_w"]), f["L1_ffn_sel_v_w"].T, f["L1_ffn_sel_o_w"].T,
                across(f["L1_ffn_route_scale"]), across(np.arange(8, 0, -1, dtype=np.float32))]
    w["l1v"] = [f["L1_ffn_v_w"].transpose(1, 0, 2).reshape(P, -1)]
    w["l1o"] = [f["L1_ffn_o_w"].transpose(1, 0, 2).reshape(P, -1)]
    w["l2x"] = [f["L2_xattn_W_in"].T, across(f["L2_xattn_g_init"][:D]), across(f["L2_xattn_b_in"]),
                f["L2_xattn_g_res"][:, None]]
    w["l2f"] = expert_weights(f["L2_ffn_w1"].transpose(2, 0, 1), f["L2_ffn_w2"].transpose(0, 2, 1))
    w["l2f_small"] = [f["L2_ffn_centroids"].T, columns(f["L2_ffn_b1"]), rows(f["L2_ffn_b2"]),
                      across(np.arange(8, 0, -1, dtype=np.float32)), f["L2_ffn_ln_g"].T, f["L2_ffn_ln_b"].T]
    kv, null = f["L3_xattn_Wkv"], f["L3_xattn_null_kv"]
    w["l3x"] = [tiles(kv[:, :8 * P]), tiles(kv[:, 8 * P:])]
    nv = np.zeros((2, 64, 8, 16), np.float32)
    half = np.zeros((2, 64, 2), np.float32)
    for j in range(2):
        half[j, :, j] = 64.0 ** -0.5
        for p in range(8):
            nv[j, :, p, 2 * p + j] = null[1]
    w["l3x_small"] = [f["L3_xattn_Wq"], tiles(f["L3_xattn_Wout"]), nv.reshape(P, -1),
                      np.concatenate([null[0], null[0]])[:, None], half.reshape(P, 2),
                      across(f["L3_xattn_ln_scale"]), across(f["L3_xattn_ln_bias"])]
    by_expert = lambda a: a.transpose(1, 0, 2).reshape(P, -1)
    w["l3f"] = [by_expert(f["L3_ffn_w_down"]), f["L3_ffn_w_router"], across(np.arange(32, 0, -1, dtype=np.float32))]
    w["l3f_small"] = [by_expert(f["L3_ffn_w_gate"]), by_expert(f["L3_ffn_w_up"])]
    return f, w


def kernel(**inputs):
    import concourse.bacc as bacc
    from concourse.bass_utils import run_bass_kernel_spmd

    f, w = pack(inputs)
    arrays = {name: np.ascontiguousarray(np.concatenate(parts, axis=1)) for name, parts in w.items()}
    arrays["x"] = tiles(f["x"].reshape(T, D)).reshape(P, NT, D)
    arrays["ctx"] = tiles(f["ctx_2048"].reshape(T, CTX)).reshape(P, NT, CTX)
    arrays["mask"] = f["mask_BxS2_fk1"].reshape(T)
    arrays["mask_col"] = np.ascontiguousarray(f["mask_BxS2_fk1"].reshape(NT, P).T)
    arrays["lens"] = np.ascontiguousarray(f["mask_BxS2_if0"].astype(np.int32, copy=False).reshape(NT, P).T)
    nc = bacc.Bacc("TRN2", target_bir_lowering=False, num_devices=1)
    dram, fed = {}, {}
    for name, a in arrays.items():
        fed[f"in_{name}"] = a
        dram[name] = nc.dram_tensor(f"in_{name}", a.shape, mybir.dt.from_np(a.dtype), kind="ExternalInput").ap()
    dram["scratch"] = lambda name: nc.dram_tensor(name, (3, P, T), BF16, kind="Internal").ap()
    out = nc.dram_tensor("out_x", (P, NT, D), F32, kind="ExternalOutput").ap()
    build(nc, dram, out)
    result = run_bass_kernel_spmd(nc, [fed], core_ids=[0]).results[0]["out_x"]
    return result.reshape(P, NT, D).transpose(1, 0, 2).reshape(B, S, D)
```

```python
from contextlib import ExitStack

import numpy as np

import concourse.bass as bass
from concourse import mybir

F32 = mybir.dt.float32
BF16 = mybir.dt.bfloat16
I32 = mybir.dt.int32
ALU = mybir.AluOpType
ACT = mybir.ActivationFunctionType
AX = mybir.AxisListType

P = 128
B, S, D = 4, 256, 128
CTX = 256
T = B * S
NT = T // P
TPB = S // P
HALF = 512
MASKED = -1.0e30
SLOT = 32
TERMS = ((0, 0), (0, 1), (0, 2), (1, 0), (1, 1), (2, 0))


class Chain:

    def __init__(self, engine, semaphore):
        self.engine, self.semaphore, self.count = engine, semaphore, 0

    def then(self, instruction):
        self.count += 1
        instruction.then_inc(self.semaphore, 1)
        self.engine.wait_ge(self.semaphore, self.count)


class Count:

    def __init__(self, semaphore, base):
        self.semaphore, self.base = semaphore, base

    def at(self, n):
        return self.semaphore, self.base + n


class Norm:

    def __init__(self, k, name):
        self.k = k
        self.var_ready = k.sem(f"{name}_var_ready")
        self.rstd_ready = k.sem(f"{name}_rstd_ready")
        self.ready = k.sem(f"{name}_ready")
        self.turned = k.sem(f"{name}_turned")
        self.T_ready = k.sem(f"{name}_T_ready")

    def statistics(self, dve, chain, n, src, eps, rms, h):
        k = self.k
        tiles = range(h * NT // 2, (h + 1) * NT // 2)
        half = slice(tiles.start, tiles.stop)
        for t in tiles:
            ins = dve.bn_stats(k.stats[:, t, :], src[:, t, :])
        chain.then(ins)
        for t in tiles:
            ins = dve.bn_aggr(k.mean_var[:, t, :], k.stats[:, t, :])
        chain.then(ins)
        if rms:
            chain.then(dve.tensor_tensor(k.var_eps[:, half], k.mean_var[:, half, 0], k.mean_var[:, half, 0], ALU.mult))
            chain.then(dve.tensor_tensor(k.var_eps[:, half], k.var_eps[:, half], k.mean_var[:, half, 1], ALU.add))
            dve.tensor_scalar(k.var_eps[:, half], k.var_eps[:, half], eps, None, ALU.add).then_inc(self.var_ready, 1)
        else:
            dve.tensor_scalar(k.var_eps[:, half], k.mean_var[:, half, 1], eps, None, ALU.add).then_inc(self.var_ready, 1)

    def vector(self, dve, chain, n, src, dst, eps, rms=False):
        k = self.k
        for h in range(2):
            self.statistics(dve, chain, n, src, eps, rms, h)
        for t in range(NT):
            if t % (NT // 2) == 0:
                dve.wait_ge(self.rstd_ready, 2 * n + t // (NT // 2) + 1)
            if rms:
                ins = dve.tensor_scalar(dst[:, t, :], src[:, t, :], k.rstd[:, t:t + 1], None, ALU.mult)
            else:
                ins = dve.tensor_scalar(dst[:, t, :], src[:, t, :], k.mean_var[:, t, 0:1], k.rstd[:, t:t + 1],
                                        ALU.subtract, ALU.mult)
            ins.then_inc(self.ready, 1)

    def gpsimd(self, pool, n):
        k = self.k
        for h in range(2):
            half = slice(h * NT // 2, (h + 1) * NT // 2)
            pool.wait_ge(self.var_ready, 2 * n + h + 1)
            pool.tensor_tensor(k.rstd[:, half], k.var_eps[:, half], k.minus_half[:, half], ALU.pow)\
                .then_inc(self.rstd_ready, 1)

    def tensor(self, pe, n, src, banks=(6, 7)):
        k = self.k
        for t in range(NT):
            pe.wait_ge(self.ready, NT * n + t + 1)
            ins = pe.transpose(k.bank[banks[t // 4]][:, (t % 4) * P:(t % 4 + 1) * P], src[:, t, :], k.ident[:, :])
            if t % 4 == 3:
                ins.then_inc(self.turned, 1)

    def scalar(self, act, n, dst, banks=(6, 7), scale=1.0):
        k = self.k
        for h in range(2):
            act.wait_ge(self.turned, 2 * n + h + 1)
            act.activation(dst[:, h * HALF:(h + 1) * HALF], k.bank[banks[h]], ACT.Copy, scale=scale)\
                .then_inc(self.T_ready, 1)


def packed_attention(k, name, number, NH, HD, key_tiles, masked, eps, W):
    NHG = NH // 4
    R_MASK = 96
    R_MAX = R_MASK + (1 if masked else 0)
    ROWS = R_MAX + 3
    NK = key_tiles * P
    STEPS = NHG * key_tiles
    NG1 = TPB * NH * NK // HALF
    HPG = HALF // NK
    PER = NG1 // STEPS
    LAG = STEPS if masked else 2
    SHARES = 1 if masked else 2
    HPS = NH // SHARES
    scale = float(HD) ** -0.5
    assert PER * STEPS == NG1 and NH * HD == D and len(TERMS) * HD <= R_MASK

    k.carve_from(0)
    QS = [k.carve(BF16, NH, S) for _ in range(2)]
    KS = [k.carve(BF16, NH, NK) for _ in range(2)]
    VA = [k.carve(F32, key_tiles, NH, SLOT) for _ in range(2)]
    NM = k.carve(F32, B, NH, TPB)
    NMr = k.carve(F32, P)
    NMp = [k.carve(BF16, P) for _ in range(3)]
    vtmp = k.carve(F32, HALF)
    mark = k.carve_mark()
    q32, k32 = k.carve(F32, T), k.carve(F32, T)
    qp = [k.carve(BF16, T) for _ in range(3)]
    kp = [k.carve(BF16, T) for _ in range(3)]
    k.carve_back(mark)
    PT = [k.carve(F32, 4 * S) for _ in range(2)]
    OT = k.carve(F32, NHG, T)
    OTn = [k.carve(F32, NHG, P) for _ in range(2)]
    R = k.carve(F32, NT, NH)
    RX = [k.carve(F32, NH * SLOT) for _ in range(2)]
    if masked:
        k.carve_from(WORK - 5 * T // 2)
        c32 = k.carve(F32, T)
        cp = [k.carve(BF16, T) for _ in range(3)]

    q_dram, k_dram = k.q_dram[number], k.k_dram[number]
    use = k.norm_use[number]

    def count(what, total):
        return k.count(f"packed_{what}", total)

    fill_done = count("fill_done", 2)
    q_psum = count("q_psum", 2)
    k_psum = count("k_psum", 2)
    v_psum = count("v_psum", B)
    biased = count("biased", 4 if masked else 0)
    part = count("part", 8)
    rest = count("rest", 8)
    c_part = count("c_part", 2 if masked else 0)
    c_rest = count("c_rest", 2 if masked else 0)
    stored = count("stored", 16 * 12)
    c_stored = k.c_stored
    loaded = [[count(f"loaded{i}{j}", 2 * k.loads_of(name)) for j in range(SHARES)] for i in range(2)]
    v_sb = count("v_sb", B)
    p1_psum = count("p1_psum", B * NG1)
    p1_max = count("p1_max", B * NG1)
    nm_psum = count("nm_psum", B)
    nm_part = count("nm_part", 2 * B)
    nm_rest = count("nm_rest", 2 * B)
    nm_loaded = count("nm_loaded", 48 * B)
    p2_psum = count("p2_psum", B * STEPS)
    p2_exp = count("p2_exp", B * STEPS)
    av_done = count("av_done", B * STEPS)
    av_out = count("av_out", B * NHG)
    den_psum = count("den_psum", 1)
    den_ready = count("den_ready", 1)
    wide_ready = count("wide_ready", NT)
    bc_psum = count("bc_psum", NT)
    normed = count("normed", NT)
    out_psum = count("out_psum", NT)

    PIECES = [(what, h) for h in range(2) for what in ("k", "q")]

    def first_of(m):
        return 4 * (m // 2) + m % 2 + 1

    def last_of(m):
        return first_of(m) + 2

    def piece(m):
        what, h = PIECES[m]
        cols = slice(h * HALF, (h + 1) * HALF)
        return (k.bank[2 + h], k32, kp, cols) if what == "k" else (k.bank[h], q32, qp, cols)

    def tensor(pe):
        bank = k.bank
        k.norm.tensor(pe, use, k.xn)
        pe.wait_ge(k.weights[name], 16)
        if masked:
            pe.wait_ge(k.ctxT_ready, 4)
        for h in range(2):
            cols = slice(h * HALF, (h + 1) * HALF)
            if masked:
                for c in range(2):
                    ins = pe.matmul(bank[2 + h][:, :], W("k")[:, c, :], k.ctxT[:, c, cols], start=c == 0, stop=c == 1)
                ins.then_inc(k_psum.semaphore, 1)
        for h in range(2):
            cols = slice(h * HALF, (h + 1) * HALF)
            pe.wait_ge(k.norm.T_ready, 2 * use + h + 1)
            if not masked:
                pe.matmul(bank[2 + h][:, :], W("k"), k.xnT[:, cols], start=True, stop=True).then_inc(k_psum.semaphore, 1)
            pe.matmul(bank[h][:, :], W("q"), k.xnT[:, cols], start=True, stop=True).then_inc(q_psum.semaphore, 1)

        def values(b):
            if b >= 1:
                pe.wait_ge(*v_sb.at(b))
                pe.wait_ge(*nm_rest.at(2 * b))
            for t in range(TPB):
                tt = b * TPB + t
                if masked:
                    for c in range(2):
                        ins = pe.matmul(bank[7][:, t * P:(t + 1) * P], k.ctxT[:, c, tt * P:(tt + 1) * P],
                                        W("v")[:, c, :], start=c == 0, stop=c == 1)
                else:
                    ins = pe.matmul(bank[7][:, t * P:(t + 1) * P], k.xnT[:, tt * P:(tt + 1) * P], W("v"),
                                    start=True, stop=True)
            ins.then_inc(v_psum.semaphore, 1)

        def first_pass(b, n):
            g = b * NG1 + n
            if g >= 2:
                pe.wait_ge(*p1_max.at(g - 1))
            t, h0 = n % TPB, n // TPB * HPG
            for j in range(HPG):
                ins = pe.matmul(bank[g % 2][:, j * NK:(j + 1) * NK],
                                QS[b % 2][0:R_MAX, h0 + j, t * P:(t + 1) * P],
                                KS[b % 2][0:R_MAX, h0 + j, :], start=True, stop=True)
            ins.then_inc(p1_psum.semaphore, 1)

        def second_pass(b, s):
            g = b * STEPS + s
            hg, kt = s // key_tiles, s % key_tiles
            if g >= 2:
                pe.wait_ge(*p2_exp.at(g - 1))
            for j in range(4):
                ins = pe.matmul(bank[2 + 2 * (g % 2) + j // 2][:, (j % 2) * S:(j % 2 + 1) * S],
                                KS[b % 2][0:ROWS, 4 * hg + j, kt * P:(kt + 1) * P],
                                QS[b % 2][0:ROWS, 4 * hg + j, :], start=True, stop=True)
            ins.then_inc(p2_psum.semaphore, 1)

        def denominators(b, hg):
            pe.wait_ge(*av_out.at(b * NHG + hg + 1))
            for t in range(b * TPB, (b + 1) * TPB):
                first = S + (t * NHG + hg) * 4
                ins = pe.matmul(bank[6][:, first:first + 4], OT[:, hg, t * P:(t + 1) * P], W("pick"),
                                start=True, stop=True)
            if b == B - 1 and hg == NHG - 1:
                ins.then_inc(den_psum.semaphore, 1)

        def weighted_values(b, s):
            g = b * STEPS + s
            hg, kt = s // key_tiles, s % key_tiles
            pe.wait_ge(*p2_exp.at(g + 1))
            if s == 0:
                pe.wait_ge(*v_sb.at(b + 1))
            if kt == 0 and g >= 1:
                denominators(*divmod(b * NHG + hg - 1, NHG))
            for j in range(4):
                ins = pe.matmul(bank[6][SLOT * j:SLOT * (j + 1), 0:S], VA[b % 2][:, kt, 4 * hg + j, :],
                                PT[g % 2][:, j * S:(j + 1) * S], start=kt == 0, stop=kt == key_tiles - 1,
                                tile_position=(0, SLOT * j))
            ins.then_inc(av_done.semaphore, 1)

        for b in range(B + 1):
            for u in range(STEPS + LAG):
                if u < STEPS and b < B:
                    if b == 0 and u == 0:
                        pe.wait_ge(*rest.at(first_of(3)))
                        pe.wait_ge(*part.at(first_of(3)))
                    if u % (STEPS // SHARES) == 0:
                        pe.wait_ge(*loaded[b % 2][u // (STEPS // SHARES)].at(k.loads_of(name) * (b // 2 + 1)))
                    for i in range(PER):
                        first_pass(b, PER * u + i)
                if u == LAG - 1 and b < B:
                    values(b)
                if u >= LAG and b > 0:
                    s = u - LAG
                    if s == 0:
                        pe.wait_ge(*nm_loaded.at(48 * b))
                    second_pass(b - 1, s)
                    if s > 0:
                        weighted_values(b - 1, s - 1)
                if u == STEPS and b < B:
                    pe.wait_ge(*p1_max.at(NG1 * (b + 1)))
                    pe.wait_ge(*v_sb.at(b + 1))
                    pe.transpose(bank[7][0:TPB * NH, 0:P], NM[:, b, :, :].rearrange("p h t -> p (h t)"),
                                 k.ident[:, :]).then_inc(nm_psum.semaphore, 1)
            if b > 0:
                weighted_values(b - 1, STEPS - 1)
        denominators(B - 1, NHG - 1)

        def spread(t):
            pe.wait_ge(*wide_ready.at(t + 1))
            if t >= 3:
                pe.wait_ge(*normed.at(t - 2))
            for hg in range(NHG):
                ins = pe.matmul(bank[1 + t % 3][:, hg * P:(hg + 1) * P], RX[t % 2][:, hg * P:(hg + 1) * P],
                                k.ident[:, :], start=True, stop=True)
            ins.then_inc(bc_psum.semaphore, 1)

        def project(t):
            pe.wait_ge(*normed.at(t + 1))
            if t >= 4:
                pe.wait_ge(k.x_tiles, NT * number + t - 3)
            dst = bank[4 + t % 4][:, 0:P]
            if masked:
                pe.matmul(dst, k.xnT[:, t * P:(t + 1) * P], W("ox"), start=True, stop=False)
            for hg in range(NHG):
                ins = pe.matmul(dst, OTn[t % 2][:, hg, :], W("o")[:, hg, :], start=hg == 0 and not masked,
                                stop=hg == NHG - 1)
            ins.then_inc(out_psum.semaphore, 1)

        for t in range(NT + 1):
            if t < NT:
                spread(t)
            if t > 0:
                project(t - 1)

    def scalar(act):
        k.norm.scalar(act, use, k.xnT)
        for pair in range(2):
            for m in (2 * pair, 2 * pair + 1):
                src, f32, parts, cols = piece(m)
                if masked:
                    act.wait_ge(*biased.at(m + 1))
                    src = f32[:, cols]
                else:
                    act.wait_ge(*(k_psum, q_psum)[m % 2].at(PIECES[m][1] + 1))
                act.activation(parts[0][:, cols], src, ACT.Copy).then_inc(part.semaphore, 1)
            for m in (2 * pair, 2 * pair + 1):
                src, f32, parts, cols = piece(m)
                act.wait_ge(*rest.at(first_of(m)))
                act.activation(parts[1][:, cols], f32[:, cols], ACT.Copy).then_inc(part.semaphore, 1)
        if masked:
            act.activation(cp[0], k.ctxT[:, 0, :], ACT.Copy).then_inc(c_part.semaphore, 1)
            act.wait_ge(*c_rest.at(1))
            act.activation(cp[1], c32, ACT.Copy).then_inc(c_part.semaphore, 1)
        act.wait_ge(*fill_done.at(2))

        rows = slice(0, TPB * NH)
        for b in range(B + 1):
            for u in range(STEPS + LAG):
                if u >= LAG and b > 0:
                    g = (b - 1) * STEPS + u - LAG
                    act.wait_ge(*p2_psum.at(g + 1))
                    if g >= 2:
                        act.wait_ge(*av_done.at(g - 1))
                    act.activation(PT[g % 2].rearrange("p (a n) -> p a n", a=2), k.pair(2 + 2 * (g % 2)),
                                   ACT.Exp, scale=scale).then_inc(p2_exp.semaphore, 1)
                if u == STEPS and b < B:
                    act.wait_ge(*nm_psum.at(b + 1))
                    if b >= 1:
                        act.wait_ge(*nm_loaded.at(48 * b))
                    act.activation(NMp[0][rows, :], k.bank[7][rows, 0:P], ACT.Copy).then_inc(nm_part.semaphore, 1)
                if u == STEPS + 1 and b < B:
                    act.wait_ge(*nm_rest.at(2 * b + 1))
                    act.activation(NMp[1][rows, :], NMr[rows, :], ACT.Copy).then_inc(nm_part.semaphore, 1)
        act.wait_ge(*den_ready.at(1))
        for t in range(NT):
            if t >= 2:
                act.wait_ge(*bc_psum.at(t - 1))
            act.activation(RX[t % 2].rearrange("p (h s) -> p h s", h=NH),
                           R[:, t, :].unsqueeze(2).broadcast_to([P, NH, SLOT]), ACT.Copy).then_inc(wide_ready.semaphore, 1)

    def gpsimd(pool):
        if not masked:
            pool.wait_ge(k.x_tiles, NT * (number - 1))
        def chained(ins):
            k.pool_count += 1
            ins.then_inc(k.pool_chain, 1)
            pool.wait_ge(k.pool_chain, k.pool_count)

        for i in range(2):
            chained(pool.memset(QS[i][:, :, :], 0.0))
            if masked:
                chained(pool.memset(QS[i][R_MASK:R_MASK + 1, :, :], 1.0))
        pool.memset(KS[0][:, :, :], 1.0).then_inc(fill_done.semaphore, 1)
        k.norm.gpsimd(pool, use)
        if masked:
            k.prepare_mask(pool)
        pool.memset(KS[1][:, :, :], 1.0)
        for i in range(2):
            pool.memset(VA[i][:, :, :, :], 0.0).then_inc(k.pool_chain, 1)
            k.pool_count += 1
        pool.wait_ge(k.pool_chain, k.pool_count)
        pool.memset(VA[0][:, :, :, HD], 1.0)
        pool.memset(VA[1][:, :, :, HD], 1.0).then_inc(fill_done.semaphore, 1)

    def sync(sp):
        def by_part(dram, i):
            return dram.rearrange("(h i d) t -> i h d t", h=NH, i=3)[i]

        def rows_of(dram, first, n, b):
            return dram.rearrange("(h r) t -> r h t", h=NH)[first * HD:(first + n) * HD, :, b * S:(b + 1) * S]

        def store_half(h):
            dram = {"k": k_dram, "q": q_dram}
            for i in range(3):
                for m in (2 * h, 2 * h + 1):
                    if i < 2:
                        sp.wait_ge(*part.at((first_of, last_of)[i](m)))
                    else:
                        sp.wait_ge(*rest.at(last_of(m)))
                    parts, cols = piece(m)[2:]
                    sp.dma_start(by_part(dram[PIECES[m][0]], i)[:, :, cols], parts[i][:, cols])\
                        .then_inc(stored.semaphore, 16)

        def load_keys(dram, b, first, share):
            at, heads = 0, slice(share * HPS, (share + 1) * HPS)
            for n in (3, 2, 1):
                sp.dma_start(KS[b % 2][at * HD:(at + n) * HD, heads, first:first + S], rows_of(dram, 0, n, b)[:, heads, :])\
                    .then_inc(loaded[b % 2][share].semaphore, 16)
                at += n

        def load_context(b, share):
            sp.wait_ge(c_stored, 16 * 3)
            load_keys(k.c_dram, b, 0, share)

        def load(b, share):
            heads = slice(share * HPS, (share + 1) * HPS)
            done = loaded[b % 2][share].semaphore
            if b == 0:
                sp.wait_ge(*stored.at(16 * 6))
                sp.wait_ge(*fill_done.at(1))
            if b == 1:
                sp.wait_ge(*fill_done.at(2))
            if b == 2:
                sp.wait_ge(*stored.at(16 * 12))
            if b >= 2:
                sp.wait_ge(*p2_psum.at(STEPS * (b - 2) + STEPS // SHARES * (share + 1)))
            load_keys(k_dram, b, NK - S, share)
            for r, (i, _) in enumerate(TERMS):
                sp.dma_start(QS[b % 2][r * HD:(r + 1) * HD, heads, :], rows_of(q_dram, i, 1, b)[:, heads, :])\
                    .then_inc(done, 16)
            if masked:
                sp.dma_start(KS[b % 2][R_MASK:R_MASK + 1, :, :],
                             k.mask_bias[0:1, b * S:(b + 1) * S].unsqueeze(1).broadcast_to([1, NH, S])).then_inc(done, 16)
            elif b > 0:
                load_context(b, share)

        if not masked:
            sp.wait_ge(*fill_done.at(1))
            for share in range(SHARES):
                load_context(0, share)
        store_half(0)
        load(0, 0)
        store_half(1)
        for share in range(1, SHARES):
            load(0, share)
        for share in range(SHARES):
            load(1, share)
        if masked:
            for i, ready in enumerate((c_part.at(1), c_part.at(2), c_rest.at(2))):
                sp.wait_ge(*ready)
                sp.dma_start(k.c_dram.rearrange("(h i d) t -> i h d t", h=16, i=3)[i], cp[i]).then_inc(c_stored, 16)
        for b in range(B):
            more = 1 <= b < B - 1
            if more:
                for share in range(SHARES - 1):
                    load(b + 1, share)
            for i in range(3):
                if i < 2:
                    sp.wait_ge(*nm_part.at(2 * b + i + 1))
                else:
                    sp.wait_ge(*nm_rest.at(2 * b + 2))
                sp.dma_start(QS[b % 2][R_MAX + i:R_MAX + i + 1, :, :].rearrange("p h (t n) -> p (h t) n", t=TPB),
                             NMp[i][0:TPB * NH, :]).then_inc(nm_loaded.semaphore, 16)
            if more:
                load(b + 1, SHARES - 1)
            if masked and b == B - 2:
                k.load_later(sp, ("l0f",))
        if masked:
            k.load_later(sp, ("l1x", "l1f", "l1v", "l2x", "l2f_small"))

    def vector(dve, chain):
        k.norm.vector(dve, chain, use, k.x, k.xn, eps)
        bank = k.bank
        dve.wait_ge(k.weights[name], 16)
        if masked:
            dve.wait_ge(k.mask_ready, 1)
            for m in range(4):
                src, f32, parts, cols = piece(m)
                dve.wait_ge(*(k_psum, q_psum)[m % 2].at(PIECES[m][1] + 1))
                dve.scalar_tensor_tensor(out=f32[:, cols], in0=src, scalar=W(("bk", "bq")[m % 2]),
                                         in1=k.mask_bc[:, cols], op0=ALU.add, op1=ALU.mult).then_inc(biased.semaphore, 1)
        for pair in range(2):
            for m in (2 * pair, 2 * pair + 1):
                src, f32, parts, cols = piece(m)
                dve.wait_ge(*part.at(first_of(m)))
                dve.tensor_tensor(f32[:, cols], f32[:, cols] if masked else src, parts[0][:, cols], ALU.subtract)\
                    .then_inc(rest.semaphore, 1)
            for m in (2 * pair, 2 * pair + 1):
                src, f32, parts, cols = piece(m)
                dve.wait_ge(*part.at(last_of(m)))
                dve.tensor_tensor(parts[2][:, cols], f32[:, cols], parts[1][:, cols], ALU.subtract)\
                    .then_inc(rest.semaphore, 1)
        if masked:
            dve.wait_ge(*c_part.at(1))
            dve.tensor_tensor(c32, k.ctxT[:, 0, :], cp[0], ALU.subtract).then_inc(c_rest.semaphore, 1)
            dve.wait_ge(*c_part.at(2))
            dve.tensor_tensor(cp[2], c32, cp[1], ALU.subtract).then_inc(c_rest.semaphore, 1)
        dve.wait_ge(*fill_done.at(2))

        def values(b):
            dve.wait_ge(*v_psum.at(b + 1))
            if b >= 2:
                dve.wait_ge(*av_done.at(STEPS * (b - 1)))
            dst = VA[b % 2][:, key_tiles - TPB:key_tiles, :, 0:HD]
            src = bank[7][:, 0:TPB * P].rearrange("p (t h d) -> p t h d", t=TPB, h=NH)
            if masked:
                tmp = vtmp[:, 0:TPB * P].rearrange("p (t n) -> p t n", t=TPB)
                chain.then(dve.tensor_tensor(tmp, bank[7][:, 0:TPB * P].rearrange("p (t n) -> p t n", t=TPB),
                                             W("bv").unsqueeze(1).broadcast_to([P, TPB, P]), ALU.add))
                for t in range(TPB):
                    tt = b * TPB + t
                    ins = dve.tensor_scalar(VA[b % 2][:, t, :, 0:HD],
                                            vtmp[:, t * P:(t + 1) * P].rearrange("p (h d) -> p h d", h=NH),
                                            k.mask_col[:, tt:tt + 1], None, ALU.mult)
            else:
                for t in range(TPB):
                    dve.tensor_copy(VA[b % 2][:, t, :, 0:HD],
                                    k.ctx_sb[:, b * TPB + t, P:2 * P].rearrange("p (h d) -> p h d", h=NH))
                for t in range(TPB):
                    ins = dve.tensor_copy(VA[b % 2][:, TPB + t, :, 0:HD],
                                          bank[7][:, t * P:(t + 1) * P].rearrange("p (h d) -> p h d", h=NH))
            ins.then_inc(v_sb.semaphore, 1)

        def row_maxima(b, n):
            g = b * NG1 + n
            t, h0 = n % TPB, n // TPB * HPG
            dve.wait_ge(*p1_psum.at(g + 1))
            dve.tensor_reduce(NM[:, b, h0:h0 + HPG, t], bank[g % 2][:, :].rearrange("p (j n) -> p j n", j=HPG),
                              AX.X, ALU.max, negate=True).then_inc(p1_max.semaphore, 1)

        rows = slice(0, TPB * NH)
        for b in range(B + 1):
            for u in range(STEPS + LAG):
                if u < STEPS and b < B:
                    for i in range(PER):
                        row_maxima(b, PER * u + i)
                if u == LAG - 1 and b < B:
                    values(b)
                s = u - LAG
                if b > 0 and s > 0 and s % key_tiles == 0:
                    take_output(dve, b - 1, s // key_tiles - 1)
                if u == STEPS and b < B:
                    dve.wait_ge(*nm_part.at(2 * b + 1))
                    dve.tensor_tensor(NMr[rows, :], bank[7][rows, 0:P], NMp[0][rows, :], ALU.subtract)\
                        .then_inc(nm_rest.semaphore, 1)
                if u == STEPS + 1 and b < B:
                    dve.wait_ge(*nm_part.at(2 * b + 2))
                    if b >= 1:
                        dve.wait_ge(*nm_loaded.at(48 * b))
                    dve.tensor_tensor(NMp[2][rows, :], NMr[rows, :], NMp[1][rows, :], ALU.subtract)\
                        .then_inc(nm_rest.semaphore, 1)
            if b > 0:
                take_output(dve, b - 1, NHG - 1)
        dve.wait_ge(*den_psum.at(1))
        dve.reciprocal(R.rearrange("p t h -> p (t h)"), bank[6][:, S:S + NT * NH]).then_inc(den_ready.semaphore, 1)

        def add_output(t):
            dve.wait_ge(*out_psum.at(t + 1))
            dve.tensor_tensor(k.x[:, t, :], k.x[:, t, :], bank[4 + t % 4][:, 0:P], ALU.add).then_inc(k.x_tiles, 1)

        chain.then(dve.tensor_tensor(k.x[:, :, :], k.x[:, :, :], W("bo").unsqueeze(1).broadcast_to([P, NT, P]), ALU.add))
        for t in range(NT):
            dve.wait_ge(*bc_psum.at(t + 1))
            if t >= 2:
                dve.wait_ge(*out_psum.at(t - 1))
            dve.tensor_tensor(OTn[t % 2], OT[:, :, t * P:(t + 1) * P],
                              bank[1 + t % 3][:, 0:NHG * P].rearrange("p (g n) -> p g n", g=NHG), ALU.mult)\
                .then_inc(normed.semaphore, 1)
            if t >= 1:
                add_output(t - 1)
        add_output(NT - 1)
        dve.wait_ge(k.x_tiles, NT * (number + 1))

    def take_output(dve, b, hg):
        dve.wait_ge(*av_done.at(STEPS * b + (hg + 1) * key_tiles))
        dve.tensor_copy(OT[:, hg, b * S:(b + 1) * S], k.bank[6][:, 0:S]).then_inc(av_out.semaphore, 1)

    return tensor, scalar, vector, gpsimd, sync


def first_of_maxima(dve, chain, values, weights, maxima, tagged, top, chosen, shape):
    chain.then(dve.tensor_reduce(maxima, values, AX.X, ALU.max))
    chain.then(dve.tensor_tensor(tagged, values, maxima.unsqueeze(2).broadcast_to(shape), ALU.is_equal))
    chain.then(dve.tensor_tensor(tagged, tagged, weights, ALU.mult))
    chain.then(dve.tensor_reduce(top, tagged, AX.X, ALU.max))
    chain.then(dve.tensor_tensor(chosen, tagged, top.unsqueeze(2).broadcast_to(shape), ALU.is_equal))


def dense_experts(k, name, number, E, W, routing):
    ROUNDS = 4 if routing else 1
    FT = 4
    ITEMS = 2 * E
    TPH = NT // 2
    shape = [P, NT, E]
    k.carve_from(REGION_B)
    H = [k.carve(F32, FT, HALF) for _ in range(2)]
    hT = None if routing else [k.carve(F32, T) for _ in range(2)]
    xl = None if routing else k.carve(F32, NT, D)
    xlT = None if routing else k.carve(F32, T)
    cwT = k.carve(F32, T)
    logits, tagged, sel1, sel2, low = (k.carve(F32, NT, E) for _ in range(5))
    cw = k.carve(F32, NT, E)
    m1, m2, top, th, w1, w2 = (k.carve(F32, NT) for _ in range(6))

    use = k.norm_use[number]

    def count(what, total):
        return k.count(f"experts_{what}", total)

    logits_psum = count("logits_psum", ROUNDS)
    margin = count("margin", ROUNDS)
    tanh_ready = count("tanh_ready", ROUNDS)
    cw_ready = count("cw_ready", ROUNDS)
    cwT_psum = count("cwT_psum", 2 * ROUNDS)
    cwT_sb = count("cwT_sb", 2 * ROUNDS)
    b2_psum = count("b2_psum", 2 * ROUNDS)
    turned = count("turned", 2 * (ROUNDS - 1))
    T_ready = count("T_ready", 2 * (ROUNDS - 1))
    up_psum = count("up_psum", FT * ITEMS * ROUNDS)
    h_ready = count("h_ready", FT * ITEMS * ROUNDS)
    down_psum = count("down_psum", ITEMS * ROUNDS)
    combined = count("combined", ITEMS * ROUNDS)
    hT_ready = count("hT_ready", 0 if routing else E)

    acc = k.xn

    def x_for(pe, e, half):
        cols = slice(half * HALF, (half + 1) * HALF)
        return k.xnT[:, cols] if routing else hT[e % 2][:, cols]

    def tensor(pe):
        bank = k.bank
        pe.wait_ge(k.weights[name], 16 if routing else 32)

        def up(r, i):
            g = r * ITEMS + i
            e, half = i // 2, i % 2
            if not routing and half == 0:
                pe.wait_ge(*hT_ready.at(e + 1))
            for f in range(FT):
                if g >= 1:
                    pe.wait_ge(*h_ready.at(FT * (g - 1) + f + 1))
                pe.matmul(bank[f], W("w1")[:, e, f * P:(f + 1) * P], x_for(pe, e, half), start=True, stop=True)\
                    .then_inc(up_psum.semaphore, 1)

        def down(r, i):
            g = r * ITEMS + i
            pe.wait_ge(*h_ready.at(FT * (g + 1)))
            if g >= 2:
                pe.wait_ge(*combined.at(g - 1))
            for t in range(TPH):
                for f in range(FT):
                    ins = pe.matmul(bank[4 + g % 2][:, t * P:(t + 1) * P], H[g % 2][:, f, t * P:(t + 1) * P],
                                    W("w2")[:, i // 2, f, :], start=f == 0, stop=f == FT - 1)
            ins.then_inc(down_psum.semaphore, 1)

        def turn(r, h):
            for t in range(h * TPH, (h + 1) * TPH):
                pe.wait_ge(*combined.at(r * ITEMS - 1 + h))
                ins = pe.transpose(bank[6 + h][:, (t % TPH) * P:(t % TPH + 1) * P], k.xn[:, t, :], k.ident[:, :])
            ins.then_inc(turned.semaphore, 1)

        for r in range(ROUNDS):
            if r == 0:
                k.norm.tensor(pe, use, k.xn)
                if not routing:
                    k.norm2.tensor(pe, 1, xl, banks=(4, 5))
                pe.wait_ge(k.norm.T_ready, 2 * use + 2)
                if routing:
                    up(r, 0)
            else:
                turn(r, 0)
                pe.wait_ge(*T_ready.at(2 * r - 1))
                up(r, 0)
                turn(r, 1)
                pe.wait_ge(*T_ready.at(2 * r))
            for t in range(NT):
                ins = pe.matmul(bank[6][:, t * E:(t + 1) * E], k.xnT[:, t * P:(t + 1) * P], W("router")[:, r, :],
                                start=True, stop=True)
            ins.then_inc(logits_psum.semaphore, 1)
            if not routing:
                up(r, 0)
            up(r, 1)
            down(r, 0)
            pe.wait_ge(*cw_ready.at(r + 1))
            for t in range(NT):
                ins = pe.transpose(bank[6 + t // TPH][0:E, (t % TPH) * P:(t % TPH + 1) * P], cw[:, t, :],
                                   k.ident[:, :])
                if t % TPH == TPH - 1:
                    ins.then_inc(cwT_psum.semaphore, 1)
            up(r, 2)
            down(r, 1)
            for t in range(NT):
                pe.wait_ge(*cwT_sb.at(2 * r + t // TPH + 1))
                ins = pe.matmul(bank[6 + t // TPH][:, (t % TPH) * P:(t % TPH + 1) * P], cwT[0:E, t * P:(t + 1) * P],
                                W("b2")[0:E, :], start=True, stop=True)
                if t % TPH == TPH - 1:
                    ins.then_inc(b2_psum.semaphore, 1)
            for i in range(3, ITEMS):
                up(r, i)
                down(r, i - 1)
            down(r, ITEMS - 1)

    def scalar(act):
        bank = k.bank
        act.wait_ge(k.weights[name], 16 if routing else 32)

        def hidden(r, i):
            g = r * ITEMS + i
            if g >= 2:
                act.wait_ge(*down_psum.at(g - 1))
            for f in range(FT):
                act.wait_ge(*up_psum.at(FT * g + f + 1))
                act.activation(H[g % 2][:, f, :], bank[f], ACT.Gelu_apprx_tanh if routing else ACT.Relu,
                               bias=W("b1")[:, (i // 2) * FT + f:(i // 2) * FT + f + 1]).then_inc(h_ready.semaphore, 1)

        def take_half(r, h):
            act.wait_ge(*turned.at(2 * (r - 1) + h + 1))
            act.activation(k.xnT[:, h * HALF:(h + 1) * HALF], bank[6 + h], ACT.Copy).then_inc(T_ready.semaphore, 1)

        for r in range(ROUNDS):
            if r == 0:
                k.norm.scalar(act, use, k.xnT)
                if not routing:
                    k.norm2.scalar(act, 1, xlT, banks=(4, 5))
            else:
                take_half(r, 0)
            hidden(r, 0)
            if r > 0:
                take_half(r, 1)
            hidden(r, 1)
            act.wait_ge(*margin.at(r + 1))
            act.activation(th, m2, ACT.Tanh, scale=0.5).then_inc(tanh_ready.semaphore, 1)
            for h in range(2):
                act.wait_ge(*cwT_psum.at(2 * r + h + 1))
                act.activation(cwT[0:E, h * HALF:(h + 1) * HALF], bank[6 + h][0:E, :], ACT.Copy).then_inc(cwT_sb.semaphore, 1)
            for i in range(2, ITEMS):
                hidden(r, i)

    def vector(dve, chain):
        bank = k.bank
        k.norm.vector(dve, chain, use, k.x, k.xn, 1e-5)
        dve.wait_ge(k.weights[name], 16 if routing else 32)
        if not routing:
            dve.wait_ge(k.norm.ready, NT * (use + 1))
            k.norm2.vector(dve, chain, 1, k.xn, xl, 1e-5)
        falling = W("falling").unsqueeze(1).broadcast_to(shape)
        for r in range(ROUNDS):
            dve.wait_ge(*logits_psum.at(r + 1))
            src = bank[6][:, 0:NT * E].rearrange("p (t e) -> p t e", t=NT)
            if routing:
                chain.then(dve.tensor_tensor(logits, src, W("bg")[:, r, :].unsqueeze(1).broadcast_to(shape), ALU.add))
            else:
                chain.then(dve.tensor_copy(logits, src))
            first_of_maxima(dve, chain, logits, falling, m1, tagged, top, sel1, shape)
            if routing:
                chain.then(dve.scalar_tensor_tensor(out=low, in0=sel1, scalar=-3.0e38, in1=logits, op0=ALU.mult,
                                                    op1=ALU.add))
                first_of_maxima(dve, chain, low, falling, m2, tagged, top, sel2, shape)
                dve.tensor_tensor(m2, m1, m2, ALU.subtract).then_inc(margin.semaphore, 1)
            else:
                dve.tensor_copy(m2, m1).then_inc(margin.semaphore, 1)
            dve.wait_ge(*tanh_ready.at(r + 1))
            chain.then(dve.tensor_scalar(w1, th, 0.5, 0.5, ALU.mult, ALU.add))
            if routing:
                chain.then(dve.tensor_scalar(w2, th, -0.5, 0.5, ALU.mult, ALU.add))
                chain.then(dve.tensor_tensor(sel1, sel1, w1.unsqueeze(2).broadcast_to(shape), ALU.mult))
                chain.then(dve.tensor_tensor(sel2, sel2, w2.unsqueeze(2).broadcast_to(shape), ALU.mult))
                dve.tensor_tensor(cw, sel1, sel2, ALU.add).then_inc(cw_ready.semaphore, 1)
            else:
                dve.tensor_tensor(cw, sel1, w1.unsqueeze(2).broadcast_to(shape), ALU.mult).then_inc(cw_ready.semaphore, 1)
            dve.wait_ge(*cw_ready.at(r + 1))
            for i in range(ITEMS):
                g = r * ITEMS + i
                dve.wait_ge(*down_psum.at(g + 1))
                if i >= 2:
                    dve.wait_ge(*combined.at(g - 1))
                if i == 2:
                    dve.wait_ge(*combined.at(g))
                    for h in range(2):
                        dve.wait_ge(*b2_psum.at(2 * r + h + 1))
                        part = acc[:, h * TPH:(h + 1) * TPH, :]
                        chain.then(dve.tensor_tensor(part, part, bank[6 + h].rearrange("p (t d) -> p t d", t=TPH), ALU.add))
                for t in range(TPH):
                    tt = (i % 2) * TPH + t
                    ins = dve.scalar_tensor_tensor(out=acc[:, tt, :], in0=bank[4 + g % 2][:, t * P:(t + 1) * P],
                                                   scalar=cw[:, tt, i // 2:i // 2 + 1], in1=acc[:, tt, :],
                                                   op0=ALU.mult, op1=ALU.add)
                ins.then_inc(combined.semaphore, 1)
        dve.wait_ge(*combined.at(ROUNDS * ITEMS))
        dve.tensor_tensor(k.x[:, :, :], k.x[:, :, :], k.xn[:, :, :], ALU.add).then_inc(k.x_tiles, NT)
        dve.wait_ge(k.x_tiles, NT * (number + 1))

    def gpsimd(pool):
        k.norm.gpsimd(pool, use)
        if not routing:
            k.norm2.gpsimd(pool, 1)
            pool.wait_ge(k.weights[name], 16 if routing else 32)
            pool.wait_ge(k.norm2.T_ready, 4)
            for e in range(E):
                if e >= 2:
                    pool.wait_ge(*h_ready.at(2 * FT * (e - 1)))
                pool.tensor_scalar(hT[e % 2], xlT, W("g")[:, e:e + 1], W("b")[:, e:e + 1],
                                   ALU.mult, ALU.add).then_inc(hT_ready.semaphore, 1)

    def sync(sp):
        pass

    return tensor, scalar, vector, gpsimd, sync


def gated_attention(k, name, number, W):
    NH, E = 8, 8
    HD = P
    GROUPS = NT * 2 * NH
    scale = float(HD) ** -0.5
    k.carve_from(REGION_B)
    qT, kT, V, oT = ([k.carve(F32, T) for _ in range(2)] for _ in range(4))
    PR = k.carve(F32, B, TPB, S)
    PT = k.carve(F32, B, TPB, S)
    probs = k.carve(F32, GROUPS, E)
    gate = k.carve(F32, GROUPS, E)
    HALF_E = E // 2
    scaled = [k.carve(F32, HALF_E, P) for _ in range(2)]
    rest = [k.carve(F32, P) for _ in range(2)]
    s1 = k.carve(F32, NT, NH, E)
    s2 = k.carve(F32, NT, NH, E)
    n1, n2, tp = (k.carve(F32, NT, NH) for _ in range(3))
    NM = k.carve(F32, NT)
    den, rec = k.carve(F32, 2, NT), k.carve(F32, NT)
    og = [k.carve(F32, NT, E) for _ in range(2)]

    use = k.norm_use[number]

    def sem(what):
        return k.sem(f"{name}_{what}")

    v_weights, o_weights = k.weights["l1v"], k.weights["l1o"]
    sel_psum = sem("sel_psum")
    probs_ready = sem("probs_ready")
    qk_psum = sem("qk_psum")
    qk_sb = sem("qk_sb")
    ex_psum = sem("ex_psum")
    first_half = sem("first_half")
    scaled_ready = sem("scaled_ready")
    rest_ready = sem("rest_ready")
    summed = sem("summed")
    gates_ready = sem("gates_ready")
    score_psum = sem("score_psum")
    max_ready = sem("max_ready")
    exp_ready = sem("exp_ready")
    pt_psum = sem("pt_psum")
    pt_sb = sem("pt_sb")
    av_psum = sem("av_psum")
    av_sb = sem("av_sb")
    og_ready = sem("og_ready")

    def values_block(h):
        return 0 if h == 0 else 2 * h - 1

    def output_block(h):
        return min(2 * h + 2, 2 * NH - 1)

    def tensor(pe):
        bank = k.bank
        k.norm.tensor(pe, use, k.xn)
        pe.wait_ge(k.weights[name], 16)
        pe.wait_ge(k.norm.T_ready, 2 * use + 2)
        for t in range(NT):
            ins = pe.matmul(bank[6 + t // 4][:, (t % 4) * P:(t % 4 + 1) * P], k.xnT[:, t * P:(t + 1) * P], W("sel"),
                            start=True, stop=True)
        ins.then_inc(sel_psum, 1)

        def queries_and_keys(h):
            for i in range(4):
                if h == 0 and i == 2:
                    pe.wait_ge(probs_ready, 1)
                if h > 0:
                    pe.wait_ge(av_sb, B * (h - 1) + i + 1)
                pe.matmul(bank[4 + i], W("q" if i < 2 else "k")[:, h, :], k.xnT[:, (i % 2) * HALF:(i % 2 + 1) * HALF],
                          start=True, stop=True).then_inc(qk_psum, 1)

        def experts(block, src, weights, h):
            for t in range(NT):
                n = block * NT + t
                for c in range(2):
                    if n >= 2:
                        pe.wait_ge(first_half if c == 0 else scaled_ready, n - 1)
                    ins = pe.matmul(bank[2 * (n % 2) + c], src[:, t * P:(t + 1) * P],
                                    weights[:, h * 2 * HALF + c * HALF:h * 2 * HALF + (c + 1) * HALF],
                                    start=True, stop=True)
                ins.then_inc(ex_psum, 1)

        pe.wait_ge(v_weights, 16)
        for h in range(NH + 1):
            if h < NH:
                queries_and_keys(h)
                if h > 0:
                    experts(values_block(h), k.xnT, k.region["A"], h)
                for b in range(B):
                    if b == 0:
                        pe.wait_ge(qk_sb, 4 * (h + 1))
                    for t in range(TPB):
                        tt = b * TPB + t
                        ins = pe.matmul(bank[4 + b][:, t * S:(t + 1) * S], qT[h % 2][:, tt * P:(tt + 1) * P],
                                        kT[h % 2][:, b * S:(b + 1) * S], start=True, stop=True)
                    ins.then_inc(score_psum, 1)
                if h == 0:
                    experts(values_block(h), k.xnT, k.region["A"], h)
            if h > 0:
                if h == 1:
                    pe.wait_ge(o_weights, 16)
                pe.wait_ge(av_sb, B * h)
                experts(output_block(h - 1), oT[(h - 1) % 2], k.region["B"], h - 1)
            if h < NH:
                for b in range(B):
                    pe.wait_ge(exp_ready, B * h + b + 1)
                    for kt in range(TPB):
                        for t in range(TPB):
                            ins = pe.transpose(bank[4 + b][:, kt * S + t * P:kt * S + (t + 1) * P],
                                               PR[:, b, t, kt * P:(kt + 1) * P], k.ident[:, :])
                    ins.then_inc(pt_psum, 1)
                for b in range(B):
                    pe.wait_ge(pt_sb, B * h + b + 1)
                    if b == 0:
                        pe.wait_ge(summed, NT * (values_block(h) + 1))
                    for kt in range(TPB):
                        tt = b * TPB + kt
                        ins = pe.matmul(bank[4 + b][:, 0:S], V[h % 2][:, tt * P:(tt + 1) * P], PT[:, b, kt, :],
                                        start=kt == 0, stop=kt == TPB - 1)
                    ins.then_inc(av_psum, 1)

    def scalar(act):
        bank = k.bank
        k.norm.scalar(act, use, k.xnT)
        act.wait_ge(sel_psum, 1)
        act.activation(probs.rearrange("p (a g) e -> p a (g e)", a=2), k.pair(6), ACT.Sigmoid).then_inc(probs_ready, 1)

        def scale_products(n, scalars):
            act.wait_ge(ex_psum, n + 1)
            if n >= 2:
                act.wait_ge(rest_ready, n - 1)
            for e in range(HALF_E):
                ins = act.activation(scaled[n % 2][:, e, :], bank[2 * (n % 2) + 1][:, e * P:(e + 1) * P], ACT.Copy,
                                     scale=scalars[:, n % NT, HALF_E + e:HALF_E + e + 1])
            ins.then_inc(scaled_ready, 1)

        def exponentials(h, b):
            act.wait_ge(max_ready, B * h + b + 1)
            if h >= 1 and b == 0:
                act.wait_ge(pt_psum, B * h)
            if h >= 2 and b == 0:
                act.wait_ge(og_ready, h - 1)
            for t in range(TPB):
                tt = b * TPB + t
                ins = act.activation(PR[:, b, t, :], bank[4 + b][:, t * S:(t + 1) * S], ACT.Exp,
                                     bias=NM[:, tt:tt + 1], accum_out=den[:, h % 2, tt:tt + 1])
            ins.then_inc(exp_ready, 1)

        gates = gate.rearrange("p (t a h) e -> p t a h e", t=NT, a=2)
        for h in range(NH + 1):
            if h < NH:
                for i in range(4):
                    act.wait_ge(qk_psum, 4 * h + i + 1)
                    dst = (qT if i < 2 else kT)[h % 2]
                    act.activation(dst[:, (i % 2) * HALF:(i % 2 + 1) * HALF], bank[4 + i], ACT.Copy,
                                   scale=scale if i < 2 else 1.0).then_inc(qk_sb, 1)
                if h == 0:
                    act.wait_ge(gates_ready, 1)
                for t in range(NT):
                    scale_products(values_block(h) * NT + t, gates[:, :, 0, h, :])
                    if h == 0 and t % TPB == TPB - 1:
                        exponentials(h, t // TPB)
            for t in range(NT):
                if h > 0:
                    if t == 0:
                        act.wait_ge(og_ready, h)
                    scale_products(output_block(h - 1) * NT + t, og[(h - 1) % 2])
                if t % TPB == TPB - 1 and 0 < h < NH:
                    exponentials(h, t // TPB)
            if h == NH:
                break
            for b in range(B):
                act.wait_ge(pt_psum, B * h + b + 1)
                if h >= 1:
                    act.wait_ge(av_psum, B * (h - 1) + b + 1)
                act.activation(PT[:, b, :, :].rearrange("p a n -> p (a n)"), bank[4 + b], ACT.Copy).then_inc(pt_sb, 1)
            for b in range(B):
                act.wait_ge(av_psum, B * h + b + 1)
                if h >= 2 and b == 0:
                    act.wait_ge(ex_psum, NT * (output_block(h - 2) + 1))
                act.activation(oT[h % 2][:, b * S:(b + 1) * S], bank[4 + b][:, 0:S], ACT.Copy).then_inc(av_sb, 1)

    def vector(dve, chain):
        bank = k.bank
        k.norm.vector(dve, chain, use, k.x, k.xn, 1e-5)
        dve.wait_ge(k.weights[name], 16)
        dve.wait_ge(probs_ready, 1)
        shape = [P, NT, NH, E]
        falling = W("falling").unsqueeze(1).unsqueeze(1).broadcast_to(shape)

        def wide(a):
            return a.unsqueeze(3).broadcast_to(shape)

        def select(side):
            of = lambda a: a.rearrange("p (t a h) e -> p t a h e", t=NT, a=2)[:, :, side, :, :]
            p, g = of(probs), of(gate)
            chain.then(dve.tensor_reduce(n1, p, AX.X, ALU.max))
            for values, largest, chosen in ((p, n1, s1), (s2, n2, s2)):
                if chosen is s2:
                    chain.then(dve.scalar_tensor_tensor(out=s2, in0=s1, scalar=-2.0, in1=p, op0=ALU.mult, op1=ALU.add))
                    chain.then(dve.tensor_reduce(n2, s2, AX.X, ALU.max))
                chain.then(dve.tensor_tensor(g, values, wide(largest), ALU.is_equal))
                chain.then(dve.tensor_tensor(g, g, falling, ALU.mult))
                chain.then(dve.tensor_reduce(tp, g, AX.X, ALU.max))
                chain.then(dve.tensor_tensor(chosen, g, wide(tp), ALU.is_equal))
            chain.then(dve.tensor_tensor(s1, s1, s2, ALU.add))
            chain.then(dve.tensor_tensor(g, s1, p, ALU.mult))
            chain.then(dve.tensor_tensor(n1, n1, n2, ALU.add))
            chain.then(dve.tensor_scalar(n1, n1, 1.0e-9, None, ALU.max))
            chain.then(dve.reciprocal(n2, n1))
            chain.then(dve.tensor_scalar(n2, n2, W("route_scale"), None, ALU.mult))
            dve.tensor_tensor(g, g, wide(n2), ALU.mult).then_inc(gates_ready, 1)
            dve.wait_ge(gates_ready, side + 1)

        select(0)
        gates = gate.rearrange("p (t a h) e -> p t a h e", t=NT, a=2)

        def sum_first_half(n, dst, scalars, first):
            dve.wait_ge(ex_psum, n + 1)
            for e in range(HALF_E):
                src = bank[2 * (n % 2)][:, e * P:(e + 1) * P]
                scalar = scalars[:, n % NT, e:e + 1]
                if e == 0 and first:
                    ins = dve.tensor_scalar(dst, src, scalar, None, ALU.mult)
                else:
                    ins = dve.scalar_tensor_tensor(out=dst, in0=src, scalar=scalar, in1=dst, op0=ALU.mult, op1=ALU.add)
                if e < HALF_E - 1:
                    chain.then(ins)
            ins.then_inc(first_half, 1)

        def add_rest(n, dst, last):
            dve.wait_ge(rest_ready, n + 1)
            dve.wait_ge(first_half, n + 1)
            dve.tensor_tensor(dst, dst, rest[n % 2], ALU.add).then_inc(k.x_tiles if last else summed, 1)

        def sum_experts(block, dst, scalars, first, last=False, middle=None):
            for t in range(NT + 1):
                n = block * NT + t
                if t < NT:
                    sum_first_half(n, dst(t), scalars, first)
                if t > 0:
                    add_rest(n - 1, dst(t - 1), last)
                if t == NT // 2 and middle:
                    middle()

        def denominators(h):
            dve.wait_ge(exp_ready, B * (h + 1))
            if h >= 2:
                dve.wait_ge(summed, NT * (output_block(h - 2) + 1))
            chain.then(dve.reciprocal(rec, den[:, h % 2, :]))
            dve.tensor_tensor(og[h % 2], gates[:, :, 1, h, :], rec.unsqueeze(2).broadcast_to([P, NT, E]), ALU.mult)\
                .then_inc(og_ready, 1)

        def maxima(h):
            if h >= 1:
                dve.wait_ge(exp_ready, B * h)
            for b in range(B):
                dve.wait_ge(score_psum, B * h + b + 1)
                dve.tensor_reduce(NM[:, b * TPB:(b + 1) * TPB], bank[4 + b].rearrange("p (t n) -> p t n", t=TPB),
                                  AX.X, ALU.max, negate=True).then_inc(max_ready, 1)

        for h in range(NH + 1):
            if h == 0:
                maxima(h)
            if h < NH:
                sum_experts(values_block(h), lambda t: V[h % 2][:, t * P:(t + 1) * P], gates[:, :, 0, h, :], True)
                if h > 0:
                    maxima(h)
                else:
                    select(1)
            if h > 0:
                dve.wait_ge(og_ready, h)
                sum_experts(output_block(h - 1), lambda t: k.x[:, t, :], og[(h - 1) % 2], False, last=h == NH)
            if h < NH:
                denominators(h)
        dve.wait_ge(k.x_tiles, NT * (number + 1))

    def gpsimd(pool):
        k.norm.gpsimd(pool, use)
        for n in range(2 * NH * NT):
            pool.wait_ge(scaled_ready, n + 1)
            pool.tensor_tensor(scaled[n % 2][:, 0:2, :], scaled[n % 2][:, 0:2, :], scaled[n % 2][:, 2:4, :], ALU.add)\
                .then_inc(k.pool_chain, 1)
            k.pool_count += 1
            if n >= 2:
                if n - 2 < (2 * NH - 1) * NT:
                    pool.wait_ge(summed, n - 1)
                else:
                    pool.wait_ge(k.x_tiles, NT * number + n - 1 - (2 * NH - 1) * NT)
            pool.wait_ge(k.pool_chain, k.pool_count)
            pool.tensor_tensor(rest[n % 2], scaled[n % 2][:, 0, :], scaled[n % 2][:, 1, :], ALU.add).then_inc(rest_ready, 1)

    def sync(sp):
        sp.wait_ge(k.x_tiles, NT * number)
        k.load_weights(sp, k.dram, "l1o")
        sp.wait_ge(ex_psum, NT * (values_block(NH - 1) + 1))
        k.load_weights(sp, k.dram, "l2f")

    return tensor, scalar, vector, gpsimd, sync


PATCH_EPS = 1.0e-3
DT = -float(np.log(-np.expm1(-PATCH_EPS)))
KEEP = float(np.exp(-PATCH_EPS))


def patch_attention(k, name, number, W):
    k.carve_from(REGION_B)
    upto = k.carve(F32, TPB, S)
    ones = k.carve(F32, P)
    column = k.carve(F32, S)
    part_id = k.carve(F32, TPB)
    lens = k.carve(F32, NT)
    ends = k.carve(F32, NT)
    wrap = k.carve(F32, NT)
    hit = k.carve(F32, NT, S)
    bound = k.carve(F32, NT)
    plug = k.carve(F32, B, S)
    G = [k.carve(F32, B, S) for _ in range(TPB)]
    keep = [k.carve(F32, B, S) for _ in range(TPB)]
    u = k.carve(F32, NT, D)
    xr = k.carve(F32, NT, D)
    xrT = k.carve(F32, T)

    def sem(what):
        return k.sem(f"{name}_{what}")

    consts = sem("consts")
    lens_ready = sem("lens_ready")
    ends_psum = sem("ends_psum")
    hit_ready = sem("hit_ready")
    count_psum = sem("count_psum")
    bound_ready = sem("bound_ready")
    plug_psum = sem("plug_psum")
    gap_ready = sem("gap_ready")
    decay_ready = sem("decay_ready")
    G_ready = sem("G_ready")
    u_ready = sem("u_ready")
    out_psum = sem("out_psum")

    def tensor(pe):
        bank = k.bank
        pe.wait_ge(consts, 1)
        pe.wait_ge(lens_ready, 1)
        by_tile = lens.rearrange("p (b t) -> p t b", t=TPB)
        pe.matmul(bank[0][:, 0:B], upto[:, 0, 0:P], by_tile[:, 0, :], start=True, stop=True)
        pe.matmul(bank[0][:, B:2 * B], ones, by_tile[:, 0, :], start=True, stop=False)
        pe.matmul(bank[0][:, B:2 * B], upto[:, 0, 0:P], by_tile[:, 1, :], start=False, stop=True).then_inc(ends_psum, 1)
        pe.wait_ge(hit_ready, 1)
        for b in range(B):
            for t in range(TPB):
                for j in range(TPB):
                    ins = pe.matmul(bank[1][:, b * TPB + t:b * TPB + t + 1], hit[:, b * TPB + j, t * P:(t + 1) * P],
                                    ones[:, 0:1], start=j == 0, stop=j == TPB - 1)
        ins.then_inc(count_psum, 1)
        pe.wait_ge(bound_ready, 1)
        for b in range(B):
            for t in range(TPB):
                ins = pe.matmul(bank[2 + b // 2][:, (b % 2) * S:(b % 2 + 1) * S],
                                bound[:, b * TPB + t:b * TPB + t + 1].broadcast_to([P, P]), upto[:, t, :],
                                start=t == 0, stop=t == TPB - 1)
        ins.then_inc(plug_psum, 1)
        k.norm2.tensor(pe, 0, xr, banks=(6, 7))
        pe.wait_ge(k.weights[name], 16)
        pe.wait_ge(k.norm2.T_ready, 2)
        pe.wait_ge(G_ready, TPB)
        pe.wait_ge(u_ready, 1)
        for t in range(NT):
            if t >= 4:
                pe.wait_ge(k.x_tiles, NT * number + t - 3)
            b, dst = t // TPB, bank[4 + t % 4][:, 0:P] if t % 4 < 2 else bank[t % 4][:, 0:P]
            for j in range(TPB):
                pe.matmul(dst, G[j][:, b, (t % TPB) * P:(t % TPB + 1) * P], u[:, b * TPB + j, :], start=j == 0, stop=False)
            pe.matmul(dst, xrT[:, t * P:(t + 1) * P], W("w"), start=False, stop=True).then_inc(out_psum, 1)

    def scalar(act):
        for j in range(TPB):
            act.wait_ge(gap_ready, j + 1)
            act.activation(G[j], G[j], ACT.Exp, scale=-DT).then_inc(decay_ready, 1)
        act.wait_ge(k.weights[name], 16)
        k.norm2.scalar(act, 0, xrT, banks=(6, 7), scale=W("g_res"))

    def vector(dve, chain):
        bank = k.bank
        k.norm_plain.vector(dve, chain, 0, k.x, k.xn, 1e-5)
        dve.wait_ge(k.norm_plain.ready, NT)
        k.norm2.vector(dve, chain, 0, k.xn, xr, 1e-5, rms=True)
        dve.wait_ge(k.mask_loaded, 48)
        dve.wait_ge(k.weights[name], 16)
        dve.wait_ge(consts, 1)
        dve.tensor_copy(lens, k.lens[:, :]).then_inc(lens_ready, 1)
        for h in range(2):
            k.norm_ctx.statistics(dve, chain, 0, k.ctx_sb, 1e-5, True, h)
        dve.wait_ge(k.norm_ctx.rstd_ready, 2)
        chain.then(dve.tensor_scalar(k.rstd[:, :], k.rstd[:, :], KEEP, None, ALU.mult))
        for t in range(NT):
            ins = dve.scalar_tensor_tensor(out=u[:, t, :], in0=k.ctx_sb[:, t, 0:D], scalar=k.rstd[:, t:t + 1],
                                           in1=W("g_init"), op0=ALU.mult, op1=ALU.mult)
        ins.then_inc(u_ready, 1)
        dve.wait_ge(ends_psum, 1)
        chain.then(dve.tensor_scalar(ends.rearrange("p (b t) -> p t b", t=TPB),
                                     bank[0][:, 0:NT].rearrange("p (t b) -> p t b", t=TPB), 1.0, None, ALU.subtract))
        chain.then(dve.tensor_scalar(wrap, ends, 0.0, float(S), ALU.is_lt, ALU.mult))
        chain.then(dve.tensor_tensor(ends, ends, wrap, ALU.add))
        for t in range(NT):
            ins = dve.tensor_scalar(hit[:, t, :], column, ends[:, t:t + 1], None, ALU.is_equal)
        ins.then_inc(hit_ready, 1)
        dve.wait_ge(count_psum, 1)
        dve.tensor_scalar(bound, bank[1][:, 0:NT], 1.0, None, ALU.min).then_inc(bound_ready, 1)
        dve.wait_ge(plug_psum, 1)
        flat = plug.rearrange("p b s -> p (b s)")
        chain.then(dve.tensor_scalar(flat.rearrange("p (a n) -> p a n", a=2), k.pair(2), 1.0, 0.0, ALU.subtract, ALU.max))
        chain.then(dve.tensor_scalar(flat, flat, float(S - 1), None, ALU.min))
        for j in range(TPB):
            dve.tensor_scalar(G[j], plug, part_id[:, j:j + 1], 0.0, ALU.subtract, ALU.max).then_inc(gap_ready, 1)
            chain.then(dve.tensor_scalar(keep[j], plug, part_id[:, j:j + 1], None, ALU.is_ge))
        for j in range(TPB):
            dve.wait_ge(decay_ready, j + 1)
            dve.tensor_tensor(G[j], G[j], keep[j], ALU.mult).then_inc(G_ready, 1)
        chain.then(dve.tensor_tensor(k.x[:, :, :], k.x[:, :, :], W("b").unsqueeze(1).broadcast_to([P, NT, P]), ALU.add))
        for t in range(NT):
            dve.wait_ge(out_psum, t + 1)
            src = bank[4 + t % 4][:, 0:P] if t % 4 < 2 else bank[t % 4][:, 0:P]
            dve.tensor_tensor(k.x[:, t, :], k.x[:, t, :], src, ALU.add).then_inc(k.x_tiles, 1)
        dve.wait_ge(k.x_tiles, NT * (number + 1))

    def gpsimd(pool):
        k.norm_plain.gpsimd(pool, 0)
        k.norm2.gpsimd(pool, 0)
        pool.memset(ones, 1.0)
        pool.memset(upto, 1.0).then_inc(k.pool_chain, 1)
        k.pool_count += 1
        pool.iota(column, [[1, S]], base=0, channel_multiplier=0, allow_small_or_imprecise_dtypes=True)
        pool.iota(part_id, [[P, TPB]], base=0, channel_multiplier=1, allow_small_or_imprecise_dtypes=True)
        pool.wait_ge(k.pool_chain, k.pool_count)
        pool.affine_select(out=upto, in_=upto, compare_op=ALU.is_ge, fill=0.0, base=0, pattern=[[-P, TPB], [1, S]],
                           channel_multiplier=-1).then_inc(consts, 1)
        k.norm_ctx.gpsimd(pool, 0)

    def sync(sp):
        sp.wait_ge(k.x_tiles, NT * number)
        for later in ("l3x", "l3x_small", "l3f_small"):
            if later in k.dram:
                k.load_weights(sp, k.dram, later)

    return tensor, scalar, vector, gpsimd, sync


def null_key_attention(k, name, number, W):
    PAIRS, DH = 8, 64
    NK = S + 1
    ITEMS = 2 * B
    CHUNKS = ("q", "k", "q", "k", "v", "v")
    MADE_IN = ((0, 1), (2, 3), (4,), (5,))
    k.carve_from(REGION_B)
    q = [[k.carve(F32, T) for _ in range(2)] for _ in range(2)]
    kT = [k.carve(F32, B, NK) for _ in range(2)]
    V = [k.carve(F32, NT, P) for _ in range(2)]
    mark = k.carve_mark()
    PR = [k.carve(F32, TPB, NK) for _ in range(4)]
    PT = [k.carve(F32, TPB, S) for _ in range(4)]
    end = k.carve_mark()
    k.carve_back(mark)
    y = k.carve(F32, NT, D)
    yn = k.carve(F32, NT, D)
    k.carve(F32, 4 * TPB)
    ENT = k.carve(F32, T)
    k.carve_back(end)
    free_a = k.region["A"][:, L3F_WORDS:]
    in_a = free_a.shape[1] // T
    oT = [free_a[:, p * T:(p + 1) * T] for p in range(in_a)]
    oT += [k.carve(F32, T) for _ in range(PAIRS - in_a)]
    EN = k.carve(F32, NT, 2 * PAIRS)
    NVW = k.carve(F32, D)
    NM, den, rec = (k.carve(F32, 4, TPB) for _ in range(3))
    use = k.norm_use[number]
    HEADS = 2 * PAIRS

    def sem(what):
        return k.sem(f"{name}_{what}")

    null_ready = sem("null_ready")
    nvw_psum = sem("nvw_psum")
    nvw_sb = sem("nvw_sb")
    proj_psum = sem("proj_psum")
    proj_sb = sem("proj_sb")
    score_psum = sem("score_psum")
    max_ready = sem("max_ready")
    exp_ready = sem("exp_ready")
    rec_ready = sem("rec_ready")
    prob_ready = sem("prob_ready")
    pt_psum = sem("pt_psum")
    pt_sb = sem("pt_sb")
    av_psum = sem("av_psum")
    av_sb = sem("av_sb")
    ent_psum = sem("ent_psum")
    ent_sb = sem("ent_sb")
    out_psum = sem("out_psum")
    y_ready = sem("y_ready")

    def tensor(pe):
        bank = k.bank
        k.norm.tensor(pe, use, k.xn)
        pe.wait_ge(k.weights[name], 32)
        for p in range(PAIRS):
            ins = pe.matmul(bank[0][0:HEADS, 0:D], W("nv")[:, p, :], W("o")[:, p, :], start=p == 0, stop=p == PAIRS - 1)
        ins.then_inc(nvw_psum, 1)
        pe.wait_ge(k.norm.T_ready, 2 * use + 2)
        pe.wait_ge(nvw_sb, 1)

        def project(p, c):
            n, h, what = len(CHUNKS) * p + c, c // 2 % 2 if c < 4 else c - 4, CHUNKS[c]
            cols, dst = slice(p * P, (p + 1) * P), bank[6 + n % 2]
            if n >= 2:
                pe.wait_ge(proj_sb, n - 1)
            if what == "q":
                ins = pe.matmul(dst, W("q")[:, cols], k.xnT[:, h * HALF:(h + 1) * HALF], start=True, stop=True)
            elif what == "k":
                for c in range(2):
                    ins = pe.matmul(dst, W("k")[:, c, cols], k.ctxT[:, c, h * HALF:(h + 1) * HALF],
                                    start=c == 0, stop=c == 1)
            else:
                for t in range(4):
                    for c in range(2):
                        ins = pe.matmul(dst[:, t * P:(t + 1) * P], k.ctxT[:, c, (4 * h + t) * P:(4 * h + t + 1) * P],
                                        W("v")[:, c, cols], start=c == 0, stop=c == 1)
            ins.then_inc(proj_psum, 1)

        def scores(g):
            p, b, j = g // ITEMS, g % ITEMS // 2, g % 2
            if j == 0 and b % 2 == 0:
                pe.wait_ge(proj_sb, len(CHUNKS) * p + b + 2)
            if g >= 2:
                pe.wait_ge(exp_ready, g - 1)
            for t in range(TPB):
                tt = b * TPB + t
                ins = pe.matmul(bank[2 * (g % 2) + t][:, 0:NK], q[p % 2][j][:, tt * P:(tt + 1) * P],
                                kT[p % 2][:, b, :], start=True, stop=True)
            ins.then_inc(score_psum, 1)

        def turn(g):
            pe.wait_ge(prob_ready, g + 1)
            if g >= 2:
                if g % 2 == 0:
                    pe.wait_ge(av_sb, g // 2)
                else:
                    pe.wait_ge(pt_sb, g - 1)
            for kt in range(TPB):
                for t in range(TPB):
                    ins = pe.transpose(bank[4 + g % 2][:, kt * S + t * P:kt * S + (t + 1) * P],
                                       PR[g % 4][:, t, kt * P:(kt + 1) * P], k.ident[:, :])
            ins.then_inc(pt_psum, 1)

        for c in range(len(CHUNKS)):
            project(0, c)
        pe.wait_ge(null_ready, 1)
        scores(0)
        scores(1)
        for p in range(PAIRS):
            for b in range(B):
                g = ITEMS * p + 2 * b
                for i in range(2):
                    if g + i + 2 < ITEMS * PAIRS:
                        scores(g + i + 2)
                    turn(g + i)
                if p + 1 < PAIRS:
                    for c in MADE_IN[b]:
                        project(p + 1, c)
                pe.wait_ge(pt_sb, g + 2)
                if b % 2 == 0:
                    pe.wait_ge(proj_sb, len(CHUNKS) * p + 5 + b // 2)
                for kt in range(TPB):
                    for j in range(2):
                        ins = pe.matmul(bank[4][j * DH:(j + 1) * DH, 0:S], V[p % 2][:, b * TPB + kt, j * DH:(j + 1) * DH],
                                        PT[(g + j) % 4][:, kt, :], start=kt == 0, stop=kt == TPB - 1,
                                        tile_position=(0, j * DH))
                ins.then_inc(av_psum, 1)
        for t in range(NT):
            ins = pe.transpose(bank[t // 4][0:HEADS, (t % 4) * P:(t % 4 + 1) * P], EN[:, t, :], k.ident[:, :])
        ins.then_inc(ent_psum, 1)
        pe.wait_ge(av_sb, B * PAIRS)
        for t in range(NT):
            dst = bank[6 + t // 4][:, (t % 4) * P:(t % 4 + 1) * P]
            for p in range(PAIRS):
                pe.matmul(dst, oT[p][:, t * P:(t + 1) * P], W("o")[:, p, :], start=p == 0, stop=False)
            if t == 0:
                pe.wait_ge(ent_sb, 1)
            ins = pe.matmul(dst, ENT[0:HEADS, t * P:(t + 1) * P], NVW[0:HEADS, :], start=False, stop=True)
            if t % 4 == 3:
                ins.then_inc(out_psum, 1)

    def scalar(act):
        bank = k.bank
        k.norm.scalar(act, use, k.xnT)
        act.wait_ge(k.weights[name], 32)

        def exponentials(g):
            act.wait_ge(max_ready, g + 1)
            if g >= 4:
                act.wait_ge(pt_psum, g - 3)
            for t in range(TPB):
                ins = act.activation(PR[g % 4][:, t, :], bank[2 * (g % 2) + t][:, 0:NK], ACT.Exp,
                                     bias=NM[:, g % 4, t:t + 1], accum_out=den[:, g % 4, t:t + 1])
            ins.then_inc(exp_ready, 1)

        def projections(p, c):
            n, h, what = len(CHUNKS) * p + c, c // 2 % 2 if c < 4 else c - 4, CHUNKS[c]
            src = bank[6 + n % 2]
            act.wait_ge(proj_psum, n + 1)
            if what == "q":
                for j in range(2):
                    ins = act.activation(q[p % 2][j][:, h * HALF:(h + 1) * HALF], src, ACT.Copy, scale=W("half")[:, j:j + 1])
            elif what == "k":
                ins = act.activation(kT[p % 2][:, 2 * h:2 * h + 2, 0:S], src.rearrange("p (b n) -> p b n", b=2), ACT.Copy)
            else:
                ins = act.activation(V[p % 2][:, 4 * h:4 * h + 4, :], src.rearrange("p (t n) -> p t n", t=4), ACT.Copy)
            ins.then_inc(proj_sb, 1)

        for c in range(len(CHUNKS)):
            projections(0, c)
        exponentials(0)
        exponentials(1)
        for p in range(PAIRS):
            for b in range(B):
                g = ITEMS * p + 2 * b
                if g + 2 < ITEMS * PAIRS:
                    exponentials(g + 2)
                    exponentials(g + 3)
                if p + 1 < PAIRS:
                    for c in MADE_IN[b]:
                        projections(p + 1, c)
                act.wait_ge(av_psum, B * p + b + 1)
                act.activation(oT[p][:, b * S:(b + 1) * S], bank[4][:, 0:S], ACT.Copy).then_inc(av_sb, 1)
        act.wait_ge(ent_psum, 1)
        act.activation(ENT[0:HEADS, :].rearrange("p (a n) -> p a n", a=2), k.pair(0)[0:HEADS, :, :], ACT.Copy)\
            .then_inc(ent_sb, 1)

    def vector(dve, chain):
        bank = k.bank
        k.norm.vector(dve, chain, use, k.x, k.xn, 1e-5)
        dve.wait_ge(nvw_psum, 1)
        dve.tensor_copy(NVW[0:HEADS, :], bank[0][0:HEADS, 0:D]).then_inc(nvw_sb, 1)

        def maxima(g):
            dve.wait_ge(score_psum, g + 1)
            dve.tensor_reduce(NM[:, g % 4, :], k.pair(2 * (g % 2))[:, :, 0:NK], AX.X, ALU.max, negate=True)\
                .then_inc(max_ready, 1)

        def reciprocals(g):
            dve.wait_ge(exp_ready, g + 1)
            if g >= 4:
                dve.wait_ge(prob_ready, g - 3)
            dve.reciprocal(rec[:, g % 4, :], den[:, g % 4, :]).then_inc(rec_ready, 1)

        def copy_turned(g):
            dve.wait_ge(pt_psum, g + 1)
            if g >= 4:
                dve.wait_ge(av_psum, g // 2 - 1)
            dve.tensor_copy(PT[g % 4].rearrange("p a n -> p (a n)"), bank[4 + g % 2]).then_inc(pt_sb, 1)

        maxima(0)
        maxima(1)
        reciprocals(0)
        reciprocals(1)
        for g in range(0, ITEMS * PAIRS, 2):
            more = g + 2 < ITEMS * PAIRS
            if more:
                maxima(g + 2)
            copy_turned(g)
            if more:
                maxima(g + 3)
                reciprocals(g + 2)
            copy_turned(g + 1)
            if more:
                reciprocals(g + 3)
        for h in range(2):
            dve.wait_ge(out_psum, h + 1)
            chain.then(dve.tensor_copy(y[:, 4 * h:4 * h + 4, :].rearrange("p t d -> p (t d)"), bank[6 + h]))
        k.norm_plain.vector(dve, chain, 1, y, yn, 1e-6)
        dve.wait_ge(k.norm_plain.ready, 2 * NT)
        wide = [P, NT, P]
        chain.then(dve.tensor_tensor(yn, yn, W("ln_scale").unsqueeze(1).broadcast_to(wide), ALU.mult))
        chain.then(dve.tensor_tensor(yn, yn, W("ln_bias").unsqueeze(1).broadcast_to(wide), ALU.add))
        dve.tensor_tensor(k.x[:, :, :], k.x[:, :, :], yn, ALU.add).then_inc(k.x_tiles, NT)
        dve.wait_ge(k.x_tiles, NT * (number + 1))

    def gpsimd(pool):
        k.norm.gpsimd(pool, use)
        pool.wait_ge(k.weights[name], 32)
        for i in range(2):
            ins = pool.tensor_copy(kT[i][:, :, S:NK], W("nk").unsqueeze(1).broadcast_to([P, B, 1]))
        ins.then_inc(null_ready, 1)
        for g in range(PAIRS * ITEMS):
            p, b, j = g // ITEMS, g % ITEMS // 2, g % 2
            pool.wait_ge(rec_ready, g + 1)
            pool.wait_ge(exp_ready, g + 1)
            r = rec[:, g % 4, :].unsqueeze(2)
            pool.tensor_tensor(EN[:, b * TPB:(b + 1) * TPB, 2 * p + j:2 * p + j + 1], PR[g % 4][:, :, S:NK], r, ALU.mult)
            pool.tensor_tensor(PR[g % 4][:, :, 0:S], PR[g % 4][:, :, 0:S], r.broadcast_to([P, TPB, S]), ALU.mult)\
                .then_inc(prob_ready, 1)
        k.norm_plain.gpsimd(pool, 1)

    def sync(sp):
        sp.wait_ge(k.x_tiles, NT * number)
        if "l3f" in k.dram:
            k.load_weights(sp, k.dram, "l3f")

    return tensor, scalar, vector, gpsimd, sync


def sparse_experts(k, name, number, W):
    E = 32
    ROOM = -(-T * 5 // (4 * E))
    SLOTS = E * ROOM
    ST = SLOTS // P
    GROUP = HALF // ROOM
    groups = [(e, min(E, e + GROUP)) for e in range(0, E, GROUP)]
    NG = len(groups)
    shape = [P, NT, E]
    assert SLOTS % P == 0 and NG == 3
    k.carve_from(REGION_B)
    mark = k.carve_mark()
    to_slot = k.carve(F32, NT, SLOTS)
    k.carve_back(mark)
    from_slot = k.carve(F32, NT, ST, P)
    bufT, silu, hid, yT = (k.carve(F32, SLOTS) for _ in range(4))
    mark = k.carve_mark()
    slot_row = k.carve(F32, SLOTS)
    k.carve_back(mark)
    y = k.carve(F32, ST, P)
    logits, tagged, chosen, exps = (k.carve(F32, NT, E) for _ in range(4))
    upto = k.carve(F32, P)
    ones = k.carve(F32, P)
    slot_id = k.carve(F32, ST)
    maxima, top, place, slot, total, gate, fits = (k.carve(F32, NT) for _ in range(7))
    use = k.norm_use[number]

    def sem(what):
        return k.sem(f"{name}_{what}")

    consts = sem("consts")
    logits_psum = sem("logits_psum")
    shifted = sem("shifted")
    exps_ready = sem("exps_ready")
    chosen_ready = sem("chosen_ready")
    place_psum = sem("place_psum")
    slot_ready = sem("slot_ready")
    to_slot_ready = sem("to_slot_ready")
    to_slot_pool = sem("to_slot_pool")
    slot_psum = sem("slot_psum")
    from_slot_ready = sem("from_slot_ready")
    buf_psum = sem("buf_psum")
    buf_sb = sem("buf_sb")
    gate_psum = sem("gate_psum")
    up_psum = sem("up_psum")
    silu_ready = sem("silu_ready")
    hid_ready = sem("hid_ready")
    yT_psum = sem("yT_psum")
    yT_sb = sem("yT_sb")
    y_psum = sem("y_psum")
    y_sb = sem("y_sb")
    out_psum = sem("out_psum")

    def of(g):
        return slice(groups[g][0] * ROOM, groups[g][1] * ROOM)

    def width(g):
        return (groups[g][1] - groups[g][0]) * ROOM

    def out_bank(t):
        return k.bank[3 + t % 5][:, 0:P]

    def tensor(pe):
        bank = k.bank
        k.norm.tensor(pe, use, k.xn)
        pe.wait_ge(k.weights[name], 32)
        pe.wait_ge(consts, 1)
        pe.wait_ge(k.norm.T_ready, 2 * use + 2)
        for t in range(NT):
            ins = pe.matmul(bank[0][:, t * E:(t + 1) * E], k.xnT[:, t * P:(t + 1) * P], W("router"), start=True, stop=True)
        ins.then_inc(logits_psum, 1)
        pe.wait_ge(chosen_ready, 1)
        pe.matmul(bank[1][:, 0:NT * E], upto, chosen.rearrange("p t e -> p (t e)"), start=True, stop=True)
        for t in range(NT - 1):
            ins = pe.matmul(bank[1][:, (t + 1) * E:NT * E], ones,
                            chosen[:, t:t + 1, :].broadcast_to([P, NT - 1 - t, E]), start=False, stop=True,
                            skip_group_check=True)
        ins.then_inc(place_psum, 1)
        pe.wait_ge(slot_ready, 1)
        for t in range(NT):
            ins = pe.matmul(bank[6 + t // 4][:, (t % 4) * P:(t % 4 + 1) * P], slot[:, t:t + 1].broadcast_to([P, P]),
                            k.ident[:, :], start=True, stop=True)
        ins.then_inc(slot_psum, 1)
        for t in range(NT):
            pe.wait_ge((to_slot_ready, to_slot_pool)[t % 2], t // 2 + 1)
            for g in range(NG):
                ins = pe.matmul(bank[g][:, 0:width(g)], k.xn[:, t, :], to_slot[:, t, of(g)], start=t == 0, stop=t == NT - 1)
                if t == NT - 1:
                    ins.then_inc(buf_psum, 1)
        for g, (first, end) in enumerate(groups):
            pe.wait_ge(buf_sb, g + 1)
            for what, dst, done in (("gate", bank[3 + g], gate_psum), ("up", bank[g], up_psum)):
                for e in range(first, end):
                    ins = pe.matmul(dst[:, (e - first) * ROOM:(e - first + 1) * ROOM], W(what)[:, e, :],
                                    bufT[:, e * ROOM:(e + 1) * ROOM], start=True, stop=True)
                ins.then_inc(done, 1)
        for g, (first, end) in enumerate(groups):
            pe.wait_ge(hid_ready, g + 1)
            for e in range(first, end):
                ins = pe.matmul(bank[3 + g][:, (e - first) * ROOM:(e - first + 1) * ROOM], W("down")[:, e, :],
                                hid[:, e * ROOM:(e + 1) * ROOM], start=True, stop=True)
            ins.then_inc(yT_psum, 1)
        pe.wait_ge(yT_sb, NG)
        for s in range(ST):
            ins = pe.transpose(bank[s // 4][:, (s % 4) * P:(s % 4 + 1) * P], yT[:, s * P:(s + 1) * P], k.ident[:, :])
            if s % 4 == 3 or s == ST - 1:
                ins.then_inc(y_psum, 1)
        for t in range(NT):
            pe.wait_ge(from_slot_ready, t + 1)
            if t == 3:
                pe.wait_ge(from_slot_ready, NT)
            if t >= 5:
                pe.wait_ge(k.x_tiles, NT * number + t - 4)
            for s in range(ST):
                if t == 0 and (s % 4 == 0):
                    pe.wait_ge(y_sb, s // 4 + 1)
                ins = pe.matmul(out_bank(t), from_slot[:, t, s, :], y[:, s, :], start=s == 0, stop=s == ST - 1)
            ins.then_inc(out_psum, 1)

    def scalar(act):
        bank = k.bank
        k.norm.scalar(act, use, k.xnT)
        act.wait_ge(shifted, 1)
        act.activation(exps, logits, ACT.Exp).then_inc(exps_ready, 1)
        for g in range(NG):
            act.wait_ge(buf_psum, g + 1)
            act.activation(bufT[:, of(g)], bank[g][:, 0:width(g)], ACT.Copy).then_inc(buf_sb, 1)
        for g in range(NG):
            act.wait_ge(gate_psum, g + 1)
            act.activation(silu[:, of(g)], bank[3 + g][:, 0:width(g)], ACT.Silu).then_inc(silu_ready, 1)
        for g in range(NG):
            act.wait_ge(yT_psum, g + 1)
            act.activation(yT[:, of(g)], bank[3 + g][:, 0:width(g)], ACT.Copy).then_inc(yT_sb, 1)
        for g in range(NG):
            act.wait_ge(y_psum, g + 1)
            n = min(4, ST - 4 * g)
            act.activation(y[:, 4 * g:4 * g + n, :].rearrange("p s d -> p (s d)"), bank[g][:, 0:n * P], ACT.Copy)\
                .then_inc(y_sb, 1)

    def vector(dve, chain):
        bank = k.bank
        k.norm.vector(dve, chain, use, k.x, k.xn, 1e-5)
        dve.wait_ge(k.weights[name], 32)
        dve.wait_ge(logits_psum, 1)
        chain.then(dve.tensor_copy(exps, bank[0][:, 0:NT * E].rearrange("p (t e) -> p t e", t=NT)))
        first_of_maxima(dve, chain, exps, W("falling").unsqueeze(1).broadcast_to(shape), maxima, tagged, top, chosen, shape)
        dve.tensor_tensor(logits, exps, maxima.unsqueeze(2).broadcast_to(shape), ALU.subtract).then_inc(shifted, 1)
        dve.tensor_tensor(k.x[:, :, :], k.x[:, :, :], k.xn[:, :, :], ALU.add).then_inc(chosen_ready, 1)
        dve.wait_ge(place_psum, 1)
        chain.then(dve.tensor_tensor(tagged, chosen, bank[1][:, 0:NT * E].rearrange("p (t e) -> p t e", t=NT), ALU.mult))
        chain.then(dve.tensor_reduce(place, tagged, AX.X, ALU.add))
        dve.tensor_scalar(fits, place, float(ROOM), None, ALU.is_le)
        chain.then(dve.tensor_scalar(top, top, -float(ROOM), float(ROOM * E), ALU.mult, ALU.add))
        chain.then(dve.tensor_tensor(slot, top, place, ALU.add))
        dve.tensor_tensor(slot, slot, fits, ALU.mult).then_inc(slot_ready, 1)
        dve.wait_ge(slot_ready, 1)
        dve.wait_ge(consts, 1)
        for t in range(0, NT, 2):
            dve.tensor_scalar(to_slot[:, t, :], slot_row, slot[:, t:t + 1], None, ALU.is_equal).then_inc(to_slot_ready, 1)
        dve.wait_ge(exps_ready, 1)
        chain.then(dve.tensor_reduce(total, exps, AX.X, ALU.add))
        chain.then(dve.reciprocal(gate, total))
        dve.wait_ge(slot_psum, 1)
        dve.wait_ge(buf_psum, NG)

        def back(t):
            dve.tensor_tensor(from_slot[:, t, :, :], bank[6 + t // 4][:, (t % 4) * P:(t % 4 + 1) * P]
                              .unsqueeze(1).broadcast_to([P, ST, P]), slot_id.unsqueeze(2).broadcast_to([P, ST, P]),
                              ALU.is_equal).then_inc(from_slot_ready, 1)

        done = 0
        for g in range(NG):
            for t in range(done, min(NT, done + 3)):
                back(t)
            done = min(NT, done + 3)
            dve.wait_ge(up_psum, g + 1)
            dve.wait_ge(silu_ready, g + 1)
            dve.tensor_tensor(hid[:, of(g)], silu[:, of(g)], bank[g][:, 0:width(g)], ALU.mult).then_inc(hid_ready, 1)
        for t in range(NT):
            dve.wait_ge(out_psum, t + 1)
            dve.scalar_tensor_tensor(out=k.x[:, t, :], in0=out_bank(t), scalar=gate[:, t:t + 1], in1=k.x[:, t, :],
                                     op0=ALU.mult, op1=ALU.add).then_inc(k.x_tiles, 1)
        dve.wait_ge(k.x_tiles, NT * (number + 1))

    def gpsimd(pool):
        k.norm.gpsimd(pool, use)
        pool.memset(ones, 1.0)
        pool.memset(upto, 1.0).then_inc(k.pool_chain, 1)
        k.pool_count += 1
        pool.iota(slot_row, [[1, SLOTS]], base=1, channel_multiplier=0, allow_small_or_imprecise_dtypes=True)
        pool.iota(slot_id, [[P, ST]], base=1, channel_multiplier=1, allow_small_or_imprecise_dtypes=True)
        pool.wait_ge(k.pool_chain, k.pool_count)
        pool.affine_select(out=upto, in_=upto, compare_op=ALU.is_ge, fill=0.0, base=0, pattern=[[1, P]],
                           channel_multiplier=-1).then_inc(consts, 1)
        pool.wait_ge(slot_ready, 1)
        pool.wait_ge(consts, 1)
        for t in range(1, NT, 2):
            pool.tensor_scalar(to_slot[:, t, :], slot_row, slot[:, t:t + 1], None, ALU.is_equal).then_inc(to_slot_pool, 1)

    def sync(sp):
        pass

    return tensor, scalar, vector, gpsimd, sync


def build(nc, dram, out, last_stage=8):
    with ExitStack() as ctx:
        k = Kit(nc, ctx, dram)
        prelude = load_and_prepare(k, dram)
        stages = [prelude]
        W0 = k.weight_views("l0x", L0X)
        stages.append(packed_attention(k, "l0x", 0, 8, 16, 2, True, 1e-5, W0))
        if last_stage >= 2:
            stages.append(dense_experts(k, "l0f", 1, 4, k.weight_views("l0f", L0F), routing=True))
        if last_stage >= 3:
            stages.append(packed_attention(k, "l1x", 2, 16, 8, 4, False, 1e-5, k.weight_views("l1x", L1X)))
        if last_stage >= 4:
            stages.append(gated_attention(k, "l1f", 3, k.weight_views("l1f", L1F)))
        if last_stage >= 5:
            stages.append(patch_attention(k, "l2x", 4, k.weight_views("l2x", L2X)))
        if last_stage >= 6:
            stages.append(dense_experts(k, "l2f", 5, 8, k.weight_views("l2f", L2F, "l2f_small", L2F_SMALL), routing=False))
        if last_stage >= 7:
            stages.append(null_key_attention(k, "l3x", 6, k.weight_views("l3x", L3X, "l3x_small", L3X_SMALL)))
        if last_stage >= 8:
            stages.append(sparse_experts(k, "l3f", 7, k.weight_views("l3f", L3F, "l3f_small", L3F_SMALL)))

        block = ctx.enter_context(nc.Block())

        @block.tensor
        def _(pe):
            for stage in stages:
                stage[0](pe)

        @block.scalar
        def _(act):
            for stage in stages:
                stage[1](act)

        @block.vector
        def _(dve):
            chain = Chain(dve, k.sem("vector_chain"))
            for stage in stages:
                stage[2](dve, chain)

        @block.gpsimd
        def _(pool):
            for stage in stages:
                stage[3](pool)

        @block.sync
        def _(sp):
            for stage in stages:
                stage[4](sp)
            sp.wait_ge(k.x_tiles, NT * last_stage)
            sp.dma_start(out, k.x[:, :, :]).then_inc(k.out_stored, 16)
            sp.wait_ge(k.out_stored, 16)


class Kit:

    def __init__(self, nc, ctx, dram):
        self.nc, self.ctx, self.dram = nc, ctx, dram
        sb = lambda name, shape, dt=F32: ctx.enter_context(nc.sbuf_tensor(name, shape, dt))
        self.x = sb("x", [P, NT, D])
        self.xn = sb("xn", [P, NT, D])
        self.xnT = sb("xnT", [P, T])
        self.ctx_sb = sb("ctx", [P, NT, CTX])
        self.ctxT = sb("ctxT", [P, 2, T])
        self.ident = sb("ident", [P, P])
        self.minus_half = sb("minus_half", [P, NT])
        self.stats = sb("stats", [P, NT, 6])
        self.mean_var = sb("mean_var", [P, NT, 2])
        self.var_eps = sb("var_eps", [P, NT])
        self.rstd = sb("rstd", [P, NT])
        self.mask_col = sb("mask_col", [P, NT])
        self.region = {"A": sb("region_a", [P, 8192]), "C": sb("region_c", [P, 4352]), "D": sb("region_d", [P, 4508]), "E": sb("region_e", [P, 584])}
        self.work = sb("work", [P, WORK])
        self.region["B"] = self.work[:, 0:REGION_B]
        self.psum = ctx.enter_context(nc.psum_tensor("psum", [P, 8, HALF], F32))
        self.bank = [self.psum[:, i, :] for i in range(8)]
        self.at = 0
        self.counts = {}
        self.c_stored = self.sem("c_stored")
        self.q_dram = {n: dram["scratch"](f"q_parts{n}") for n in (0, 2)}
        self.k_dram = {n: dram["scratch"](f"k_parts{n}") for n in (0, 2)}
        self.c_dram = dram["scratch"]("ctx_parts")
        self.weights = {n: self.sem(f"{n}_weights") for n in WEIGHTS if not n.endswith("_small")}
        self.x_tiles = self.sem("x_tiles")
        self.out_stored = self.sem("out_stored")
        self.x_loaded = self.sem("x_loaded")
        self.ctx_loaded = self.sem("ctx_loaded")
        self.mask_loaded = self.sem("mask_loaded")
        self.consts_ready = self.sem("consts_ready")
        self.ctx_turned = self.sem("ctx_turned")
        self.ctxT_ready = self.sem("ctxT_ready")
        self.mask_ready = self.sem("mask_ready")
        self.pool_chain = self.sem("pool_chain")
        self.pool_count = 0
        self.norm = Norm(self, "norm")
        self.norm2 = Norm(self, "inner_norm")
        self.norm_use = {0: 0, 1: 1, 2: 2, 3: 3, 5: 4, 6: 5, 7: 6}
        self.norm_plain = Norm(self, "plain_norm")
        self.norm_ctx = Norm(self, "ctx_norm")
        self.lens = sb("lens", [P, NT], I32)

    def sem(self, name):
        return self.ctx.enter_context(self.nc.semaphore(name))

    def count(self, name, total):
        if name not in self.counts:
            self.counts[name] = [self.sem(name), 0]
        semaphore, base = self.counts[name]
        self.counts[name][1] += total
        return Count(semaphore, base)

    def pair(self, i):
        return self.psum[:, i:i + 2, :]

    def carve(self, dtype, *shape):
        size = int(np.prod(shape))
        words = size if dtype != BF16 else size // 2
        flat = self.work[:, self.at:self.at + words]
        self.at += words
        assert self.at <= WORK, (self.at, WORK)
        if dtype != F32:
            flat = flat.bitcast(dtype)
        names = [f"a{i}" for i in range(len(shape))]
        if len(shape) == 1:
            return flat
        return flat.rearrange(f"p ({' '.join(names)}) -> p {' '.join(names)}", **dict(zip(names, shape)))

    def carve_mark(self):
        return self.at

    def carve_back(self, mark):
        self.at = mark

    def carve_from(self, start):
        self.at = start

    def loads_of(self, name):
        return 16 * (len(TERMS) + (3 + 1 if name == "l0x" else 3 + 3))

    def weight_views(self, name, layout, *more):
        region, at = WEIGHTS[name]
        views = {}
        if more:
            rest = self.weight_views(*more)
            views = {what: rest(what) for what, *_ in more[1]}
        for what, *shape in layout:
            size = int(np.prod(shape))
            flat = self.region[region][:, at:at + size]
            if len(shape) > 1:
                names = [f"a{i}" for i in range(len(shape))]
                flat = flat.rearrange(f"p ({' '.join(names)}) -> p {' '.join(names)}", **dict(zip(names, shape)))
            views[what] = flat
            at += size
        return lambda what: views[what]

    def load_weights(self, engine, dram, name):
        region, at = WEIGHTS[name]
        src = dram[name]
        engine.dma_start(self.region[region][:, at:at + src.shape[1]], src)\
            .then_inc(self.weights[name.removesuffix("_small")], 16)


REGION_B = 8192
WORK = REGION_B + 18090
WEIGHTS = {"l0x": ("D", 0), "l0f": ("C", 0), "l1x": ("D", 1290), "l1f": ("D", 2320), "l1v": ("A", 0), "l1o": ("B", 0), "l2x": ("E", 0),
           "l2f": ("A", 0), "l2f_small": ("E", 386),
           "l3x": ("C", 0), "l3x_small": ("D", 0), "l3f": ("A", 0), "l3f_small": ("B", 0)}
L0X = (("k", 2, P), ("v", 2, P), ("q", P), ("ox", P), ("o", 2, P), ("pick", 4), ("bk", 1), ("bq", 1), ("bv", P), ("bo", P))
L0F = (("w1", 4, 512), ("w2", 4, 4, P), ("router", 4, 4), ("bg", 4, 4), ("b1", 16), ("b2", P), ("falling", 4))
L1F = (("q", 8, P), ("k", 8, P), ("sel", P), ("route_scale", 1), ("falling", 8))
L2X = (("w", P), ("g_init", P), ("b", P), ("g_res", 1))
L2F = (("w1", 8, 512), ("w2", 8, 4, P))
L3X = (("k", 2, 8 * P), ("v", 2, 8 * P))
L3X_SMALL = (("q", 8 * P), ("o", 8, P), ("nv", 8, 16), ("nk", 1), ("half", 2), ("ln_scale", P), ("ln_bias", P))
L3F = (("down", 32, P), ("router", 32), ("falling", 32))
L3F_WORDS = 32 * P + 32 + 32
L3F_SMALL = (("gate", 32, P), ("up", 32, P))
L2F_SMALL = (("router", 1, 8), ("b1", 32), ("b2", P), ("falling", 8), ("g", 8), ("b", 8))
L1X = (("k", P), ("v", P), ("q", P), ("o", 4, P), ("pick", 4), ("bo", P))


def load_and_prepare(k, dram):

    def tensor(pe):
        pe.wait_ge(k.consts_ready, 1)
        pe.wait_ge(k.ctx_loaded, 16)
        for c in range(2):
            for t in range(NT):
                ins = pe.transpose(k.bank[2 * c + t // 4][:, (t % 4) * P:(t % 4 + 1) * P],
                                   k.ctx_sb[:, t, c * P:(c + 1) * P], k.ident[:, :])
                if t % 4 == 3:
                    ins.then_inc(k.ctx_turned, 1)

    def scalar(act):
        for i in range(4):
            act.wait_ge(k.ctx_turned, i + 1)
            act.activation(k.ctxT[:, i // 2, (i % 2) * HALF:(i % 2 + 1) * HALF], k.bank[i], ACT.Copy)\
                .then_inc(k.ctxT_ready, 1)

    def vector(dve, chain):
        dve.wait_ge(k.x_loaded, 16)

    def gpsimd(pool):
        pool.memset(k.minus_half[:, :], -0.5)
        pool.memset(k.ident[:, :], 0.0).then_inc(k.pool_chain, 1)
        k.pool_count += 1
        pool.wait_ge(k.pool_chain, k.pool_count)
        pool.affine_select(out=k.ident[:, :], in_=k.ident[:, :], compare_op=ALU.not_equal, fill=1.0,
                           base=0, pattern=[[-1, P]], channel_multiplier=1).then_inc(k.consts_ready, 1)

    def mask(pool):
        pool.wait_ge(k.mask_loaded, 48)
        pool.tensor_scalar(k.mask_bias[0:1, :], k.mask_bc[0:1, :], 0.0, MASKED, ALU.is_equal, ALU.mult)\
            .then_inc(k.mask_ready, 1)

    def sync(sp):
        sp.dma_start(k.x[:, :, :], dram["x"]).then_inc(k.x_loaded, 16)
        sp.dma_start(k.ctx_sb[:, :, :], dram["ctx"]).then_inc(k.ctx_loaded, 16)
        sp.dma_start(k.mask_bc[:, :], dram["mask"].partition_broadcast(P)).then_inc(k.mask_loaded, 16)
        sp.dma_start(k.mask_col[:, :], dram["mask_col"]).then_inc(k.mask_loaded, 16)
        sp.dma_start(k.lens[:, :], dram["lens"]).then_inc(k.mask_loaded, 16)
        k.load_weights(sp, dram, "l0x")

    def load_later(sp, names):
        for name in names:
            k.load_weights(sp, dram, name)

    k.load_later = load_later
    k.prepare_mask = mask
    k.mask_bc = k.ctx.enter_context(k.nc.sbuf_tensor("mask_bc", [P, T], F32))
    k.mask_bias = k.ctx.enter_context(k.nc.sbuf_tensor("mask_bias", [1, T], BF16))
    return tensor, scalar, vector, gpsimd, sync


def tiles(a):
    n = a.shape[0] // P
    return np.ascontiguousarray(a.reshape(n, P, -1).transpose(1, 0, 2)).reshape(P, -1)


def across(v):
    return np.broadcast_to(v.reshape(1, -1), (P, v.size))


def slots(w, heads):
    width = w.shape[0] // heads
    out = np.zeros((heads, SLOT, w.shape[1]), w.dtype)
    out[:, :width] = w.reshape(heads, width, -1)
    return out.reshape(heads * SLOT, -1)


def pick(width):
    out = np.zeros((P, P // SLOT), np.float32)
    for j in range(P // SLOT):
        out[SLOT * j + width, j] = 1.0
    return out


def columns(v):
    return v.reshape(-1, P).T


def rows(v):
    out = np.zeros((P, v.shape[1]), v.dtype)
    out[:v.shape[0]] = v
    return out


def expert_weights(w1, w2):
    E = w2.shape[0]
    return [w1.reshape(P, -1), w2.reshape(E, 4, P, D).transpose(2, 0, 1, 3).reshape(P, -1)]


def pack(i):
    f = {n: np.asarray(a) for n, a in i.items()}
    w = {}
    src, wo = f["L0_xattn_W_src"], f["L0_xattn_W_out"]
    w["l0x"] = [tiles(src[:D].T), tiles(src[D:].T), f["L0_xattn_W_tgt"].T, wo[:, :D].T, tiles(slots(wo[:, D:].T, 8)),
                pick(16), f["L0_xattn_b_src"][:D, None], f["L0_xattn_b_tgt"][:, None],
                across(f["L0_xattn_b_src"][D:]), across(f["L0_xattn_b_out"])]
    qkv = f["L1_xattn_w_qkv"]
    w["l1x"] = [qkv[D:2 * D].T, qkv[2 * D:].T, qkv[:D].T, tiles(slots(f["L1_xattn_w_proj"].T, 16)), pick(8),
                across(f["L1_xattn_b_proj"])]
    w["l0f"] = expert_weights(f["L0_ffn_W1"].transpose(1, 0, 2), f["L0_ffn_W2"])
    w["l0f"] += [f["L0_ffn_Wg"].transpose(1, 0, 2).reshape(P, -1), across(f["L0_ffn_bg"]),
                 columns(f["L0_ffn_b1"]), rows(f["L0_ffn_b2"]), across(np.arange(4, 0, -1, dtype=np.float32))]
    by_head = lambda a: a.reshape(8, P, D).transpose(2, 0, 1).reshape(P, -1)
    w["l1f"] = [by_head(f["L1_ffn_q_w"]), by_head(f["L1_ffn_k_w"]), f["L1_ffn_sel_v_w"].T, f["L1_ffn_sel_o_w"].T,
                across(f["L1_ffn_route_scale"]), across(np.arange(8, 0, -1, dtype=np.float32))]
    w["l1v"] = [f["L1_ffn_v_w"].transpose(1, 0, 2).reshape(P, -1)]
    w["l1o"] = [f["L1_ffn_o_w"].transpose(1, 0, 2).reshape(P, -1)]
    w["l2x"] = [f["L2_xattn_W_in"].T, across(f["L2_xattn_g_init"][:D]), across(f["L2_xattn_b_in"]),
                f["L2_xattn_g_res"][:, None]]
    w["l2f"] = expert_weights(f["L2_ffn_w1"].transpose(2, 0, 1), f["L2_ffn_w2"].transpose(0, 2, 1))
    w["l2f_small"] = [f["L2_ffn_centroids"].T, columns(f["L2_ffn_b1"]), rows(f["L2_ffn_b2"]),
                      across(np.arange(8, 0, -1, dtype=np.float32)), f["L2_ffn_ln_g"].T, f["L2_ffn_ln_b"].T]
    kv, null = f["L3_xattn_Wkv"], f["L3_xattn_null_kv"]
    w["l3x"] = [tiles(kv[:, :8 * P]), tiles(kv[:, 8 * P:])]
    nv = np.zeros((2, 64, 8, 16), np.float32)
    half = np.zeros((2, 64, 2), np.float32)
    for j in range(2):
        half[j, :, j] = 64.0 ** -0.5
        for p in range(8):
            nv[j, :, p, 2 * p + j] = null[1]
    w["l3x_small"] = [f["L3_xattn_Wq"], tiles(f["L3_xattn_Wout"]), nv.reshape(P, -1),
                      np.concatenate([null[0], null[0]])[:, None], half.reshape(P, 2),
                      across(f["L3_xattn_ln_scale"]), across(f["L3_xattn_ln_bias"])]
    by_expert = lambda a: a.transpose(1, 0, 2).reshape(P, -1)
    w["l3f"] = [by_expert(f["L3_ffn_w_down"]), f["L3_ffn_w_router"], across(np.arange(32, 0, -1, dtype=np.float32))]
    w["l3f_small"] = [by_expert(f["L3_ffn_w_gate"]), by_expert(f["L3_ffn_w_up"])]
    return f, w


def kernel(**inputs):
    import concourse.bacc as bacc
    from concourse.bass_utils import run_bass_kernel_spmd

    f, w = pack(inputs)
    arrays = {name: np.ascontiguousarray(np.concatenate(parts, axis=1)) for name, parts in w.items()}
    arrays["x"] = tiles(f["x"].reshape(T, D)).reshape(P, NT, D)
    arrays["ctx"] = tiles(f["ctx_2048"].reshape(T, CTX)).reshape(P, NT, CTX)
    arrays["mask"] = f["mask_BxS2_fk1"].reshape(T)
    arrays["mask_col"] = np.ascontiguousarray(f["mask_BxS2_fk1"].reshape(NT, P).T)
    arrays["lens"] = np.ascontiguousarray(f["mask_BxS2_if0"].astype(np.int32, copy=False).reshape(NT, P).T)
    nc = bacc.Bacc("TRN2", target_bir_lowering=False, num_devices=1)
    dram, fed = {}, {}
    for name, a in arrays.items():
        fed[f"in_{name}"] = a
        dram[name] = nc.dram_tensor(f"in_{name}", a.shape, mybir.dt.from_np(a.dtype), kind="ExternalInput").ap()
    dram["scratch"] = lambda name: nc.dram_tensor(name, (3 * P, T), BF16, kind="Internal").ap()
    out = nc.dram_tensor("out_x", (P, NT, D), F32, kind="ExternalOutput").ap()
    build(nc, dram, out)
    result = run_bass_kernel_spmd(nc, [fed], core_ids=[0]).results[0]["out_x"]
    return result.reshape(P, NT, D).transpose(1, 0, 2).reshape(B, S, D)
```
